# Optimizing a Trainium2 kernel written in Bass

```python
import numpy as np
import jax
import jax.numpy as jnp

def _softmax(x, axis=-1):
    return jax.nn.softmax(x, axis=axis)

def _gelu(x):
    return jax.nn.gelu(x, approximate=True)

def _silu(x):
    return jax.nn.silu(x)

def _sigmoid(x):
    return jax.nn.sigmoid(x)

def _layernorm(x, axis=-1, eps=1e-05):
    m = jnp.mean(x, axis=axis, keepdims=True)
    v = jnp.var(x, axis=axis, keepdims=True)
    return (x - m) / jnp.sqrt(v + eps)

def _scatter_add(tgt, idx, src, axis=0):
    return tgt.at[idx].add(src)

def _segment_sum(src, seg, n):
    return jax.ops.segment_sum(src, seg, n)
kernel_name = 'mk_gnn_resnorm_d2_gnn_r32_436851'

def setup_inputs(seed: int=0):
    np.random.seed(seed)
    _w = jnp.asarray

    def _rec_inputs():
        import jax
        import jax.numpy as jnp
        _gk = jax.random.key(seed)
        x = -0.0005121 + 1.001 * jax.random.normal(jax.random.fold_in(_gk, 1), (3125, 32), jnp.float32)
        _s = jax.random.randint(jax.random.fold_in(_gk, 2), (25000,), 0, 3125, jnp.int32)
        _d = jax.random.randint(jax.random.fold_in(_gk, 3), (25000,), 0, 3125, jnp.int32)
        _loop = jnp.arange(3125, dtype=jnp.int32)
        src = jnp.concatenate([_s, _d, _loop])
        dst = jnp.concatenate([_d, _s, _loop])
        _o = jnp.argsort(dst, stable=True)
        src = src[_o]
        dst = dst[_o]
        edge_attr_3 = jax.random.uniform(jax.random.fold_in(_gk, 11), (53125, 3), jnp.float32, 0.0, 0.999998)
        return (x, src, dst, edge_attr_3)
    x, src, dst, edge_attr_3 = _rec_inputs()

    def _L0_gnn_setup():
        import jax, jax.numpy as jnp
        import numpy as np
        N_NODES = 3125
        N_EDGES = 50000
        IN_C, HID_C, OUT_C = (32, 64, 32)

        def _sage_conv(x, src, dst, W_l, W_r, b, num_nodes):
            msg = x[src]
            agg = jax.ops.segment_sum(msg, dst, num_segments=num_nodes)
            deg = jax.ops.segment_sum(jnp.ones((src.shape[0],), dtype=x.dtype), dst, num_segments=num_nodes)
            mean = agg / jnp.maximum(deg, 1.0)[:, None]
            return mean @ W_l.T + x @ W_r.T + b
        key = jax.random.key(seed)
        ks = jax.random.split(key, 9)
        x = jax.random.normal(ks[0], (N_NODES, IN_C), dtype=jnp.float32)
        edge_index = jax.random.randint(ks[1], (2, N_EDGES), 0, N_NODES, dtype=jnp.int64)
        s1 = 1.0 / np.sqrt(IN_C)
        s2 = 1.0 / np.sqrt(HID_C)
        W1_l = jax.random.uniform(ks[2], (HID_C, IN_C), minval=-s1, maxval=s1, dtype=jnp.float32)
        W1_r = jax.random.uniform(ks[3], (HID_C, IN_C), minval=-s1, maxval=s1, dtype=jnp.float32)
        b1 = jax.random.uniform(ks[4], (HID_C,), minval=-s1, maxval=s1, dtype=jnp.float32)
        W2_l = jax.random.uniform(ks[5], (OUT_C, HID_C), minval=-s2, maxval=s2, dtype=jnp.float32)
        W2_r = jax.random.uniform(ks[6], (OUT_C, HID_C), minval=-s2, maxval=s2, dtype=jnp.float32)
        b2 = jax.random.uniform(ks[7], (OUT_C,), minval=-s2, maxval=s2, dtype=jnp.float32)
        return {'x': x, 'W1_l': W1_l, 'W1_r': W1_r, 'b1': b1, 'W2_l': W2_l, 'W2_r': W2_r, 'b2': b2, 'edge_index': edge_index}
    _L0_gnn_all = _L0_gnn_setup()
    _L0_gnn_in = {k: v for k, v in _L0_gnn_all.items() if k in ('W1_l', 'W1_r', 'b1', 'W2_l', 'W2_r', 'b2')}
    del _L0_gnn_all

    def _L1_gnn_setup():
        import jax, jax.numpy as jnp
        import numpy as np
        D = 3
        KS = 5
        K = KS ** D
        S = 2 ** D
        _COMBOS = np.array([[s >> d & 1 for d in range(D)] for s in range(S)], dtype=np.int32)
        _STRIDES = np.array([KS ** (D - 1 - d) for d in range(D)], dtype=np.int32)

        def spline_basis(pseudo):
            pos = pseudo * (KS - 1)
            i0 = jnp.clip(jnp.floor(pos), 0, KS - 2).astype(jnp.int32)
            frac = pos - i0
            combos = jnp.asarray(_COMBOS)
            basis = jnp.prod(jnp.where(combos[None] == 1, frac[:, None, :], 1.0 - frac[:, None, :]), axis=-1)
            idx = jnp.sum((i0[:, None, :] + combos[None]) * jnp.asarray(_STRIDES)[None, None, :], axis=-1)
            return (basis, idx)

        def spline_conv(x, row, col, basis, idx, W, b):
            N = x.shape[0]
            Fout = W.shape[2]
            z = jnp.einsum('ni,kio->nko', x, W).reshape(N * K, Fout)
            gathered = z[col[:, None] * K + idx]
            msg = jnp.einsum('es,eso->eo', basis, gathered)
            out = jax.ops.segment_sum(msg, row, num_segments=N)
            deg = jax.ops.segment_sum(jnp.ones_like(msg[:, 0]), row, num_segments=N)
            return out / jnp.maximum(deg, 1.0)[:, None] + b
        key = jax.random.key(seed)
        ks = jax.random.split(key, 13)
        N, E, Fin, Fout = (625, 10000, 32, 32)

        def u(k, shape, size):
            bound = 1.0 / np.sqrt(size)
            return jax.random.uniform(k, shape, jnp.float32, -bound, bound)
        return dict(x=jax.random.normal(ks[0], (N, Fin), jnp.float32), edge_index=jax.random.randint(ks[1], (2, E), 0, N, dtype=jnp.int32), pseudo=jax.random.uniform(ks[2], (E, D), jnp.float32), stn1_w=u(ks[3], (K, 1, 64), 1 * S), stn1_b=u(ks[4], (64,), 1 * S), stn2_w=u(ks[5], (K, 64, 64), 64 * S), stn2_b=u(ks[6], (64,), 64 * S), stn3_w=u(ks[7], (64, 64), 64), stn3_b=u(ks[8], (64,), 64), stn4_w=u(ks[9], (64, 3), 64), stn4_b=u(ks[10], (3,), 64), conv_w=u(ks[11], (K, Fin, Fout), Fin * S), conv_b=u(ks[12], (Fout,), Fin * S))
    _L1_gnn_all = _L1_gnn_setup()
    _L1_gnn_in = {k: v for k, v in _L1_gnn_all.items() if k in ('stn1_w', 'stn1_b', 'stn2_w', 'stn2_b', 'stn3_w', 'stn3_b', 'stn4_w', 'stn4_b', 'conv_w', 'conv_b')}
    del _L1_gnn_all
    return {'x': x, 'src': src, 'dst': dst, 'edge_attr_3': edge_attr_3, 'L0_gnn_W1_l': _L0_gnn_in['W1_l'], 'L0_gnn_W1_r': _L0_gnn_in['W1_r'], 'L0_gnn_b1': _L0_gnn_in['b1'], 'L0_gnn_W2_l': _L0_gnn_in['W2_l'], 'L0_gnn_W2_r': _L0_gnn_in['W2_r'], 'L0_gnn_b2': _L0_gnn_in['b2'], 'L1_gnn_stn1_w': _L1_gnn_in['stn1_w'], 'L1_gnn_stn1_b': _L1_gnn_in['stn1_b'], 'L1_gnn_stn2_w': _L1_gnn_in['stn2_w'], 'L1_gnn_stn2_b': _L1_gnn_in['stn2_b'], 'L1_gnn_stn3_w': _L1_gnn_in['stn3_w'], 'L1_gnn_stn3_b': _L1_gnn_in['stn3_b'], 'L1_gnn_stn4_w': _L1_gnn_in['stn4_w'], 'L1_gnn_stn4_b': _L1_gnn_in['stn4_b'], 'L1_gnn_conv_w': _L1_gnn_in['conv_w'], 'L1_gnn_conv_b': _L1_gnn_in['conv_b']}

def reference(x, src, dst, edge_attr_3, L0_gnn_W1_l, L0_gnn_W1_r, L0_gnn_b1, L0_gnn_W2_l, L0_gnn_W2_r, L0_gnn_b2, L1_gnn_stn1_w, L1_gnn_stn1_b, L1_gnn_stn2_w, L1_gnn_stn2_b, L1_gnn_stn3_w, L1_gnn_stn3_b, L1_gnn_stn4_w, L1_gnn_stn4_b, L1_gnn_conv_w, L1_gnn_conv_b):
    import jax
    import jax.numpy as jnp

    def _L0_gnn_ref(x, W1_l, W1_r, b1, W2_l, W2_r, b2, edge_index):
        import jax, jax.numpy as jnp
        import numpy as np
        N_NODES = 3125
        N_EDGES = 50000
        IN_C, HID_C, OUT_C = (32, 64, 32)

        def _sage_conv(x, src, dst, W_l, W_r, b, num_nodes):
            msg = x[src]
            agg = jax.ops.segment_sum(msg, dst, num_segments=num_nodes)
            deg = jax.ops.segment_sum(jnp.ones((src.shape[0],), dtype=x.dtype), dst, num_segments=num_nodes)
            mean = agg / jnp.maximum(deg, 1.0)[:, None]
            return mean @ W_l.T + x @ W_r.T + b
        src, dst = (edge_index[0], edge_index[1])
        h = _sage_conv(x, src, dst, W1_l, W1_r, b1, N_NODES)
        h = jax.nn.relu(h)
        out = _sage_conv(h, src, dst, W2_l, W2_r, b2, N_NODES)
        return out

    def _L1_gnn_ref(x, edge_index, pseudo, stn1_w, stn1_b, stn2_w, stn2_b, stn3_w, stn3_b, stn4_w, stn4_b, conv_w, conv_b):
        import jax, jax.numpy as jnp
        import numpy as np
        D = 3
        KS = 5
        K = KS ** D
        S = 2 ** D
        _COMBOS = np.array([[s >> d & 1 for d in range(D)] for s in range(S)], dtype=np.int32)
        _STRIDES = np.array([KS ** (D - 1 - d) for d in range(D)], dtype=np.int32)

        def spline_basis(pseudo):
            pos = pseudo * (KS - 1)
            i0 = jnp.clip(jnp.floor(pos), 0, KS - 2).astype(jnp.int32)
            frac = pos - i0
            combos = jnp.asarray(_COMBOS)
            basis = jnp.prod(jnp.where(combos[None] == 1, frac[:, None, :], 1.0 - frac[:, None, :]), axis=-1)
            idx = jnp.sum((i0[:, None, :] + combos[None]) * jnp.asarray(_STRIDES)[None, None, :], axis=-1)
            return (basis, idx)

        def spline_conv(x, row, col, basis, idx, W, b):
            N = x.shape[0]
            Fout = W.shape[2]
            z = jnp.einsum('ni,kio->nko', x, W).reshape(N * K, Fout)
            gathered = z[col[:, None] * K + idx]
            msg = jnp.einsum('es,eso->eo', basis, gathered)
            out = jax.ops.segment_sum(msg, row, num_segments=N)
            deg = jax.ops.segment_sum(jnp.ones_like(msg[:, 0]), row, num_segments=N)
            return out / jnp.maximum(deg, 1.0)[:, None] + b
        N = x.shape[0]
        row, col = (edge_index[0], edge_index[1])
        basis, idx = spline_basis(pseudo)
        h = jnp.ones((N, 1), x.dtype)
        h = jax.nn.elu(spline_conv(h, row, col, basis, idx, stn1_w, stn1_b))
        h = jax.nn.elu(spline_conv(h, row, col, basis, idx, stn2_w, stn2_b))
        h = jax.nn.elu(h @ stn3_w + stn3_b)
        t = h @ stn4_w + stn4_b
        new_pseudo = jnp.clip(pseudo + t[col] - t[row], 0.0, 1.0)
        basis2, idx2 = spline_basis(new_pseudo)
        return spline_conv(x, row, col, basis2, idx2, conv_w, conv_b)
    edge_index = jnp.stack([src, dst])
    x = _layernorm(x + _L0_gnn_ref(x, L0_gnn_W1_l, L0_gnn_W1_r, L0_gnn_b1, L0_gnn_W2_l, L0_gnn_W2_r, L0_gnn_b2, edge_index), axis=-1)
    x = _layernorm(x + _L1_gnn_ref(x, edge_index, edge_attr_3, L1_gnn_stn1_w, L1_gnn_stn1_b, L1_gnn_stn2_w, L1_gnn_stn2_b, L1_gnn_stn3_w, L1_gnn_stn3_b, L1_gnn_stn4_w, L1_gnn_stn4_b, L1_gnn_conv_w, L1_gnn_conv_b), axis=-1)
    return x

_drawn_inputs = setup_inputs


def setup_inputs(seed=0):
    import zlib

    import numpy as np

    out = dict(_drawn_inputs(seed))
    spreads = {}
    factors = {'L1_gnn_stn1_w': 8.0,
     'L1_gnn_stn1_b': 8.0,
     'L1_gnn_stn2_w': 8.0,
     'L1_gnn_stn2_b': 8.0,
     'L1_gnn_stn3_w': 8.0,
     'L1_gnn_stn3_b': 8.0,
     'L1_gnn_stn4_w': 8.0,
     'L1_gnn_stn4_b': 8.0}
    for name, (base, spread) in spreads.items():
        noise = np.random.default_rng([zlib.crc32(name.encode()), seed]).standard_normal(out[name].shape)
        drawn = base * np.exp(spread * noise) if base else spread * noise
        out[name] = jnp.asarray(drawn.astype(out[name].dtype))
    for name, factor in factors.items():
        out[name] = (out[name] * factor).astype(out[name].dtype)
    return out
```

```python
import concourse.bass as bass
from concourse import mybir
from contextlib import ExitStack

fp32 = mybir.dt.float32
bf16 = mybir.dt.bfloat16
fp16 = mybir.dt.float16
i32 = mybir.dt.int32
i16 = mybir.dt.int16
ALU = mybir.AluOpType
ACT = mybir.ActivationFunctionType
AX = mybir.AxisListType.X

P = 128
N = 3125
E = 53125
F = 32
H = 64
KS = 5
KK = KS ** 3
NCH = -(-N // P)
NPAD = NCH * P
NREM = N - (NCH - 1) * P
CELLS = (KS - 1) ** 3
HALF = 8
RING = 2 * HALF
EC = -(-(-(-E // P)) // RING) * RING
EFULL = E // EC
EREM = E - EFULL * EC
TS = -(-((E + NCH * (P - 1)) // P) // RING) * RING
TC = -(-((E + CELLS * (P - 1)) // P) // RING) * RING
FAR = P * 8192 + P - 1
DSEG = -(-N // 7)
DPAD = 7 * DSEG
RW = 8
CW = 4
XW = 36
assert EFULL == P - 1 and EREM > 0 and NPAD <= 7 * 512


class Chain:

    def __init__(self, eng, sem, base=0):
        self.eng, self.sem, self.base, self.n = eng, sem, base, 0

    def __call__(self, ins):
        self.n += 1
        ins.then_inc(self.sem, 1)
        self.eng.wait_ge(self.sem, self.base + self.n)


def gnn_kernel(nc, x, xT, src, dst, ps, w1l, w1r, b1, w2l, w2r, b2,
               s1w, s1b, s2w, s2b, s3w, s3b, s4w, s4b, cw, cb, out):
    ctx = ExitStack()

    def dram(name, shape, dt=fp32):
        return nc.dram_tensor(name, shape, dt, kind="Internal").ap()

    rec_s = dram("rec_s", (P * TS, RW))
    rec_c = dram("rec_c", (P * TC, CW))
    h1_tab = dram("h1_tab", (NPAD, H))
    msg2 = dram("msg2", (P * TC, H))
    xt_tab = dram("xt_tab", (NPAD, XW))
    rec_d = dram("rec_d", (P * TC, XW))
    msg3 = dram("msg3", (P * TC, F))

    def sb(name, shape, dt=fp32, c=ctx):
        return c.enter_context(nc.sbuf_tensor(name, shape, dt))

    def sem(name, c=ctx):
        return c.enter_context(nc.semaphore(name))

    def pb(name, shape, c, dt=fp32):
        return c.enter_context(nc.psum_tensor(name, shape, dt))

    with ctx:
        iota16 = sb("iota16", [P, DPAD], fp16)
        iota_f = sb("iota_f", [P, 512])
        iota_p = sb("iota_p", [P, 1])
        consts = sem("consts_made")
        ident = sb("ident", [P, P])
        identb = sb("identb", [P, P], bf16)
        tri = sb("tri", [P, P])
        ones = sb("ones", [P, P])
        zeros = sb("zeros", [P, 512])
        tick = sb("tick", [P, 4])

        def hold(held, n):
            nc.gpsimd.wait_ge(held, n)
            nc.gpsimd.tensor_tensor(tick[:, 2:3], zeros[:, 0:1], zeros[:, 0:1], op=ALU.add).then_inc(held, 1)

        xn = sb("xn", [P, NCH, F])
        x1 = sb("x1", [P, NCH, F])
        rdeg_s = sb("rdeg_s", [P, NCH])
        tn3 = sb("tn3", [P, NCH, 9], bf16)
        rs = sb("rs", [P, TS, RW])
        tsrc = sb("tsrc", [P, TS, 3])
        chunk_i = sb("chunk_i", [P, TS], i32)
        cell_i = sb("cell_i", [P, TC], i32)

        def sort_block(tag, key, C, K, T, row, tile_i, c):
            cnt = sb(tag + "cnt", [P, K], c=c)
            base = sb(tag + "base", [P, K], c=c)
            tiles = sb(tag + "tiles", [P, K], c=c)
            endt = sb(tag + "endt", [P, K], c=c)
            ti = sb(tag + "ti", [P, K], i32, c=c)
            ecol = sb(tag + "ecol", [P, 1], c=c)
            mask = sb(tag + "mask", [P, C], i16, c=c)
            run = sb(tag + "run", [P, C], c=c)
            pos = sb(tag + "pos", [P, C], c=c)
            rowlo = sb(tag + "rowlo", [P, C], i32, c=c)
            cmp = sb(tag + "cmp", [P, T], c=c)
            cs = ExitStack()
            with cs:
                pp = pb(tag + "pp", [P, 512], cs)
                pt = pb(tag + "pt", [P, 512], cs)
                v_cnt = sem(tag + "v_cnt", cs)
                pe_px = sem(tag + "pe_px", cs)
                v_cmp = sem(tag + "v_cmp", cs)
                pe_tb = sem(tag + "pe_tb", cs)
                ch = sem(tag + "ch", cs)
                ch2 = sem(tag + "ch2", cs)
                ch3 = sem(tag + "ch3", cs)
                block = cs.enter_context(nc.Block())

                @block.tensor
                def _(pe):
                    pe.wait_ge(v_cnt, K)
                    nc.tensor.matmul(pp[:, 0:K], tri[:, :], cnt[:, :], start=True, stop=True).then_inc(pe_px, 1)
                    nc.tensor.matmul(pt[:, 0:K], ones[:, :], cnt[:, :], start=True, stop=True).then_inc(pe_px, 1)
                    pe.wait_ge(v_cmp, 1)
                    nc.tensor.matmul(pp[:, 0:T], ones[0:K, :], cmp[0:K, :], start=True, stop=True).then_inc(pe_tb, 1)

                @block.vector
                def _(v):
                    with v.Fori(0, K) as b:
                        nc.vector.tensor_scalar(mask[:, :], key, iota_f[:, bass.ds(b, 1)], 0.0, ALU.is_equal,
                                                ALU.add, accum_out=cnt[:, bass.ds(b, 1)]).then_inc(v_cnt, 1)
                        v.wait_ge(v_cnt, b + 1)
                    go = Chain(v, ch)
                    v.wait_ge(pe_px, 2)
                    go(nc.vector.tensor_scalar(ti[:, :], pt[:, 0:K], float(P - 1), None, ALU.add))
                    go(nc.vector.tensor_scalar(ti[:, :], ti[:, :], 7, None, ALU.arith_shift_right))
                    go(nc.vector.tensor_copy(tiles[:, :], ti[:, :]))
                    go(nc.vector.tensor_tensor_scan(endt[:, :], tiles[:, :], zeros[:, 0:K], 0.0, ALU.add, ALU.add))
                    go(nc.vector.tensor_tensor(tiles[:, :], endt[:, :], tiles[:, :], ALU.subtract))
                    go(nc.vector.tensor_scalar(tiles[:, :], tiles[:, :], float(P), -1.0, ALU.mult, ALU.add))
                    go(nc.vector.tensor_tensor(base[:, :], pp[:, 0:K], tiles[:, :], ALU.add))
                    go(nc.vector.tensor_tensor(endt[:, :], endt[:, :], ident[:, 0:K], ALU.mult))
                    go(nc.vector.reduce_sum(ecol[:, :], endt[:, :], axis=AX))
                    nc.vector.tensor_scalar(cmp[:, :], iota_f[:, 0:T], ecol[:, :], None, ALU.is_ge).then_inc(v_cmp, 1)
                    v.wait_ge(pe_tb, 1)
                    go(nc.vector.tensor_scalar(cmp[:, :], pp[:, 0:T], float(K - 1), None, ALU.min))
                    go(nc.vector.tensor_copy(tile_i[:, :], cmp[:, :]))
                    go(nc.vector.memset(pos[:, :], float(FAR)))
                    with v.Fori(0, K) as b:
                        lk = Chain(v, ch2, b * 3)
                        lk(nc.vector.tensor_scalar(mask[:, :], key, iota_f[:, bass.ds(b, 1)], None, ALU.is_equal))
                        lk(nc.vector.tensor_tensor_scan(run[:, :], mask[:, :], zeros[:, 0:C], base[:, bass.ds(b, 1)],
                                                        ALU.add, ALU.add))
                        nc.vector.memset(tick[:, 1:2], 0.0)
                        lk(nc.vector.copy_predicated(pos[:, :], mask[:, :], run[:, :]))
                    g3 = Chain(v, ch3)
                    g3(nc.vector.tensor_copy(row, pos[:, :]))
                    g3(nc.vector.tensor_scalar(rowlo[:, :], row, P - 1, None, ALU.bitwise_and))
                    g3(nc.vector.tensor_scalar(row, row, 7, None, ALU.arith_shift_right))
                    g3(nc.vector.tensor_copy(run[:, :], row))
                    g3(nc.vector.scalar_tensor_tensor(run[:, :], rowlo[:, :], float(T), run[:, :], ALU.mult, ALU.add))
                    g3(nc.vector.tensor_copy(row, run[:, :]))

        def cell_steps(go, p, flo, t, key):
            go(nc.vector.tensor_scalar(flo, p, 1.0, None, ALU.is_ge))
            go(nc.vector.tensor_scalar(t, p, 2.0, None, ALU.is_ge))
            go(nc.vector.tensor_tensor(flo, flo, t, ALU.add))
            go(nc.vector.tensor_scalar(t, p, 3.0, None, ALU.is_ge))
            go(nc.vector.tensor_tensor(flo, flo, t, ALU.add))
            go(nc.vector.tensor_scalar(key, flo[:, :, 0], 16.0, None, ALU.mult))
            go(nc.vector.scalar_tensor_tensor(key, flo[:, :, 1], 4.0, key, ALU.mult, ALU.add))
            go(nc.vector.tensor_tensor(key, key, flo[:, :, 2], ALU.add))
            go(nc.vector.tensor_tensor(flo, p, flo, ALU.subtract))

        def scatter_block(tag, jobs, C):
            cs = ExitStack()
            with cs:
                bufs = [(sb(f"{tag}d{n}", [P, RING, a.shape[2]], c=cs), sb(f"{tag}i{n}", [P, RING], i32, c=cs))
                        for n, (a, _, _, _) in enumerate(jobs)]
                held = sem(tag + "held", cs)
                staged = sem(tag + "staged", cs)
                sent = [sem(f"{tag}sent{h}", cs) for h in range(2)]
                block = cs.enter_context(nc.Block())
                per = 16 * HALF * len(jobs)

                @block.scalar
                def _(act):
                    with act.Fori(0, C // RING) as i:
                        for h in range(2):
                            act.wait_ge(sent[h], i * per)
                            for (a, r, _, _), (d, ix) in zip(jobs, bufs):
                                s = slice(h * HALF, h * HALF + HALF)
                                nc.scalar.copy(d[:, s, :], a[:, bass.ds(i * RING + h * HALF, HALF), :]).then_inc(staged, 1)
                                nc.scalar.copy(ix[:, s], r[:, bass.ds(i * RING + h * HALF, HALF)]).then_inc(staged, 1)

                @block.gpsimd
                def _(pool):
                    with pool.Fori(0, C // RING) as i:
                        for h in range(2):
                            pool.wait_ge(staged, i * (4 * len(jobs)) + (h + 1) * 2 * len(jobs))
                            hold(held, i * 2 + h)
                            for (_, _, tab, rows), (d, ix) in zip(jobs, bufs):
                                for k in range(h * HALF, h * HALF + HALF):
                                    nc.gpsimd.indirect_dma_start(
                                        out=tab, out_offset=bass.IndirectOffsetOnAxis(ap=ix[:, k:k + 1], axis=0),
                                        in_=d[:, k, :], in_offset=None, bounds_check=rows - 1,
                                        oob_is_err=False).then_inc(sent[h], 16)
                    for h in range(2):
                        pool.wait_ge(sent[h], per * (C // RING))

        c1 = ExitStack()
        with c1:
            ei = sb("ei", [P, 2, EC], i32, c=c1)
            ri = sb("ri", [P, EC], i32, c=c1)
            recS = sb("recS", [P, EC, RW], c=c1)
            recC = sb("recC", [P, EC, CW], c=c1)
            key_s = sb("key_s", [P, EC], c=c1)
            key_c = sb("key_c", [P, EC], c=c1)
            pos4 = sb("pos4", [P, EC, 3], c=c1)
            flo = sb("flo", [P, EC, 3], c=c1)
            tmp3 = sb("tmp3", [P, EC, 3], c=c1)
            row_s = sb("row_s", [P, EC], i32, c=c1)
            row_c = sb("row_c", [P, EC], i32, c=c1)
            iota_i = sb("iota_i", [P, 512], i32, c=c1)
            iop_i = sb("iop_i", [P, 1], i32, c=c1)
            pse = sb("pse", [P, EC, 3], c=c1)
            cs = ExitStack()
            with cs:
                fz = sb("fz", [P, TC * XW], c=cs)
                fillS = sb("fillS", [P, TS, RW], c=cs)
                ld = sem("ld", cs)
                fill = sem("fill", cs)
                pre = sem("pre", cs)
                ch = sem("ch0", cs)
                block = cs.enter_context(nc.Block())

                @block.sync
                def _(sp):
                    sp.wait_ge(pre, 1)
                    for n, a in enumerate((src, dst)):
                        sp.dma_start(ei[0:EFULL, n, :], a[0:EFULL * EC].rearrange("(p c) -> p c", c=EC)).then_inc(ld, 16)
                        sp.dma_start(ei[EFULL:P, n, 0:EREM], a[EFULL * EC:E].rearrange("(p c) -> p c", p=1)).then_inc(ld, 16)
                    sp.dma_start(pse[0:EFULL, :, :], ps[0:EFULL * EC, :].rearrange("(p c) d -> p c d", c=EC)).then_inc(ld, 16)
                    sp.dma_start(pse[EFULL:P, 0:EREM, :], ps[EFULL * EC:E, :].rearrange("(p c) d -> p c d", p=1)).then_inc(ld, 16)
                    sp.wait_ge(ld, 96)
                    sp.dma_start(rec_s.rearrange("(p t) w -> p (t w)", p=P), fillS[:, :, :].rearrange("p t w -> p (t w)")).then_inc(fill, 16)
                    sp.dma_start(rec_c.rearrange("(p a) w -> p (a w)", p=P), fz[:, 0:TC * CW]).then_inc(fill, 16)
                    sp.dma_start(rec_d.rearrange("(p a) w -> p a w", p=P)[:, :, :], fz[:, :].rearrange("p (a w) -> p a w", w=XW)).then_inc(fill, 16)
                    sp.wait_ge(fill, 48)

                @block.gpsimd
                def _(g):
                    g.iota(iota_i[:, :], pattern=[[1, 512]], base=0, channel_multiplier=0).then_inc(consts, 1)
                    g.iota(iop_i[:, :], pattern=[[1, 1]], base=0, channel_multiplier=1).then_inc(consts, 1)
                    g.iota(iota16[:, :], pattern=[[1, DPAD]], base=-(N // 2), channel_multiplier=0,
                           allow_small_or_imprecise_dtypes=True).then_inc(consts, 1)
                    g.memset(ones[:, :], 1.0).then_inc(consts, 1)
                    g.memset(zeros[:, :], 0.0).then_inc(consts, 1)
                    g.wait_ge(consts, 5)
                    g.affine_select(out=ident[:, :], in_=ones[:, :], compare_op=ALU.is_equal, fill=0.0,
                                    base=0, pattern=[[-1, P]], channel_multiplier=1).then_inc(consts, 1)
                    g.affine_select(out=tri[:, :], in_=ones[:, :], compare_op=ALU.is_gt, fill=0.0,
                                    base=0, pattern=[[1, P]], channel_multiplier=-1).then_inc(consts, 1)

                @block.vector
                def _(v):
                    go = Chain(v, ch)
                    go(nc.vector.memset(fz[:, :], 0.0))
                    go(nc.vector.memset(fillS[:, :, :], 0.0))
                    go(nc.vector.memset(fillS[:, :, 0:2], -1.0))
                    go(nc.vector.memset(ei[:, :, :], 127 * P))
                    nc.vector.memset(pse[:, :, :], 0.0).then_inc(pre, 1)
                    go(nc.vector.memset(recS[:, :, :], 0.0))
                    v.wait_ge(consts, 7)
                    go(nc.vector.tensor_copy(iota_f[:, :], iota_i[:, :]))
                    go(nc.vector.tensor_copy(iota_p[:, :], iop_i[:, :]))
                    go(nc.vector.tensor_copy(identb[:, :], ident[:, :]))
                    v.wait_ge(ld, 96)
                    go(nc.vector.tensor_scalar(ri[:, :], ei[:, 0, :], 7, None, ALU.arith_shift_right))
                    go(nc.vector.tensor_copy(key_s[:, :], ri[:, :]))
                    go(nc.vector.tensor_scalar(ri[:, :], ei[:, 0, :], P - 1, None, ALU.bitwise_and))
                    go(nc.vector.tensor_copy(recS[:, :, 0], ri[:, :]))
                    go(nc.vector.tensor_copy(recS[:, :, 1], ei[:, 1, :]))
                    go(nc.vector.tensor_copy(recC[:, :, 0], ei[:, 1, :]))
                    go(nc.vector.tensor_copy(recS[:, :, 2:5], pse[:, :, :]))
                    go(nc.vector.tensor_scalar(pos4[:, :, :], pse[:, :, :], float(KS - 1), None, ALU.mult))
                    cell_steps(go, pos4[:, :, :], flo[:, :, :], tmp3[:, :, :], key_c[:, :])
                    go(nc.vector.tensor_copy(recC[:, :, 1:4], flo[:, :, :]))
                    go(nc.vector.tensor_scalar(tmp3[:, :, 0], key_s[:, :], 100.0, 1000.0, ALU.is_ge, ALU.mult))
                    go(nc.vector.tensor_tensor(key_c[:, :], key_c[:, :], tmp3[:, :, 0], ALU.add))

            c2 = ExitStack()
            with c2:
                sort_block("ss", key_s[:, :], EC, NCH, TS, row_s[:, :], chunk_i, c2)
            c2 = ExitStack()
            with c2:
                sort_block("sc", key_c[:, :], EC, CELLS, TC, row_c[:, :], cell_i, c2)
            cs = ExitStack()
            with cs:
                ch = sem("ch1", cs)
                block = cs.enter_context(nc.Block())

                @block.vector
                def _(v):
                    Chain(v, ch)(nc.vector.tensor_copy(recS[:, :, 5], row_c[:, :]))

            scatter_block("xs", [(recS, row_s, rec_s, P * TS), (recC, row_c, rec_c, P * TC)], EC)

        def load_ids(pe, table, i, h):
            return [pe.value_load(table[0:1, bass.ds(i * RING + h * HALF + k, 1)], min_val=0,
                                  max_val=CELLS - 1 if table is cell_i else NCH - 1) for k in range(HALF)]

        def onehots(out_, h, i, dt_out=None):
            return nc.vector.tensor_tensor(
                out_, iota_f[:, None, 0:P].to_broadcast([P, HALF, P]),
                rs[:, bass.ds(i * RING + h * HALF, HALF), 0:1].to_broadcast([P, HALF, P]), ALU.is_equal)


        def split3(go, a, parts, rest):
            go(nc.vector.tensor_copy(parts[0], a))
            go(nc.vector.tensor_tensor(rest, a, parts[0], ALU.subtract))
            go(nc.vector.tensor_copy(parts[1], rest))
            go(nc.vector.tensor_tensor(rest, rest, parts[1], ALU.subtract))
            go(nc.vector.tensor_copy(parts[2], rest))

        def elu_steps(v, go, h, low, exp_ready, exp_done, n):
            nc.vector.tensor_scalar(low, h, 0.0, None, ALU.min).then_inc(exp_ready, 1)
            go(nc.vector.tensor_scalar(h, h, 0.0, None, ALU.max))
            v.wait_ge(exp_done, n)
            go(nc.vector.scalar_tensor_tensor(h, low, 1.0, h, ALU.subtract, ALU.add))

        def cell_loop(tag, win, wout, w, koff, wt, rows, table, linear, msg):
            cs = ExitStack()
            with cs:
                wrow = XW if linear is not None else win
                u = sb(tag + "u", [P, RING, wrow], c=cs)
                ix = sb(tag + "ix", [P, RING], i32, c=cs)
                ut = sb(tag + "ut", [win, 2, HALF, P], c=cs)
                pr = sb(tag + "pr", [P, 2, 2, 8, wout], c=cs)
                m = sb(tag + "m", [P, RING, wout], c=cs)
                tp = pb(tag + "tp", [win, 2, HALF, P], cs)
                z = pb(tag + "z", [P, 4, 512], cs)
                got = [sem(f"{tag}got{h}", cs) for h in range(2)]
                held = sem(tag + "held", cs)
                staged = sem(tag + "staged", cs)
                trd = sem(tag + "trd", cs)
                tev = sem(tag + "tev", cs)
                zd = sem(tag + "zd", cs)
                zu = sem(tag + "zu", cs)
                red = sem(tag + "red", cs)
                put = [sem(f"{tag}put{h}", cs) for h in range(2)]
                block = cs.enter_context(nc.Block())
                n_it = TC // RING
                per = 16 if linear is not None else 16 * HALF
                msg_v = msg.rearrange("(p t) f -> p t f", p=P)

                @block.scalar
                def _(act):
                    with act.Fori(0, n_it) as i:
                        for h in range(2):
                            s = slice(h * HALF, h * HALF + HALF)
                            if linear is None:
                                act.wait_ge(got[h], i * per)
                                nc.scalar.copy(ix[:, s], rows[:, bass.ds(i * RING + h * HALF, HALF)]).then_inc(staged, 1)
                        for h in range(2):
                            act.wait_ge(trd, i * 2 + h + 1)
                            act.wait_ge(zd, (i * 2 + h) * 4)
                            nc.scalar.copy(ut[:, h, :, :], tp[:, h, :, :]).then_inc(tev, 1)

                def load(eng):
                    with eng.Fori(0, n_it) as i:
                        for h in range(2):
                            s = slice(h * HALF, h * HALF + HALF)
                            if linear is None:
                                eng.wait_ge(staged, i * 2 + h + 1)
                            else:
                                eng.wait_ge(trd, i * 2)
                            if linear is None:
                                eng.wait_ge(trd, i * 2)
                                hold(held, i * 2 + h)
                                for k in range(h * HALF, h * HALF + HALF):
                                    nc.gpsimd.indirect_dma_start(
                                        out=u[:, k, :], out_offset=None, in_=table,
                                        in_offset=bass.IndirectOffsetOnAxis(ap=ix[:, k:k + 1], axis=0),
                                        bounds_check=NPAD - 1, oob_is_err=False).then_inc(got[h], 16)
                            else:
                                eng.dma_start(u[:, s, :], linear.rearrange("(p t) f -> p t f", p=P)
                                              [:, bass.ds(i * RING + h * HALF, HALF), :]).then_inc(got[h], 16)

                if linear is None:
                    block.gpsimd(load)
                else:
                    block.gpsimd(load)

                @block.sync
                def _(sp):
                    with sp.Fori(0, n_it) as i:
                        for h in range(2):
                            sp.wait_ge(red, (i * 2 + h + 1) * 4)
                            sp.dma_start(msg_v[:, bass.ds(i * RING + h * HALF, HALF), :],
                                         m[:, h * HALF:h * HALF + HALF, :]).then_inc(put[h], 16)
                    for h in range(2):
                        sp.wait_ge(put[h], 16 * n_it)

                @block.tensor
                def _(pe):
                    with pe.Fori(0, n_it) as i:
                        for h in range(2):
                            pe.wait_ge(got[h], (i + 1) * per)
                            pe.wait_ge(tev, i * 2)
                            nc.tensor.matmul(tp[:, h, 0, 0:1], u[:, h * HALF, 0:win], ident[:, 0:1], start=True, stop=True)
                            for k in range(HALF):
                                last = nc.tensor.transpose(tp[:, h, k, :], u[:, h * HALF + k, 0:win], ident[:, :])
                            last.then_inc(trd, 1)
                            for q in range(HALF // 2):
                                if q == 0:
                                    pe.wait_ge(tev, i * 2 + h + 1)
                                if q >= 2:
                                    pe.wait_ge(zu, (i * 2 + h) * 4 + q - 1)
                                elif h == 1:
                                    pe.wait_ge(zu, i * 8 + 4 + q - 1)
                                else:
                                    pe.wait_ge(zu, i * 8)
                                for k in (2 * q, 2 * q + 1):
                                    r = pe.value_load(koff[0:1, bass.ds(i * RING + h * HALF + k, 1)], min_val=0, max_val=93)
                                    sub = w[:, bass.ds(r * wout, wout)]
                                    ker = bass.AP(sub.tensor, sub.offset,
                                                  [sub.ap[0], (KS * KS * wout, 2), (KS * wout, 2), (1, 2 * wout)])
                                    last = nc.tensor.matmul(z[:, (q % 2) * 2 + k % 2, 0:8 * wout],
                                                            ut[:, h, k, :], ker, start=True, stop=True)
                                last.then_inc(zd, 1)

                @block.vector
                def _(v):
                    with v.Fori(0, n_it) as i:
                        for h in range(2):
                            for q in range(HALF // 2):
                                n = (i * 2 + h) * 4 + q
                                b = q % 2
                                v.wait_ge(zd, n + 1)
                                nc.vector.tensor_tensor(
                                    pr[:, b, :, :, :].rearrange("p t s o -> p (t s) o"),
                                    z[:, 2 * b:2 * b + 2, 0:8 * wout].rearrange("p t (s o) -> p t s o", s=8),
                                    wt[:, bass.ds(i * RING + h * HALF + 2 * q, 2), :, None].to_broadcast([P, 2, 8, wout])
                                    if False else
                                    wt[:, bass.ds(i * RING + h * HALF + 2 * q, 2), :, None].to_broadcast([P, 2, 8, wout]),
                                    ALU.mult).then_inc(zu, 1)
                                v.wait_ge(zu, n + 1)
                                if q == 0:
                                    v.wait_ge(put[h], i * 16)
                                nc.vector.reduce_sum(
                                    m[:, h * HALF + 2 * q:h * HALF + 2 * q + 2, :],
                                    pr[:, b, :, :, :].rearrange("p t s o -> p t o s"), axis=AX).then_inc(red, 1)

        def segment_loop(tag, width, rows, msg, acc):
            cs = ExitStack()
            with cs:
                g = sb(tag + "g", [P, RING, width], c=cs)
                ix = sb(tag + "ix", [P, RING], i32, c=cs)
                oh = sb(tag + "oh", [P, 2, HALF, P], c=cs)
                got = [sem(f"{tag}got{h}", cs) for h in range(2)]
                held = sem(tag + "held", cs)
                staged = sem(tag + "staged", cs)
                made = sem(tag + "made", cs)
                used = sem(tag + "used", cs)
                block = cs.enter_context(nc.Block())
                n_it = TS // RING
                per = 16 * HALF

                @block.scalar
                def _(act):
                    with act.Fori(0, n_it) as i:
                        for h in range(2):
                            act.wait_ge(got[h], i * per)
                            nc.scalar.copy(ix[:, h * HALF:h * HALF + HALF],
                                           rows[:, bass.ds(i * RING + h * HALF, HALF)]).then_inc(staged, 1)

                @block.gpsimd
                def _(pool):
                    with pool.Fori(0, n_it) as i:
                        for h in range(2):
                            pool.wait_ge(staged, i * 2 + h + 1)
                            pool.wait_ge(used, i * 2)
                            hold(held, i * 2 + h)
                            for k in range(h * HALF, h * HALF + HALF):
                                nc.gpsimd.indirect_dma_start(
                                    out=g[:, k, :], out_offset=None, in_=msg,
                                    in_offset=bass.IndirectOffsetOnAxis(ap=ix[:, k:k + 1], axis=0),
                                    bounds_check=P * TC - 1, oob_is_err=False).then_inc(got[h], 16)

                @block.vector
                def _(v):
                    with v.Fori(0, n_it) as i:
                        for h in range(2):
                            v.wait_ge(used, i * 2)
                            onehots(oh[:, h, :, :], h, i).then_inc(made, 1)

                @block.tensor
                def _(pe):
                    flat = acc[:, :, :].rearrange("p a b -> p (a b)")
                    for s in range(acc.shape[1]):
                        nc.tensor.matmul(acc[:, s, :], zeros[:, 0:P], zeros[:, :], start=True, stop=True)
                    with pe.Fori(0, n_it) as i:
                        for h in range(2):
                            ids = load_ids(pe, chunk_i, i, h)
                            pe.wait_ge(made, i * 2 + h + 1)
                            pe.wait_ge(got[h], (i + 1) * per)
                            for k in range(HALF):
                                last = nc.tensor.matmul(flat[:, bass.ds(ids[k] * width, width)], oh[:, h, k, :],
                                                        g[:, h * HALF + k, :], start=False, stop=True, skip_group_check=True)
                            last.then_inc(used, 1)

        def norm_steps(v, go, y, o, mean, sq, rootd, root_ready, n):
            bc = lambda a: a[:, :, None].to_broadcast([P, NCH, F])
            go(nc.vector.reduce_sum(mean[:, :], y, axis=AX))
            go(nc.vector.tensor_scalar(mean[:, :], mean[:, :], 1.0 / F, None, ALU.mult))
            go(nc.vector.tensor_tensor(o, y, bc(mean), ALU.subtract))
            go(nc.vector.tensor_tensor(sq[:, :, :], o, o, ALU.mult))
            go(nc.vector.reduce_sum(mean[:, :], sq[:, :, :], axis=AX))
            nc.vector.tensor_scalar(mean[:, :], mean[:, :], 1.0 / F, 1e-5, ALU.mult, ALU.add).then_inc(root_ready, 1)
            v.wait_ge(rootd, n)
            go(nc.vector.reciprocal(mean[:, :], mean[:, :]))
            go(nc.vector.tensor_tensor(o, o, bc(mean), ALU.mult))

        c_oht = ExitStack()
        with c_oht:
            oht = sb("oht", [P, TS, P], bf16, c=c_oht)
            c3 = ExitStack()
            with c3:
                hat = sb("hat", [P, TS, 3, KS], c=c3)
                cs = ExitStack()
                with cs:
                    pp4 = sb("pp4", [P, TS, 3], c=cs)
                    ta = sb("ta", [P, TS, 3], c=cs)
                    ld = sem("ldB", cs)
                    ch = sem("chB", cs)
                    block = cs.enter_context(nc.Block())

                    @block.sync
                    def _(sp):
                        sp.dma_start(rs[:, :, :].rearrange("p t w -> p (t w)"),
                                     rec_s.rearrange("(p t) w -> p (t w)", p=P)).then_inc(ld, 16)

                    @block.vector
                    def _(v):
                        go = Chain(v, ch)
                        v.wait_ge(ld, 16)
                        p, t = pp4[:, :, :], ta[:, :, :]
                        hk = lambda k: hat[:, :, :, k]
                        go(nc.vector.tensor_scalar(p, rs[:, :, 2:5], float(KS - 1), None, ALU.mult))
                        go(nc.vector.tensor_scalar(t, p, -1.0, 1.0, ALU.mult, ALU.add))
                        go(nc.vector.tensor_scalar(hk(0), t, 0.0, None, ALU.max))
                        go(nc.vector.tensor_scalar(t, p, -1.0, 2.0, ALU.mult, ALU.add))
                        go(nc.vector.scalar_tensor_tensor(hk(1), t, 0.0, p, ALU.max, ALU.min))
                        go(nc.vector.tensor_scalar(t, p, -1.0, 3.0, ALU.mult, ALU.add))
                        go(nc.vector.scalar_tensor_tensor(t, p, 1.0, t, ALU.subtract, ALU.min))
                        go(nc.vector.tensor_scalar(hk(2), t, 0.0, None, ALU.max))
                        go(nc.vector.tensor_scalar(t, p, 2.0, 0.0, ALU.subtract, ALU.max))
                        go(nc.vector.tensor_scalar(hk(3), p, -1.0, 4.0, ALU.mult, ALU.add))
                        go(nc.vector.tensor_tensor(hk(3), hk(3), t, ALU.min))
                        go(nc.vector.tensor_scalar(hk(4), p, 3.0, 0.0, ALU.subtract, ALU.max))

                cp = ExitStack()
                with cp:
                    acc = pb("acc1", [P, 7, 512], cp)
                    cs = ExitStack()
                    with cs:
                        ohf = sb("ohf", [P, 2, HALF, P], c=cs)
                        ohb = sb("ohb", [P, 2, HALF, P], bf16, c=cs)
                        b01 = sb("b01", [P, 2, HALF, KS * KS], c=cs)
                        bas = sb("bas", [P, 2, HALF, KK + 1], c=cs)
                        tp = pb("tp1", [P, HALF, P], cs, bf16)
                        made = sem("made", cs)
                        chv = sem("chv", cs)
                        used = sem("used", cs)
                        trd = sem("trd", cs)
                        tev = sem("tev", cs)
                        ini = sem("ini1", cs)
                        block = cs.enter_context(nc.Block())

                        @block.vector
                        def _(v):
                            nc.vector.memset(bas[:, :, :, KK:KK + 1], 1.0).then_inc(ini, 1)
                            v.wait_ge(ini, 1)
                            with v.Fori(0, TS // RING) as i:
                                for h in range(2):
                                    v.wait_ge(used, i * 2)
                                    v.wait_ge(trd, i * 2)
                                    at = bass.ds(i * RING + h * HALF, HALF)
                                    lk = Chain(v, chv, i * 4 + h * 2)
                                    lk(onehots(ohf[:, h, :, :], h, i))
                                    nc.vector.tensor_copy(ohb[:, h, :, :], ohf[:, h, :, :])
                                    lk(nc.vector.tensor_tensor(
                                        b01[:, h, :, :].rearrange("p t (a b) -> p t a b", a=KS),
                                        hat[:, at, 0, :, None].to_broadcast([P, HALF, KS, KS]),
                                        hat[:, at, 1, None, :].to_broadcast([P, HALF, KS, KS]), ALU.mult))
                                    nc.vector.tensor_tensor(
                                        bas[:, h, :, 0:KK].rearrange("p t (a b) -> p t a b", b=KS),
                                        b01[:, h, :, :, None].to_broadcast([P, HALF, KS * KS, KS]),
                                        hat[:, at, 2, None, :].to_broadcast([P, HALF, KS * KS, KS]),
                                        ALU.mult).then_inc(made, 1)

                        @block.tensor
                        def _(pe):
                            flat = acc[:, :, :].rearrange("p a b -> p (a b)")
                            for s in range(7):
                                nc.tensor.matmul(acc[:, s, :], zeros[:, 0:P], zeros[:, :], start=True, stop=True)
                            with pe.Fori(0, TS // RING) as i:
                                for h in range(2):
                                    ids = load_ids(pe, chunk_i, i, h)
                                    pe.wait_ge(made, i * 2 + h + 1)
                                    pe.wait_ge(tev, i * 2 + h)
                                    for k in range(HALF):
                                        last = nc.tensor.transpose(tp[:, k, :], ohb[:, h, k, :], identb[:, :])
                                    last.then_inc(trd, 1)
                                    for k in range(HALF):
                                        last = nc.tensor.matmul(flat[0:KK + 1, bass.ds(ids[k] * P, P)], bas[:, h, k, :],
                                                                ohf[:, h, k, :], start=False, stop=True, skip_group_check=True)
                                    last.then_inc(used, 1)

                        @block.scalar
                        def _(act):
                            with act.Fori(0, TS // RING) as i:
                                for h in range(2):
                                    act.wait_ge(trd, i * 2 + h + 1)
                                    nc.scalar.copy(oht[:, bass.ds(i * RING + h * HALF, HALF), :], tp[:, :, :]).then_inc(tev, 1)

                    s1acc = sb("s1acc", [KK + 1, NPAD], c=c3)
                    cs = ExitStack()
                    with cs:
                        cpd = sem("cpd", cs)
                        block = cs.enter_context(nc.Block())

                        @block.vector
                        def _(v):
                            nc.vector.tensor_copy(s1acc[:, :], acc[:, :, :].rearrange("p a b -> p (a b)")[0:KK + 1, 0:NPAD]).then_inc(cpd, 1)
                            v.wait_ge(cpd, 1)

                cs = ExitStack()
                with cs:
                    w1x = sb("w1x", [KK + 1, H + 1], c=cs)
                    bb1 = sb("bb1", [P, H], c=cs)
                    h1 = sb("h1", [P, NCH, H + 1], c=cs)
                    low = sb("low", [P, NCH, H], c=cs)
                    hp = pb("hp", [P, 4, 512], cs)
                    ld = sem("ldC", cs)
                    wz = sem("wz", cs)
                    ch = sem("chC", cs)
                    h1p = sem("h1p", cs)
                    er = sem("er", cs)
                    ed = sem("ed", cs)
                    st = sem("stC", cs)
                    h1d = sem("h1d", cs)
                    block = cs.enter_context(nc.Block())

                    @block.sync
                    def _(sp):
                        sp.wait_ge(wz, 1)
                        sp.dma_start(w1x[0:KK, 0:H], s1w.rearrange("k a h -> k (a h)")).then_inc(ld, 16)
                        sp.dma_start(w1x[KK:KK + 1, H:H + 1], ones[0:1, 0:1]).then_inc(ld, 16)
                        sp.dma_start(bb1[:, :], s1b.rearrange("(a n) -> a n", a=1).to_broadcast([P, H])).then_inc(ld, 16)
                        sp.wait_ge(h1d, 1)
                        sp.dma_start(h1_tab.rearrange("(c p) h -> p c h", p=P), h1[:, :, 0:H]).then_inc(st, 16)
                        sp.wait_ge(st, 16)

                    @block.tensor
                    def _(pe):
                        pe.wait_ge(ld, 48)
                        for c in range(NCH):
                            last = nc.tensor.matmul(hp[:, c // 7, (c % 7) * (H + 1):(c % 7 + 1) * (H + 1)],
                                                    s1acc[:, c * P:(c + 1) * P], w1x[:, :], start=True, stop=True)
                        last.then_inc(h1p, 1)

                    @block.scalar
                    def _(act):
                        act.wait_ge(er, 1)
                        nc.scalar.activation(low[:, :, :], low[:, :, :], ACT.Exp).then_inc(ed, 1)

                    @block.vector
                    def _(v):
                        nc.vector.memset(w1x[:, :], 0.0).then_inc(wz, 1)
                        go = Chain(v, ch)
                        v.wait_ge(h1p, 1)
                        v.wait_ge(ld, 48)
                        for b in range(4):
                            n = min(7, NCH - 7 * b)
                            go(nc.vector.tensor_copy(h1[:, 7 * b:7 * b + n, :].rearrange("p c h -> p (c h)"), hp[:, b, 0:n * (H + 1)]))
                        go(nc.vector.tensor_scalar(rdeg_s[:, :], h1[:, :, H], 1.0, None, ALU.max))
                        go(nc.vector.reciprocal(rdeg_s[:, :], rdeg_s[:, :]))
                        hh = h1[:, :, 0:H]
                        go(nc.vector.tensor_tensor(hh, hh, rdeg_s[:, :, None].to_broadcast([P, NCH, H]), ALU.mult))
                        go(nc.vector.tensor_tensor(hh, hh, bb1[:, None, :].to_broadcast([P, NCH, H]), ALU.add))
                        elu_steps(v, go, hh, low[:, :, :], er, ed, 1)
                        nc.vector.memset(low[0:1, 0, 0:1], 0.0).then_inc(h1d, 1)

            dstc = sb("dstc", [P, TS], c=c_oht)

            def sage_loop(tag, tab3, acc):
                cs = ExitStack()
                with cs:
                    d = sb(tag + "d", [P, 2, DPAD], bf16, c=cs)
                    gs = sb(tag + "gs", [P, 4, 4, P], bf16, c=cs)
                    gp = pb(tag + "gp", [P, 512], cs)
                    dm = sem(tag + "dm", cs)
                    du = sem(tag + "du", cs)
                    gd = sem(tag + "gd", cs)
                    ge = sem(tag + "ge", cs)
                    ini = sem(tag + "ini", cs)
                    block = cs.enter_context(nc.Block())

                    @block.vector
                    def _(v):
                        nc.vector.memset(gs[:, :, :, 3 * F:P], 1.0).then_inc(ini, 1)
                        with v.Fori(0, TS // RING) as i:
                            for k in range(RING):
                                v.wait_ge(du, i * RING + max(k - 1, 0))
                                nc.vector.tensor_scalar(d[:, k % 2, :], iota16[:, :], dstc[:, bass.ds(i * RING + k, 1)],
                                                        None, ALU.is_equal).then_inc(dm, 1)

                    @block.scalar
                    def _(act):
                        act.wait_ge(ini, 1)
                        with act.Fori(0, TS // RING) as i:
                            for q in range(4):
                                act.wait_ge(gd, i * 4 + q + 1)
                                act.wait_ge(du, i * RING)
                                nc.scalar.copy(gs[:, q, :, 0:3 * F], gp[:, 0:12 * F].rearrange("p (a b) -> p a b", a=4)).then_inc(ge, 1)

                    @block.tensor
                    def _(pe):
                        for s in range(7):
                            nc.tensor.matmul(acc[:, s, :], zeros[:, 0:P], zeros[:, :], start=True, stop=True)
                        with pe.Fori(0, TS // RING) as i:
                            for q in range(4):
                                pe.wait_ge(ge, i * 4 + q)
                                for k in range(4):
                                    r = pe.value_load(chunk_i[0:1, bass.ds(i * RING + q * 4 + k, 1)], min_val=0, max_val=NCH - 1)
                                    oh = oht[:, bass.ds(i * RING + q * 4 + k, 1), :].rearrange("p a b -> p (a b)")
                                    last = nc.tensor.matmul(gp[:, k * 3 * F:(k + 1) * 3 * F], oh,
                                                            tab3[:, bass.ds(r * 3 * F, 3 * F)], start=True, stop=True)
                                last.then_inc(gd, 1)
                                pe.wait_ge(ge, i * 4 + q + 1)
                                for k in range(4):
                                    t = q * 4 + k
                                    pe.wait_ge(dm, i * RING + t + 1)
                                    for s in range(7):
                                        last = nc.tensor.matmul(acc[:, s, 0:DSEG], gs[:, q, k, :], d[:, t % 2, s * DSEG:(s + 1) * DSEG],
                                                                start=False, stop=True, skip_group_check=True)
                                    last.then_inc(du, 1)

            c4 = ExitStack()
            with c4:
                x3 = sb("x3", [P, NCH, 3 * F], bf16, c=c4)
                agg = sb("agg", [P, NPAD], c=c4)
                q2 = sb("q2", [P, NCH, F], c=c4)
                wa = sb("wa", [P, H], c=c4)
                wd = sb("wd", [P, H], c=c4)
                wr1 = sb("wr1", [F, H], c=c4)
                w2 = sb("w2", [H, 2 * F], c=c4)
                bc1 = sb("bc1", [H, 1], c=c4)
                bb2 = sb("bb2", [P, F], c=c4)
                fold = sb("fold", [P, F + 1], c=c4)
                cs = ExitStack()
                with cs:
                    rest = sb("rest", [P, NCH, F], c=cs)
                    ld = sem("ldD", cs)
                    ldx = sem("ldx", cs)
                    ch = sem("chD", cs)
                    wz = sem("wzD", cs)
                    block = cs.enter_context(nc.Block())

                    @block.sync
                    def _(sp):
                        sp.wait_ge(wz, 2)
                        sp.dma_start(xn[:, 0:NCH - 1, :], x[0:(NCH - 1) * P, :].rearrange("(c p) f -> p c f", p=P)).then_inc(ldx, 16)
                        sp.dma_start(xn[0:NREM, NCH - 1, :], x[(NCH - 1) * P:N, :]).then_inc(ldx, 16)
                        for k in range(3):
                            sp.dma_start(wa[k * F:(k + 1) * F, :], w1l).then_inc(ld, 16)
                        sp.dma_start(wd[3 * F:3 * F + 1, :], ones[0:1, 0:H]).then_inc(ld, 16)
                        sp.dma_start(wr1[:, :], w1r).then_inc(ld, 16)
                        sp.dma_start(w2[:, 0:F], w2l).then_inc(ld, 16)
                        sp.dma_start(w2[:, F:2 * F], w2r).then_inc(ld, 16)
                        sp.dma_start(bc1[:, :], b1.rearrange("(n a) -> n a", a=1)).then_inc(ld, 16)
                        sp.dma_start(bb2[:, :], b2.rearrange("(a n) -> a n", a=1).to_broadcast([P, F])).then_inc(ld, 16)
                        for k in range(3):
                            sp.dma_start(fold[k * F:(k + 1) * F, 0:F], ident[0:F, 0:F]).then_inc(ld, 16)
                        sp.dma_start(fold[3 * F:3 * F + 1, F:F + 1], ones[0:1, 0:1]).then_inc(ld, 16)
                        sp.wait_ge(ld, 16 * 13)

                    @block.vector
                    def _(v):
                        nc.vector.memset(xn[:, :, :], 0.0).then_inc(wz, 1)
                        nc.vector.memset(wa[:, :], 0.0)
                        nc.vector.memset(fold[:, :], 0.0)
                        nc.vector.memset(wd[:, :], 0.0).then_inc(wz, 1)
                        go = Chain(v, ch)
                        go(nc.vector.tensor_scalar(dstc[:, :], rs[:, :, 1], float(N // 2), None, ALU.subtract))
                        v.wait_ge(ldx, 32)
                        split3(go, xn[:, :, :], [x3[:, :, k * F:(k + 1) * F] for k in range(3)], rest[:, :, :])

                def sage_sum(tag, tab3):
                    cp = ExitStack()
                    with cp:
                        acc = pb(tag + "acc", [P, 7, 512], cp)
                        sage_loop(tag, tab3[:, :, :].rearrange("p c f -> p (c f)"), acc)
                        cs = ExitStack()
                        with cs:
                            cpd = sem(tag + "cpd", cs)
                            block = cs.enter_context(nc.Block())

                            @block.vector
                            def _(v):
                                nc.vector.memset(agg[:, N:NPAD], 0.0).then_inc(cpd, 1)
                                v.wait_ge(cpd, 1)
                                nc.vector.tensor_copy(agg[:, 0:6 * DSEG].rearrange("p (a b) -> p a b", a=6), acc[:, 0:6, 0:DSEG])
                                nc.vector.tensor_copy(agg[:, 6 * DSEG:N], acc[:, 6, 0:N - 6 * DSEG]).then_inc(cpd, 1)
                                v.wait_ge(cpd, 2)

                sage_sum("g1", x3)

                cs = ExitStack()
                with cs:
                    xt = sb("xt", [F, NPAD], c=cs)
                    hT = sb("hT", [H, NPAD], c=cs)
                    tmp = sb("tmph", [H, 2, 512], c=cs)
                    rest = agg[:, 0:NCH * F].rearrange("p (c f) -> p c f", f=F)
                    pn = agg[:, NCH * F:2 * NCH * F].rearrange("p (c f) -> p c f", f=F)
                    pa = pb("pa", [H, 512], cs)
                    pd = pb("pd", [H, 512], cs)
                    pr_ = pb("prr", [H, 512], cs)
                    pq = pb("pq", [P, 4, 512], cs)
                    ld = sem("ldE", cs)
                    mm = sem("mmE", cs)
                    fr = sem("frE", cs)
                    ch = sem("chE", cs)
                    rl = sem("rlE", cs)
                    pqd = sem("pqd", cs)
                    wz = sem("wzE", cs)
                    block = cs.enter_context(nc.Block())

                    @block.sync
                    def _(sp):
                        sp.wait_ge(wz, 1)
                        sp.dma_start(xt[:, 0:N], xT).then_inc(ld, 16)

                    @block.tensor
                    def _(pe):
                        pe.wait_ge(ld, 16)
                        for s in range(7):
                            w = min(512, NPAD - s * 512)
                            c = slice(s * 512, s * 512 + w)
                            if s:
                                pe.wait_ge(fr, s)
                            nc.tensor.matmul(pa[:, 0:w], wa[:, :], agg[:, c], start=True, stop=True)
                            nc.tensor.matmul(pd[:, 0:w], wd[:, :], agg[:, c], start=True, stop=True)
                            nc.tensor.matmul(pr_[:, 0:w], wr1[:, :], xt[:, c], start=True, stop=True).then_inc(mm, 1)
                        pe.wait_ge(rl, 7)
                        for c in range(NCH):
                            last = nc.tensor.matmul(pq[:, c // 8, (c % 8) * H:(c % 8 + 1) * H], hT[:, c * P:(c + 1) * P], w2[:, :],
                                                    start=True, stop=True)
                        last.then_inc(pqd, 1)

                    @block.scalar
                    def _(act):
                        for s in range(7):
                            w = min(512, NPAD - s * 512)
                            act.wait_ge(fr, s + 1)
                            nc.scalar.activation(hT[:, s * 512:s * 512 + w], tmp[:, s % 2, 0:w], ACT.Relu, bias=bc1[:, :]).then_inc(rl, 1)

                    @block.vector
                    def _(v):
                        nc.vector.memset(xt[:, :], 0.0).then_inc(wz, 1)
                        go = Chain(v, ch)
                        for s in range(7):
                            w = min(512, NPAD - s * 512)
                            v.wait_ge(mm, s + 1)
                            if s >= 2:
                                v.wait_ge(rl, s - 1)
                            a = tmp[:, s % 2, 0:w]
                            go(nc.vector.tensor_scalar(a, pd[:, 0:w], 1.0, None, ALU.max))
                            go(nc.vector.reciprocal(a, a))
                            go(nc.vector.tensor_tensor(a, a, pa[:, 0:w], ALU.mult))
                            nc.vector.tensor_tensor(a, a, pr_[:, 0:w], ALU.add).then_inc(fr, 1)
                        v.wait_ge(pqd, 1)
                        for b in range(4):
                            n = min(8, NCH - 8 * b)
                            view = pq[:, b, 0:n * H].rearrange("p (c f) -> p c f", f=H)
                            go(nc.vector.tensor_copy(pn[:, 8 * b:8 * b + n, :], view[:, :, 0:F]))
                            go(nc.vector.tensor_tensor(q2[:, 8 * b:8 * b + n, :], view[:, :, F:H],
                                                       bb2[:, None, :].to_broadcast([P, n, F]), ALU.add))
                        split3(go, pn[:, :, :], [x3[:, :, k * F:(k + 1) * F] for k in range(3)], rest[:, :, :])

                sage_sum("g2", x3)

                cs = ExitStack()
                with cs:
                    pf = pb("pf", [P, 2, 512], cs)
                    y = sb("yE", [P, NCH, F], c=cs)
                    rd = sb("rdE", [P, NCH], c=cs)
                    mean = sb("meanE", [P, NCH], c=cs)
                    sq = sb("sqE", [P, NCH, F], c=cs)
                    fd = sem("fdF", cs)
                    ch = sem("chF", cs)
                    rr = sem("rrF", cs)
                    rt = sem("rtF", cs)
                    block = cs.enter_context(nc.Block())
                    CB = 512 // (F + 1)

                    @block.tensor
                    def _(pe):
                        for c in range(NCH):
                            last = nc.tensor.matmul(pf[:, c // CB, (c % CB) * (F + 1):(c % CB + 1) * (F + 1)],
                                                    agg[:, c * P:(c + 1) * P], fold[:, :], start=True, stop=True)
                        last.then_inc(fd, 1)

                    @block.scalar
                    def _(act):
                        act.wait_ge(rr, 1)
                        nc.scalar.activation(mean[:, :], mean[:, :], ACT.Sqrt).then_inc(rt, 1)

                    @block.vector
                    def _(v):
                        go = Chain(v, ch)
                        v.wait_ge(fd, 1)
                        for b in range(2):
                            n = min(CB, NCH - CB * b)
                            view = pf[:, b, 0:n * (F + 1)].rearrange("p (c f) -> p c f", f=F + 1)
                            s = slice(CB * b, CB * b + n)
                            go(nc.vector.tensor_scalar(rd[:, s], view[:, :, F], 1.0, None, ALU.max))
                            go(nc.vector.reciprocal(rd[:, s], rd[:, s]))
                            go(nc.vector.tensor_tensor(y[:, s, :], view[:, :, 0:F], rd[:, s, None].to_broadcast([P, n, F]), ALU.mult))
                        go(nc.vector.tensor_tensor(y[:, :, :], y[:, :, :], q2[:, :, :], ALU.add))
                        go(nc.vector.tensor_tensor(y[:, :, :], y[:, :, :], xn[:, :, :], ALU.add))
                        norm_steps(v, go, y[:, :, :], x1[:, :, :], mean, sq, rt, rr, 1)

        c9 = ExitStack()
        with c9:
            koff = sb("koff", [P, TC], i32, c=c9)
            dst_i = sb("dst_i", [P, TS], i32, c=c9)
            posc_i = sb("posc_i", [P, TS], i32, c=c9)

            def first_kernel_steps(go, sh, lo):
                go(nc.vector.tensor_scalar(sh[:, :], cell_i[:, :], 4, None, ALU.arith_shift_right))
                go(nc.vector.tensor_copy(koff[:, :], sh[:, :]))
                go(nc.vector.tensor_scalar(koff[:, :], koff[:, :], float(KS), None, ALU.mult))
                go(nc.vector.tensor_scalar(sh[:, :], cell_i[:, :], 2, 3, ALU.arith_shift_right, ALU.bitwise_and))
                go(nc.vector.tensor_tensor(koff[:, :], koff[:, :], sh[:, :], ALU.add))
                go(nc.vector.tensor_scalar(koff[:, :], koff[:, :], float(KS), None, ALU.mult))
                go(nc.vector.tensor_scalar(lo[:, :], cell_i[:, :], 3, None, ALU.bitwise_and))
                go(nc.vector.tensor_tensor(koff[:, :], koff[:, :], lo[:, :], ALU.add))

            def corner_steps(go, fr, fg, w01, wt):
                go(nc.vector.tensor_copy(fg[:, :, :, 1], fr))
                go(nc.vector.tensor_scalar(fg[:, :, :, 0], fr, -1.0, 1.0, ALU.mult, ALU.add))
                go(nc.vector.tensor_tensor(w01[:, :, :, :], fg[:, :, 0, :, None].to_broadcast([P, TC, 2, 2]),
                                           fg[:, :, 1, None, :].to_broadcast([P, TC, 2, 2]), ALU.mult))
                go(nc.vector.tensor_tensor(wt[:, :, :].rearrange("p t (a b) -> p t a b", b=2),
                                           w01[:, :, :, :].rearrange("p t a b -> p t (a b)")[:, :, :, None].to_broadcast([P, TC, 4, 2]),
                                           fg[:, :, 2, None, :].to_broadcast([P, TC, 4, 2]), ALU.mult))

            c5 = ExitStack()
            with c5:
                w2s = sb("w2s", [H, KK * H], c=c5)
                wt = sb("wt2", [P, TC, 8], c=c5)
                cdst = sb("cdst", [P, TC], i32, c=c5)
                cs = ExitStack()
                with cs:
                    rc = sb("rc", [P, TC, CW], c=cs)
                    fg = sb("fg", [P, TC, 3, 2], c=cs)
                    w01 = sb("w01", [P, TC, 2, 2], c=cs)
                    sh = sb("shG", [P, TC], i32, c=cs)
                    lo = sb("loG", [P, TC], i32, c=cs)
                    ld = sem("ldG", cs)
                    ch = sem("chG", cs)
                    block = cs.enter_context(nc.Block())

                    @block.sync
                    def _(sp):
                        sp.dma_start(rc[:, :, :].rearrange("p t w -> p (t w)"),
                                     rec_c.rearrange("(p t) w -> p (t w)", p=P)).then_inc(ld, 16)
                        sp.dma_start(w2s[:, :].rearrange("i (k o) -> i k o", o=H), s2w.rearrange("k i o -> i k o")).then_inc(ld, 16)
                        sp.wait_ge(ld, 32)

                    @block.vector
                    def _(v):
                        go = Chain(v, ch)
                        first_kernel_steps(go, sh, lo)
                        go(nc.vector.tensor_scalar(dst_i[:, :], rs[:, :, 1], 0.0, None, ALU.max))
                        go(nc.vector.tensor_copy(posc_i[:, :], rs[:, :, 5]))
                        v.wait_ge(ld, 32)
                        go(nc.vector.tensor_copy(cdst[:, :], rc[:, :, 0]))
                        corner_steps(go, rc[:, :, 1:4], fg, w01, wt)

                cell_loop("c2", H, H, w2s, koff, wt, cdst, h1_tab, None, msg2)

            def node_copy(tag, acc, o, width):
                cs = ExitStack()
                with cs:
                    cpd = sem(tag + "cpd", cs)
                    block = cs.enter_context(nc.Block())

                    @block.vector
                    def _(v):
                        nc.vector.tensor_tensor(o[:, :, :], acc[:, :, :].rearrange("p a b -> p (a b)")[:, 0:NCH * width]
                                                .rearrange("p (c f) -> p c f", f=width),
                                                rdeg_s[:, :, None].to_broadcast([P, NCH, width]), ALU.mult).then_inc(cpd, 1)
                        v.wait_ge(cpd, 1)

            c6 = ExitStack()
            with c6:
                h2 = sb("h2", [P, NCH, H], c=c6)
                cp = ExitStack()
                with cp:
                    acc = pb("acc2", [P, 4, 512], cp)
                    segment_loop("m2", H, posc_i, msg2, acc)
                    node_copy("n2", acc, h2, H)
                cs = ExitStack()
                with cs:
                    low = sb("lowH", [P, NCH, H], c=cs)
                    h2T = sb("h2T", [H, NPAD], c=cs)
                    h3T = sb("h3T", [H, NPAD], c=cs)
                    lowT = sb("lowT", [H, NPAD], c=cs)
                    w3 = sb("w3", [H, H], c=cs)
                    w4 = sb("w4", [H, 3], c=cs)
                    bb = sb("bbH", [P, H], c=cs)
                    bc3 = sb("bc3", [H, 1], c=cs)
                    bb4 = sb("bb4", [P, 3], c=cs)
                    xtn = sb("xtn", [P, NCH, XW], c=cs)
                    trest = sb("trest", [P, NCH, 3], c=cs)
                    pT = pb("pT", [H, 7, 512], cs)
                    p4 = pb("p4", [P, 512], cs)
                    ld = sem("ldH", cs)
                    ch = sem("chH", cs)
                    er = sem("erH", cs)
                    ed = sem("edH", cs)
                    h2d = sem("h2d", cs)
                    ptd = sem("ptd", cs)
                    ptc = sem("ptc", cs)
                    st = sem("stH", cs)
                    xd = sem("xdH", cs)
                    block = cs.enter_context(nc.Block())

                    @block.sync
                    def _(sp):
                        sp.dma_start(w3[:, :], s3w).then_inc(ld, 16)
                        sp.dma_start(w4[:, :], s4w).then_inc(ld, 16)
                        sp.dma_start(bb[:, :], s2b.rearrange("(a n) -> a n", a=1).to_broadcast([P, H])).then_inc(ld, 16)
                        sp.dma_start(bb4[:, :], s4b.rearrange("(a n) -> a n", a=1).to_broadcast([P, 3])).then_inc(ld, 16)
                        sp.dma_start(bc3[:, :], s3b.rearrange("(n a) -> n a", a=1)).then_inc(ld, 16)
                        sp.wait_ge(xd, 1)
                        sp.dma_start(xt_tab.rearrange("(c p) w -> p c w", p=P), xtn[:, :, :]).then_inc(st, 16)
                        sp.wait_ge(st, 16)

                    @block.scalar
                    def _(act):
                        act.wait_ge(er, 1)
                        nc.scalar.activation(low[:, :, :], low[:, :, :], ACT.Exp).then_inc(ed, 1)
                        act.wait_ge(er, 2)
                        nc.scalar.activation(lowT[:, :], lowT[:, :], ACT.Exp).then_inc(ed, 1)

                    @block.tensor
                    def _(pe):
                        pe.wait_ge(h2d, 1)
                        for c in range(NCH):
                            last = nc.tensor.transpose(pT[:, c // 4, (c % 4) * P:(c % 4 + 1) * P], h2[:, c, :], ident[:, :])
                        last.then_inc(ptd, 1)
                        pe.wait_ge(ptc, 1)
                        for s in range(7):
                            w = min(512, NPAD - s * 512)
                            last = nc.tensor.matmul(pT[:, s, 0:w], w3[:, :], h2T[:, s * 512:s * 512 + w], start=True, stop=True)
                        last.then_inc(ptd, 1)
                        pe.wait_ge(ptc, 2)
                        for c in range(NCH):
                            last = nc.tensor.matmul(p4[:, c * 3:c * 3 + 3], h3T[:, c * P:(c + 1) * P], w4[:, :], start=True, stop=True)
                        last.then_inc(ptd, 1)

                    @block.vector
                    def _(v):
                        go = Chain(v, ch)
                        go(nc.vector.memset(xtn[:, :, :], 0.0))
                        v.wait_ge(ld, 80)
                        go(nc.vector.tensor_tensor(h2[:, :, :], h2[:, :, :], bb[:, None, :].to_broadcast([P, NCH, H]), ALU.add))
                        elu_steps(v, go, h2[:, :, :], low[:, :, :], er, ed, 1)
                        nc.vector.memset(low[0:1, 0, 0:1], 0.0).then_inc(h2d, 1)
                        flat = pT[:, :, :].rearrange("p a b -> p (a b)")[:, 0:NPAD]
                        v.wait_ge(ptd, 1)
                        nc.vector.tensor_copy(h2T[:, :], flat).then_inc(ptc, 1)
                        v.wait_ge(ptd, 2)
                        go(nc.vector.tensor_scalar(h3T[:, :], flat, bc3[:, :], None, ALU.add))
                        elu_steps(v, go, h3T[:, :], lowT[:, :], er, ed, 2)
                        nc.vector.memset(lowT[0:1, 0:1], 0.0).then_inc(ptc, 1)
                        v.wait_ge(ptd, 3)
                        tt = xtn[:, :, F:F + 3]
                        go(nc.vector.tensor_tensor(tt, p4[:, 0:3 * NCH].rearrange("p (c f) -> p c f", f=3),
                                                   bb4[:, None, :].to_broadcast([P, NCH, 3]), ALU.add))
                        split3(go, tt, [tn3[:, :, 3 * k:3 * k + 3] for k in range(3)], trest[:, :, :])
                        nc.vector.tensor_copy(xtn[:, :, 0:F], x1[:, :, :]).then_inc(xd, 1)

            cs = ExitStack()
            with cs:
                oh = sb("ohT", [P, 2, HALF, P], bf16, c=cs)
                ot = sb("otT", [P, 2, HALF, P], bf16, c=cs)
                tp = pb("tpT", [P, 2, HALF, P], cs, bf16)
                gp = pb("gpT", [P, 2, 512], cs)
                made = sem("madeT", cs)
                trd = sem("trdT", cs)
                tev = sem("tevT", cs)
                gd = sem("gdT", cs)
                ge = sem("geT", cs)
                block = cs.enter_context(nc.Block())

                @block.scalar
                def _(act):
                    with act.Fori(0, TS // RING) as i:
                        for h in range(2):
                            act.wait_ge(trd, i * 2 + h + 1)
                            act.wait_ge(gd, i * 2)
                            nc.scalar.copy(ot[:, h, :, :], tp[:, h, :, :]).then_inc(tev, 1)

                @block.tensor
                def _(pe):
                    t3 = tn3[:, :, :].rearrange("p c f -> p (c f)")
                    with pe.Fori(0, TS // RING) as i:
                        for h in range(2):
                            pe.wait_ge(made, i * 2 + h + 1)
                            pe.wait_ge(tev, i * 2)
                            for k in range(HALF):
                                last = nc.tensor.transpose(tp[:, h, k, :], oh[:, h, k, :], identb[:, :])
                            last.then_inc(trd, 1)
                            ids = load_ids(pe, chunk_i, i, h)
                            pe.wait_ge(tev, i * 2 + h + 1)
                            pe.wait_ge(ge, i * 2)
                            for k in range(HALF):
                                last = nc.tensor.matmul(gp[:, h, k * 9:k * 9 + 9], ot[:, h, k, :], t3[:, bass.ds(ids[k] * 9, 9)],
                                                        start=True, stop=True)
                            last.then_inc(gd, 1)

                @block.vector
                def _(v):
                    with v.Fori(0, TS // RING) as i:
                        for h in range(2):
                            v.wait_ge(trd, i * 2)
                            onehots(oh[:, h, :, :], h, i).then_inc(made, 1)
                            v.wait_ge(gd, i * 2 + h + 1)
                            nc.vector.reduce_sum(tsrc[:, bass.ds(i * RING + h * HALF, HALF), :],
                                                 gp[:, h, 0:9 * HALF].rearrange("p (k a d) -> p k d a", a=3, d=3), axis=AX).then_inc(ge, 1)

        c7 = ExitStack()
        with c7:
            koff = sb("koff3", [P, TC], i32, c=c7)
            dst_i = sb("dst_i3", [P, TS], i32, c=c7)
            row_d = sb("row_d", [P, TS], i32, c=c7)
            c8 = ExitStack()
            with c8:
                xd = sb("xdst", [P, TS, XW], c=c8)
                key_d = sb("key_d", [P, TS], c=c8)
                cs = ExitStack()
                with cs:
                    g = sb("gX", [P, RING, XW], c=cs)
                    ix = sb("ixX", [P, RING], i32, c=cs)
                    got = [sem(f"gotX{h}", cs) for h in range(2)]
                    held = sem("heldX", cs)
                    staged = sem("stagedX", cs)
                    cpy = sem("cpyX", cs)
                    ini = sem("iniX", cs)
                    block = cs.enter_context(nc.Block())
                    per = 16 * HALF

                    @block.scalar
                    def _(act):
                        act.wait_ge(ini, 1)
                        with act.Fori(0, TS // RING) as i:
                            for h in range(2):
                                act.wait_ge(got[h], i * per)
                                nc.scalar.copy(ix[:, h * HALF:h * HALF + HALF], dst_i[:, bass.ds(i * RING + h * HALF, HALF)]).then_inc(staged, 1)

                    @block.gpsimd
                    def _(pool):
                        with pool.Fori(0, TS // RING) as i:
                            for h in range(2):
                                pool.wait_ge(staged, i * 2 + h + 1)
                                pool.wait_ge(cpy, i * 2)
                                hold(held, i * 2 + h)
                                for k in range(h * HALF, h * HALF + HALF):
                                    nc.gpsimd.indirect_dma_start(
                                        out=g[:, k, :], out_offset=None, in_=xt_tab,
                                        in_offset=bass.IndirectOffsetOnAxis(ap=ix[:, k:k + 1], axis=0),
                                        bounds_check=NPAD - 1, oob_is_err=False).then_inc(got[h], 16)

                    @block.vector
                    def _(v):
                        nc.vector.tensor_scalar(dst_i[:, :], rs[:, :, 1], 0.0, None, ALU.max).then_inc(ini, 1)
                        with v.Fori(0, TS // RING) as i:
                            for h in range(2):
                                v.wait_ge(got[h], (i + 1) * per)
                                nc.vector.tensor_copy(xd[:, bass.ds(i * RING + h * HALF, HALF), :], g[:, h * HALF:h * HALF + HALF, :]).then_inc(cpy, 1)

                cs = ExitStack()
                with cs:
                    np_ = sb("np_", [P, TS, 3], c=cs)
                    fl = sb("fl3", [P, TS, 3], c=cs)
                    tt = sb("tt3", [P, TS, 3], c=cs)
                    ch = sem("chP", cs)
                    block = cs.enter_context(nc.Block())

                    @block.vector
                    def _(v):
                        go = Chain(v, ch)
                        p = np_[:, :, :]
                        go(nc.vector.tensor_tensor(p, rs[:, :, 2:5], xd[:, :, F:F + 3], ALU.add))
                        go(nc.vector.tensor_tensor(p, p, tsrc[:, :, :], ALU.subtract))
                        go(nc.vector.tensor_scalar(p, p, 0.0, 1.0, ALU.max, ALU.min))
                        go(nc.vector.tensor_scalar(p, p, float(KS - 1), None, ALU.mult))
                        cell_steps(go, p, fl[:, :, :], tt[:, :, :], key_d[:, :])
                        go(nc.vector.tensor_copy(xd[:, :, F:F + 3], fl[:, :, :]))
                        go(nc.vector.tensor_scalar(tt[:, :, 0], rs[:, :, 0], 0.0, 1000.0, ALU.is_lt, ALU.mult))
                        go(nc.vector.tensor_tensor(key_d[:, :], key_d[:, :], tt[:, :, 0], ALU.add))

                c2 = ExitStack()
                with c2:
                    sort_block("sd", key_d[:, :], TS, CELLS, TC, row_d[:, :], cell_i, c2)
                scatter_block("xd", [(xd, row_d, rec_d, P * TC)], TS)

            c5 = ExitStack()
            with c5:
                cws = sb("cws", [F, KK * F], c=c5)
                wt = sb("wt3", [P, TC, 8], c=c5)
                cs = ExitStack()
                with cs:
                    fr = sb("fr3", [P, TC, 3], c=cs)
                    fg = sb("fg3", [P, TC, 3, 2], c=cs)
                    w01 = sb("w013", [P, TC, 2, 2], c=cs)
                    sh = sb("shI", [P, TC], i32, c=cs)
                    lo = sb("loI", [P, TC], i32, c=cs)
                    ld = sem("ldI", cs)
                    ch = sem("chI", cs)
                    block = cs.enter_context(nc.Block())

                    @block.sync
                    def _(sp):
                        sp.dma_start(fr[:, :, :], rec_d.rearrange("(p t) w -> p t w", p=P)[:, :, F:F + 3]).then_inc(ld, 16)
                        sp.dma_start(cws[:, :].rearrange("i (k o) -> i k o", o=F), cw.rearrange("k i o -> i k o")).then_inc(ld, 16)
                        sp.wait_ge(ld, 32)

                    @block.vector
                    def _(v):
                        go = Chain(v, ch)
                        first_kernel_steps(go, sh, lo)
                        go(nc.vector.tensor_scalar(row_d[:, :], row_d[:, :], float(P * TC - 1), None, ALU.min))
                        v.wait_ge(ld, 32)
                        corner_steps(go, fr[:, :, :], fg, w01, wt)

                cell_loop("c3", F, F, cws, koff, wt, None, None, rec_d, msg3)

            cs = ExitStack()
            with cs:
                y = sb("yJ", [P, NCH, F], c=cs)
                o = sb("oJ", [P, NCH, F], c=cs)
                cp = ExitStack()
                with cp:
                    acc = pb("acc3", [P, 2, 512], cp)
                    segment_loop("m3", F, row_d, msg3, acc)
                    node_copy("n3", acc, y, F)
                mean = sb("meanJ", [P, NCH], c=cs)
                sq = sb("sqJ", [P, NCH, F], c=cs)
                bb = sb("bbJ", [P, F], c=cs)
                ld = sem("ldJ", cs)
                ch = sem("chJ", cs)
                rr = sem("rrJ", cs)
                rt = sem("rtJ", cs)
                done = sem("doneJ", cs)
                st = sem("stJ", cs)
                block = cs.enter_context(nc.Block())

                @block.sync
                def _(sp):
                    sp.dma_start(bb[:, :], cb.rearrange("(a n) -> a n", a=1).to_broadcast([P, F])).then_inc(ld, 16)
                    sp.wait_ge(done, 1)
                    sp.dma_start(out[0:(NCH - 1) * P, :].rearrange("(c p) f -> p c f", p=P), o[:, 0:NCH - 1, :]).then_inc(st, 16)
                    sp.dma_start(out[(NCH - 1) * P:N, :], o[0:NREM, NCH - 1, :]).then_inc(st, 16)
                    sp.wait_ge(st, 32)

                @block.scalar
                def _(act):
                    act.wait_ge(rr, 1)
                    nc.scalar.activation(mean[:, :], mean[:, :], ACT.Sqrt).then_inc(rt, 1)

                @block.vector
                def _(v):
                    go = Chain(v, ch)
                    v.wait_ge(ld, 16)
                    go(nc.vector.tensor_tensor(y[:, :, :], y[:, :, :], bb[:, None, :].to_broadcast([P, NCH, F]), ALU.add))
                    go(nc.vector.tensor_tensor(y[:, :, :], y[:, :, :], x1[:, :, :], ALU.add))
                    norm_steps(v, go, y[:, :, :], o[:, :, :], mean, sq, rt, rr, 1)
                    nc.vector.memset(mean[0:1, 0:1], 0.0).then_inc(done, 1)


def kernel(**inputs):
    import numpy as np
    import concourse.bacc as bacc
    from concourse.bass_utils import run_bass_kernel_spmd

    g = {k: np.asarray(v) for k, v in inputs.items()}
    lay = {
        "x": g["x"], "xT": g["x"].T, "src": g["src"], "dst": g["dst"], "ps": g["edge_attr_3"],
        "w1l": g["L0_gnn_W1_l"].T, "w1r": g["L0_gnn_W1_r"].T, "b1": g["L0_gnn_b1"],
        "w2l": g["L0_gnn_W2_l"].T, "w2r": g["L0_gnn_W2_r"].T, "b2": g["L0_gnn_b2"],
        "s1w": g["L1_gnn_stn1_w"], "s1b": g["L1_gnn_stn1_b"], "s2w": g["L1_gnn_stn2_w"], "s2b": g["L1_gnn_stn2_b"],
        "s3w": g["L1_gnn_stn3_w"], "s3b": g["L1_gnn_stn3_b"], "s4w": g["L1_gnn_stn4_w"], "s4b": g["L1_gnn_stn4_b"],
        "cw": g["L1_gnn_conv_w"], "cb": g["L1_gnn_conv_b"],
    }
    nc = bacc.Bacc("TRN2", target_bir_lowering=False, num_devices=1)
    arrays, args = {}, []
    for name, a in lay.items():
        a = np.ascontiguousarray(a)
        arrays["in_" + name] = a
        args.append(nc.dram_tensor("in_" + name, a.shape, mybir.dt.from_np(a.dtype), kind="ExternalInput").ap())
    args.append(nc.dram_tensor("out_0", (N, F), fp32, kind="ExternalOutput").ap())
    gnn_kernel(nc, *args)
    r = run_bass_kernel_spmd(nc, [arrays], core_ids=[0])
    return r.results[0]["out_0"]
```

```python
import concourse.bass as bass
from concourse import mybir
from contextlib import ExitStack

fp32 = mybir.dt.float32
bf16 = mybir.dt.bfloat16
fp16 = mybir.dt.float16
i32 = mybir.dt.int32
i16 = mybir.dt.int16
ALU = mybir.AluOpType
ACT = mybir.ActivationFunctionType
AX = mybir.AxisListType.X

P = 128
N = 3125
E = 53125
F = 32
H = 64
KS = 5
KK = KS ** 3
NCH = -(-N // P)
NPAD = NCH * P
NREM = N - (NCH - 1) * P
CELLS = (KS - 1) ** 3
HALF = 8
RING = 2 * HALF
EC = -(-(-(-E // P)) // RING) * RING
EFULL = E // EC
EREM = E - EFULL * EC
NBK = 2 * NCH
TS = -(-((E + NBK * (P - 1)) // P) // RING) * RING
TC = -(-((E + CELLS * (P - 1)) // P) // RING) * RING
FAR = P * 8192 + P - 1
DSEG = -(-N // 7)
DHALF = 4 * DSEG
RW = 6
CW = 4
TW = 4
XT = 3 * F + 9
assert EFULL == P - 1 and EREM > 0 and NPAD <= 7 * 512


QUAD = 4
LOOK = 4
SORT_TURNS = 8
MID_TURNS = 5


def free(step):
    return step + 1


def done(step):
    return step + 3


class Chain:

    def __init__(self, eng, sem, base=0):
        self.eng, self.sem, self.base, self.n = eng, sem, base, 0

    def on(self, eng):
        self.eng = eng
        return self

    def __call__(self, ins):
        self.n += 1
        ins.then_inc(self.sem, 1)
        self.eng.wait_ge(self.sem, self.base + self.n)


def gnn_kernel(nc, x, xT, src, dst, ps, w1l, w1r, b1, w2l, w2r, b2,
               s1w, s1b, s2w, s2b, s3w, s3b, s4w, s4b, cw, cb, out):
    ctx = ExitStack()

    def dram(name, shape, dt=fp32):
        return nc.dram_tensor(name, shape, dt, kind="Internal").ap()

    rec_s = dram("rec_s", (P * TS, RW))
    rec_c = dram("rec_c", (P * TC, CW))
    h1_tab = dram("h1_tab", (NPAD, H))
    msg2 = dram("msg2", (P * TC, H))
    oht_d = dram("oht_d", (P, TS * P), bf16)
    t_tab = dram("t_tab", (NPAD, TW))
    x1_tab = dram("x1_tab", (NPAD, F))
    rec_d = dram("rec_d", (P * TC, CW))
    msg3 = dram("msg3", (P * TC, F))

    def sb(name, shape, dt=fp32, c=ctx):
        return c.enter_context(nc.sbuf_tensor(name, shape, dt))

    def sem(name, c=ctx):
        return c.enter_context(nc.semaphore(name))

    def pb(name, shape, c, dt=fp32):
        return c.enter_context(nc.psum_tensor(name, shape, dt))

    with ctx:
        iota16 = sb("iota16", [P, DHALF], fp16)
        iota_f = sb("iota_f", [P, 512])
        iota_p = sb("iota_p", [P, 1])
        line = Chain(None, sem("dve_line"))
        consts = sem("consts_made")
        ident = sb("ident", [P, P])
        identb = sb("identb", [P, P], bf16)
        tri = sb("tri", [P, P])
        ones = sb("ones", [P, P])
        zeros = sb("zeros", [P, 512])
        tick = sb("tick", [P, 4])

        def hold(held, n):
            nc.gpsimd.wait_ge(held, n)
            nc.gpsimd.tensor_tensor(tick[:, 2:3], zeros[:, 0:1], zeros[:, 0:1], op=ALU.add).then_inc(held, 1)

        x1 = sb("x1", [P, NCH, F])
        rdeg_s = sb("rdeg_s", [P, NCH])
        xt3 = sb("xt3", [P, NCH, XT], bf16)
        rs = sb("rs", [P, TS, RW])
        chunk_i = sb("chunk_i", [P, TS], i32)
        half_i = sb("half_i", [P, TS], i32)
        cell_i = sb("cell_i", [P, TC], i32)

        def sort_block(tag, key, C, K, T, row, tile_i, c, beside=None, turns=0):
            KP = -(-K // LOOK) * LOOK
            cnt = sb(tag + "cnt", [P, KP], c=c)
            base = sb(tag + "base", [P, KP], c=c)
            tiles = sb(tag + "tiles", [P, KP], c=c)
            endt = sb(tag + "endt", [P, KP], c=c)
            ti = sb(tag + "ti", [P, KP], i32, c=c)
            ecol = sb(tag + "ecol", [P, 1], c=c)
            key16 = sb(tag + "key16", [P, C], fp16, c=c)
            mask = sb(tag + "mask", [P, LOOK, C], i16, c=c)
            run = sb(tag + "run", [P, LOOK, C], c=c)
            pos = sb(tag + "pos", [P, C], c=c)
            rowlo = sb(tag + "rowlo", [P, C], i32, c=c)
            cmp = sb(tag + "cmp", [P, T], c=c)
            cs = ExitStack()
            with cs:
                pp = pb(tag + "pp", [P, 512], cs)
                pt = pb(tag + "pt", [P, 512], cs)
                v_cnt = sem(tag + "v_cnt", cs)
                pe_px = sem(tag + "pe_px", cs)
                v_cmp = sem(tag + "v_cmp", cs)
                pe_tb = sem(tag + "pe_tb", cs)
                ch2 = sem(tag + "ch2", cs)
                block = cs.enter_context(nc.Block())

                if beside:
                    @block.sync
                    def _(sp):
                        beside.on_sync(sp, 0, turns)

                    @block.gpsimd
                    def _(pool):
                        beside.on_pool(pool, 0, turns)

                @block.tensor
                def _(pe):
                    pe.wait_ge(v_cnt, LOOK + KP)
                    nc.tensor.matmul(pp[:, 0:KP], tri[:, :], cnt[:, :], start=True, stop=True).then_inc(pe_px, 1)
                    nc.tensor.matmul(pt[:, 0:KP], ones[:, :], cnt[:, :], start=True, stop=True).then_inc(pe_px, 1)
                    pe.wait_ge(v_cmp, 1)
                    nc.tensor.matmul(pp[:, 0:T], ones[0:KP, :], cmp[0:KP, :], start=True, stop=True).then_inc(pe_tb, 1)

                @block.vector
                def _(v):
                    go = line.on(v)
                    go(nc.vector.tensor_copy(key16[:, :], key))
                    v.sem_inc(v_cnt, LOOK)
                    with v.Fori(0, KP // LOOK) as b:
                        for k in range(LOOK):
                            v.wait_ge(v_cnt, b * LOOK + (k + 1))
                            nc.vector.tensor_scalar(mask[:, k, :], key16[:, :], iota_f[:, bass.ds(b * LOOK + k, 1)], 0.0,
                                                    ALU.is_equal, ALU.add,
                                                    accum_out=cnt[:, bass.ds(b * LOOK + k, 1)]).then_inc(v_cnt, 1)
                    v.wait_ge(pe_px, 2)
                    go(nc.vector.tensor_scalar(ti[:, :], pt[:, 0:KP], float(P - 1), None, ALU.add))
                    go(nc.vector.tensor_scalar(ti[:, :], ti[:, :], 7, None, ALU.arith_shift_right))
                    go(nc.vector.tensor_copy(tiles[:, :], ti[:, :]))
                    go(nc.vector.tensor_tensor_scan(endt[:, :], tiles[:, :], zeros[:, 0:KP], 0.0, ALU.add, ALU.add))
                    go(nc.vector.tensor_tensor(tiles[:, :], endt[:, :], tiles[:, :], ALU.subtract))
                    go(nc.vector.tensor_scalar(tiles[:, :], tiles[:, :], float(P), -1.0, ALU.mult, ALU.add))
                    go(nc.vector.tensor_tensor(base[:, :], pp[:, 0:KP], tiles[:, :], ALU.add))
                    go(nc.vector.tensor_tensor(endt[:, :], endt[:, :], ident[:, 0:KP], ALU.mult))
                    go(nc.vector.reduce_sum(ecol[:, :], endt[:, :], axis=AX))
                    nc.vector.tensor_scalar(cmp[:, :], iota_f[:, 0:T], ecol[:, :], None, ALU.is_ge).then_inc(v_cmp, 1)
                    v.wait_ge(pe_tb, 1)
                    go(nc.vector.tensor_scalar(cmp[:, :], pp[:, 0:T], float(K - 1), None, ALU.min))
                    go(nc.vector.tensor_copy(tile_i[:, :], cmp[:, :]))
                    go(nc.vector.memset(pos[:, :], float(FAR)))
                    v.sem_inc(ch2, 1)
                    with v.Fori(0, KP // LOOK) as b:
                        at = b * (3 * LOOK) + 1
                        for k in range(LOOK):
                            v.wait_ge(ch2, at)
                            nc.vector.tensor_scalar(mask[:, k, :], key16[:, :], iota_f[:, bass.ds(b * LOOK + k, 1)], None,
                                                    ALU.is_equal).then_inc(ch2, 1)
                        for k in range(LOOK):
                            v.wait_ge(ch2, at + (k + 1))
                            nc.vector.tensor_tensor_scan(run[:, k, :], mask[:, k, :], zeros[:, 0:C],
                                                         base[:, bass.ds(b * LOOK + k, 1)], ALU.add, ALU.add).then_inc(ch2, 1)
                        for k in range(LOOK):
                            v.wait_ge(ch2, at + (2 * LOOK if k else LOOK + 1) + k)
                            nc.vector.memset(tick[:, 1:2], 0.0)
                            nc.vector.copy_predicated(pos[:, :], mask[:, k, :], run[:, k, :]).then_inc(ch2, 1)
                    g3 = line.on(v)
                    v.wait_ge(ch2, 3 * KP + 1)
                    g3(nc.vector.tensor_copy(row, pos[:, :]))
                    g3(nc.vector.tensor_scalar(rowlo[:, :], row, P - 1, None, ALU.bitwise_and))
                    g3(nc.vector.tensor_scalar(row, row, 7, None, ALU.arith_shift_right))
                    g3(nc.vector.tensor_copy(pos[:, :], row))
                    g3(nc.vector.scalar_tensor_tensor(pos[:, :], rowlo[:, :], float(T), pos[:, :], ALU.mult, ALU.add))
                    g3(nc.vector.tensor_copy(row, pos[:, :]))

        def cell_steps(go, p, flo, t, key):
            go(nc.vector.tensor_scalar(flo, p, 1.0, None, ALU.is_ge))
            go(nc.vector.tensor_scalar(t, p, 2.0, None, ALU.is_ge))
            go(nc.vector.tensor_tensor(flo, flo, t, ALU.add))
            go(nc.vector.tensor_scalar(t, p, 3.0, None, ALU.is_ge))
            go(nc.vector.tensor_tensor(flo, flo, t, ALU.add))
            go(nc.vector.tensor_scalar(key, flo[:, :, 0], 16.0, None, ALU.mult))
            go(nc.vector.scalar_tensor_tensor(key, flo[:, :, 1], 4.0, key, ALU.mult, ALU.add))
            go(nc.vector.tensor_tensor(key, key, flo[:, :, 2], ALU.add))
            go(nc.vector.tensor_tensor(flo, p, flo, ALU.subtract))

        class Scatter:

            def __init__(self, tag, a, r, table, rows, c):
                self.a, self.r, self.table, self.rows = a, r, table, rows
                self.d = sb(tag + "d", [P, RING, a.shape[2]], c=c)
                self.ix = sb(tag + "ix", [P, RING], i32, c=c)
                self.held = sem(tag + "held", c)
                self.staged = [sem(f"{tag}staged{h}", c) for h in range(2)]
                self.sent = [sem(f"{tag}sent{h}", c) for h in range(2)]

            def stage(self, sp, i, h):
                s = slice(h * HALF, h * HALF + HALF)
                sp.wait_ge(self.sent[h], i * (16 * HALF))
                sp.dma_start(self.d[:, s, :], self.a[:, bass.ds(i * RING + h * HALF, HALF), :]).then_inc(self.staged[h], 16)
                sp.dma_start(self.ix[:, s], self.r[:, bass.ds(i * RING + h * HALF, HALF)]).then_inc(self.staged[h], 16)

            def send(self, pool, i, h):
                pool.wait_ge(self.staged[h], (i + 1) * 32)
                hold(self.held, i * 2 + h)
                for k in range(h * HALF, h * HALF + HALF):
                    nc.gpsimd.indirect_dma_start(
                        out=self.table, out_offset=bass.IndirectOffsetOnAxis(ap=self.ix[:, k:k + 1], axis=0),
                        in_=self.d[:, k, :], in_offset=None, bounds_check=self.rows - 1,
                        oob_is_err=False).then_inc(self.sent[h], 16)

            def on_sync(self, sp, first, end):
                with sp.Fori(first, end) as i:
                    for h in range(2):
                        self.stage(sp, i, h)
                for h in range(2):
                    sp.wait_ge(self.sent[h], end * (16 * HALF))

            def on_pool(self, pool, first, end):
                with pool.Fori(first, end) as i:
                    for h in range(2):
                        self.send(pool, i, h)

            def first(self, act):
                pass

            def after(self, act, i, h, last_turn):
                pass

        class Gather:

            def __init__(self, tag, table, rows, r, o, c):
                self.table, self.rows, self.r, self.o = table, rows, r, o
                self.g = sb(tag + "g", [P, RING, o.shape[2]], c=c)
                self.ix = sb(tag + "ix", [P, RING], i32, c=c)
                self.staged = sem(tag + "staged", c)
                self.kept = sem(tag + "kept", c)
                self.held = sem(tag + "held", c)
                self.got = [sem(f"{tag}got{h}", c) for h in range(2)]

            def stage(self, act, i, h):
                nc.scalar.copy(self.ix[:, h * HALF:h * HALF + HALF],
                               self.r[:, bass.ds(i * RING + h * HALF, HALF)]).then_inc(self.staged, 1)

            def first(self, act):
                act.sem_inc(self.kept, 2)
                for h in range(2):
                    self.stage(act, 0, h)

            def keep(self, act, i, h):
                act.wait_ge(self.got[h], (i + 1) * (16 * HALF))
                nc.scalar.copy(self.o[:, bass.ds(i * RING + h * HALF, HALF), :],
                               self.g[:, h * HALF:h * HALF + HALF, :]).then_inc(self.kept, 1)

            def on_sync(self, sp, first, end):
                pass

            def on_pool(self, pool, first, end):
                with pool.Fori(first, end) as i:
                    for h in range(2):
                        self.send(pool, i, h)

            def after(self, act, i, h, last_turn):
                self.keep(act, i, h)
                if not last_turn:
                    self.stage(act, i + 1, h)

            def send(self, pool, i, h):
                pool.wait_ge(self.staged, i * 2 + h + 1)
                pool.wait_ge(self.kept, free(i * 2 + h))
                hold(self.held, i * 2 + h)
                for k in range(h * HALF, h * HALF + HALF):
                    nc.gpsimd.indirect_dma_start(
                        out=self.g[:, k, :], out_offset=None, in_=self.table,
                        in_offset=bass.IndirectOffsetOnAxis(ap=self.ix[:, k:k + 1], axis=0),
                        bounds_check=self.rows - 1, oob_is_err=False).then_inc(self.got[h], 16)

        def scatter_block(tag, a, r, table, rows, C):
            cs = ExitStack()
            with cs:
                sc = Scatter(tag, a, r, table, rows, cs)
                block = cs.enter_context(nc.Block())

                @block.sync
                def _(sp):
                    sc.on_sync(sp, 0, C // RING)

                @block.gpsimd
                def _(pool):
                    sc.on_pool(pool, 0, C // RING)

        c0 = ExitStack()
        recC = sb("recC", [P, EC, CW], c=c0)
        row_c = sb("row_c", [P, EC], i32, c=c0)
        by_cell = Scatter("xc", recC, row_c, rec_c, P * TC, c0)
        c1 = ExitStack()
        with c1:
            ei = sb("ei", [P, 2, EC], i32, c=c1)
            ri = sb("ri", [P, EC], i32, c=c1)
            recS = sb("recS", [P, EC, RW], c=c1)
            key_s = sb("key_s", [P, EC], c=c1)
            key_c = sb("key_c", [P, EC], c=c1)
            pos4 = sb("pos4", [P, EC, 3], c=c1)
            flo = sb("flo", [P, EC, 3], c=c1)
            tmp3 = sb("tmp3", [P, EC, 3], c=c1)
            row_s = sb("row_s", [P, EC], i32, c=c1)
            iota_i = sb("iota_i", [P, 512], i32, c=c1)
            iop_i = sb("iop_i", [P, 1], i32, c=c1)
            pse = sb("pse", [P, EC, 3], c=c1)
            cs = ExitStack()
            with cs:
                fz = sb("fz", [P, TC * CW], c=cs)
                fillS = sb("fillS", [P, TS, RW], c=cs)
                ld = sem("ld", cs)
                fill = sem("fill", cs)
                pre = sem("pre", cs)
                block = cs.enter_context(nc.Block())

                @block.sync
                def _(sp):
                    sp.wait_ge(pre, 1)
                    for n, a in enumerate((src, dst)):
                        sp.dma_start(ei[0:EFULL, n, :], a[0:EFULL * EC].rearrange("(p c) -> p c", c=EC)).then_inc(ld, 16)
                        sp.dma_start(ei[EFULL:P, n, 0:EREM], a[EFULL * EC:E].rearrange("(p c) -> p c", p=1)).then_inc(ld, 16)
                    sp.dma_start(pse[0:EFULL, :, :], ps[0:EFULL * EC, :].rearrange("(p c) d -> p c d", c=EC)).then_inc(ld, 16)
                    sp.dma_start(pse[EFULL:P, 0:EREM, :], ps[EFULL * EC:E, :].rearrange("(p c) d -> p c d", p=1)).then_inc(ld, 16)
                    sp.wait_ge(ld, 96)
                    sp.dma_start(rec_s.rearrange("(p t) w -> p (t w)", p=P), fillS[:, :, :].rearrange("p t w -> p (t w)")).then_inc(fill, 16)
                    sp.dma_start(rec_c.rearrange("(p a) w -> p (a w)", p=P), fz[:, :]).then_inc(fill, 16)
                    sp.dma_start(rec_d.rearrange("(p a) w -> p (a w)", p=P), fz[:, :]).then_inc(fill, 16)
                    sp.wait_ge(fill, 48)

                @block.gpsimd
                def _(g):
                    g.iota(iota_i[:, :], pattern=[[1, 512]], base=0, channel_multiplier=0).then_inc(consts, 1)
                    g.iota(iop_i[:, :], pattern=[[1, 1]], base=0, channel_multiplier=1).then_inc(consts, 1)
                    g.iota(iota16[:, :], pattern=[[1, DHALF]], base=0, channel_multiplier=0,
                           allow_small_or_imprecise_dtypes=True).then_inc(consts, 1)
                    g.memset(ones[:, :], 1.0).then_inc(consts, 1)
                    g.memset(zeros[:, :], 0.0).then_inc(consts, 1)
                    g.wait_ge(consts, 5)
                    g.affine_select(out=ident[:, :], in_=ones[:, :], compare_op=ALU.is_equal, fill=0.0,
                                    base=0, pattern=[[-1, P]], channel_multiplier=1).then_inc(consts, 1)
                    g.affine_select(out=tri[:, :], in_=ones[:, :], compare_op=ALU.is_gt, fill=0.0,
                                    base=0, pattern=[[1, P]], channel_multiplier=-1).then_inc(consts, 1)

                @block.vector
                def _(v):
                    go = line.on(v)
                    go(nc.vector.memset(fz[:, :], 0.0))
                    go(nc.vector.memset(fillS[:, :, :], 0.0))
                    go(nc.vector.memset(fillS[:, :, 0:2], -1.0))
                    go(nc.vector.memset(ei[:, :, :], 127 * P))
                    nc.vector.memset(pse[:, :, :], 0.0).then_inc(pre, 1)
                    go(nc.vector.memset(recS[:, :, :], 0.0))
                    v.wait_ge(consts, 7)
                    go(nc.vector.tensor_copy(iota_f[:, :], iota_i[:, :]))
                    go(nc.vector.tensor_copy(iota_p[:, :], iop_i[:, :]))
                    go(nc.vector.tensor_copy(identb[:, :], ident[:, :]))
                    v.wait_ge(ld, 96)
                    go(nc.vector.tensor_scalar(ri[:, :], ei[:, 0, :], 7, None, ALU.arith_shift_right))
                    go(nc.vector.tensor_copy(key_s[:, :], ri[:, :]))
                    go(nc.vector.tensor_scalar(tmp3[:, :, 1], ei[:, 1, :], float(DHALF), None, ALU.is_ge))
                    go(nc.vector.scalar_tensor_tensor(key_s[:, :], key_s[:, :], 2.0, tmp3[:, :, 1], ALU.mult, ALU.add))
                    go(nc.vector.tensor_scalar(ri[:, :], ei[:, 0, :], P - 1, None, ALU.bitwise_and))
                    go(nc.vector.tensor_copy(recS[:, :, 0], ri[:, :]))
                    go(nc.vector.tensor_copy(recS[:, :, 1], ei[:, 1, :]))
                    go(nc.vector.tensor_copy(recC[:, :, 0], ei[:, 1, :]))
                    go(nc.vector.tensor_copy(recS[:, :, 2:5], pse[:, :, :]))
                    go(nc.vector.tensor_scalar(pos4[:, :, :], pse[:, :, :], float(KS - 1), None, ALU.mult))
                    cell_steps(go, pos4[:, :, :], flo[:, :, :], tmp3[:, :, :], key_c[:, :])
                    go(nc.vector.tensor_copy(recC[:, :, 1:4], flo[:, :, :]))
                    go(nc.vector.tensor_scalar(tmp3[:, :, 0], key_s[:, :], 100.0, 1000.0, ALU.is_ge, ALU.mult))
                    go(nc.vector.tensor_tensor(key_c[:, :], key_c[:, :], tmp3[:, :, 0], ALU.add))

            c2 = ExitStack()
            with c2:
                sort_block("sc", key_c[:, :], EC, CELLS, TC, row_c[:, :], cell_i, c2)
            c2 = ExitStack()
            with c2:
                sort_block("ss", key_s[:, :], EC, NBK, TS, row_s[:, :], chunk_i, c2, by_cell, SORT_TURNS)
            cs = ExitStack()
            with cs:
                block = cs.enter_context(nc.Block())

                @block.vector
                def _(v):
                    go = line.on(v)
                    go(nc.vector.tensor_copy(recS[:, :, 5], row_c[:, :]))
                    go(nc.vector.tensor_scalar(half_i[:, :], chunk_i[:, :], 1, None, ALU.bitwise_and))
                    go(nc.vector.tensor_scalar(chunk_i[:, :], chunk_i[:, :], 1, None, ALU.arith_shift_right))

            scatter_block("xs", recS, row_s, rec_s, P * TS, EC)

        def id_registers(pe, tag, n=HALF):
            return [pe.alloc_register(f"{tag}_tile{k}") for k in range(n)]

        def load_ids(pe, regs, table, at, most):
            pe.load(regs, table[0:1, bass.ds(at, len(regs))])
            return [pe.snap(r, min_val=0, max_val=most) for r in regs]

        def onehots(out_, h, i):
            return nc.vector.tensor_tensor(
                out_, iota_f[:, None, 0:P].to_broadcast([P, HALF, P]),
                rs[:, bass.ds(i * RING + h * HALF, HALF), 0:1].to_broadcast([P, HALF, P]), ALU.is_equal)


        def split3(go, a, parts, rest):
            go(nc.vector.tensor_copy(parts[0], a))
            go(nc.vector.tensor_tensor(rest, a, parts[0], ALU.subtract))
            go(nc.vector.tensor_copy(parts[1], rest))
            go(nc.vector.tensor_tensor(rest, rest, parts[1], ALU.subtract))
            go(nc.vector.tensor_copy(parts[2], rest))

        def elu_steps(v, go, h, low, exp_ready, exp_done, n):
            nc.vector.tensor_scalar(low, h, 0.0, None, ALU.min).then_inc(exp_ready, 1)
            go(nc.vector.tensor_scalar(h, h, 0.0, None, ALU.max))
            v.wait_ge(exp_done, n)
            go(nc.vector.scalar_tensor_tensor(h, low, 1.0, h, ALU.subtract, ALU.add))

        def cell_loop(tag, win, wout, w, koff, wa, wb, rows, table, msg):
            na = P // win
            nb = 8 // na
            steps = {2: [(KS * KS * wout, 2), (KS * wout, 2), (1, wout)], 4: [(KS * KS * wout, 2), (1, wout)]}[na]
            n_it = TC // RING
            per = 16 * HALF
            cs = ExitStack()
            with cs:
                u = sb(tag + "u", [P, RING, win], c=cs)
                ix = sb(tag + "ix", [P, RING], i32, c=cs)
                us = sb(tag + "us", [P, 2, QUAD, na, win], c=cs)
                ut = sb(tag + "ut", [P, 2, QUAD, P], c=cs)
                pr = sb(tag + "pr", [P, 2, QUAD, nb, wout], c=cs)
                m = sb(tag + "m", [P, RING, wout], c=cs)
                tp = pb(tag + "tp", [P, 2, QUAD, P], cs)
                z = pb(tag + "z", [P, 2, 1024], cs)
                got = [sem(f"{tag}got{h}", cs) for h in range(2)]
                put = [sem(f"{tag}put{h}", cs) for h in range(2)]
                held = sem(tag + "held", cs)
                staged = sem(tag + "staged", cs)
                uf = sem(tag + "uf", cs)
                sd = sem(tag + "sd", cs)
                trd = sem(tag + "trd", cs)
                tev = sem(tag + "tev", cs)
                zd = sem(tag + "zd", cs)
                zu = sem(tag + "zu", cs)
                red = sem(tag + "red", cs)
                mf = sem(tag + "mf", cs)
                block = cs.enter_context(nc.Block())
                msg_v = msg.rearrange("(p t) f -> p t f", p=P)
                cols = nb * wout

                def zq(b):
                    return z[:, b, 0:QUAD * cols]

                @block.scalar
                def _(act):
                    act.sem_inc(tev, 2)

                    def stage(i, h):
                        act.wait_ge(uf, free(i * 2 + h))
                        nc.scalar.copy(ix[:, h * HALF:h * HALF + HALF],
                                       rows[:, bass.ds(i * RING + h * HALF, HALF)]).then_inc(staged, 1)

                    def turn(i, last_turn):
                        for q in range(4):
                            act.wait_ge(trd, done(i * 4 + q))
                            act.wait_ge(zd, free(i * 4 + q))
                            nc.scalar.copy(ut[:, q % 2, :, :], tp[:, q % 2, :, :]).then_inc(tev, 1)
                            if q % 2 == 0 and not last_turn:
                                stage(i + 1, q // 2)

                    for h in range(2):
                        stage(0, h)
                    with act.Fori(0, n_it - 1) as i:
                        turn(i, False)
                    turn(n_it - 1, True)

                @block.gpsimd
                def _(pool):
                    with pool.Fori(0, n_it) as i:
                        for h in range(2):
                            pool.wait_ge(staged, i * 2 + h + 1)
                            hold(held, i * 2 + h)
                            for k in range(h * HALF, h * HALF + HALF):
                                nc.gpsimd.indirect_dma_start(
                                    out=u[:, k, :], out_offset=None, in_=table,
                                    in_offset=bass.IndirectOffsetOnAxis(ap=ix[:, k:k + 1], axis=0),
                                    bounds_check=NPAD - 1, oob_is_err=False).then_inc(got[h], 16)

                @block.sync
                def _(sp):
                    sp.sem_inc(mf, 2)
                    with sp.Fori(0, n_it) as i:
                        for h in range(2):
                            sp.wait_ge(red, done(i * 4 + 2 * h + 1))
                            sp.dma_start(msg_v[:, bass.ds(i * RING + h * HALF, HALF), :],
                                         m[:, h * HALF:h * HALF + HALF, :]).then_inc(put[h], 16)
                            sp.wait_ge(put[h], (i + 1) * 16)
                            sp.sem_inc(mf, 1)

                @block.tensor
                def _(pe):
                    regs = id_registers(pe, tag + "_z")
                    pe.sem_inc(trd, 2)
                    pe.sem_inc(zd, 2)

                    def transposes(n, b):
                        pe.wait_ge(sd, done(n))
                        pe.wait_ge(tev, free(n))
                        for k in range(QUAD):
                            last = nc.tensor.transpose(tp[:, b, k, :], us[:, b, k, :, :].rearrange("p a f -> p (a f)"), ident[:, :])
                        last.then_inc(trd, 1)

                    def turn(i, last_turn):
                        for q in range(4):
                            if not (last_turn and q == 3):
                                transposes(i * 4 + (q + 1), (q + 1) % 2)
                            if q % 2 == 0:
                                ids = load_ids(pe, regs, koff, i * RING + q * QUAD, 93)
                            pe.wait_ge(tev, done(i * 4 + q))
                            pe.wait_ge(zu, free(i * 4 + q))
                            for k in range(QUAD):
                                sub = w[:, bass.ds(ids[(q % 2) * QUAD + k] * wout, wout)]
                                ker = bass.AP(sub.tensor, sub.offset, [sub.ap[0]] + steps)
                                last = nc.tensor.matmul(zq(q % 2)[:, k * cols:(k + 1) * cols],
                                                        ut[:, q % 2, k, :], ker, start=True, stop=True)
                            last.then_inc(zd, 1)

                    transposes(0, 0)
                    with pe.Fori(0, n_it - 1) as i:
                        turn(i, False)
                    turn(n_it - 1, True)

                @block.vector
                def _(v):
                    v.sem_inc(uf, 2)
                    v.sem_inc(sd, 2)
                    v.sem_inc(zu, 2)
                    v.sem_inc(red, 2)

                    def scale(i, q, n):
                        if q % 2 == 0:
                            v.wait_ge(got[q // 2], (i + 1) * per)
                        v.wait_ge(trd, free(n))
                        nc.vector.tensor_tensor(
                            us[:, q % 2, :, :, :], u[:, q * QUAD:(q + 1) * QUAD, None, :].to_broadcast([P, QUAD, na, win]),
                            wa[:, bass.ds(i * RING + q * QUAD, QUAD), :, None].to_broadcast([P, QUAD, na, win]),
                            ALU.mult).then_inc(sd, 1)
                        if q % 2 == 1:
                            v.wait_ge(sd, done(n))
                            v.sem_inc(uf, 1)

                    def turn(i, last_turn):
                        for q in range(4):
                            n = i * 4 + q
                            if not (last_turn and q >= 2):
                                scale(i + (q + 2) // 4, (q + 2) % 4, n + 2)
                            v.wait_ge(zd, done(n))
                            v.wait_ge(red, free(n))
                            nc.vector.tensor_tensor(
                                pr[:, q % 2, :, :, :].rearrange("p t b o -> p (t b) o"),
                                zq(q % 2).rearrange("p (s o) -> p s o", o=wout),
                                wb[:, bass.ds(i * RING + q * QUAD, QUAD), :].rearrange("p t b -> p (t b)")
                                [:, :, None].to_broadcast([P, QUAD * nb, wout]),
                                ALU.mult).then_inc(zu, 1)
                            v.wait_ge(zu, done(n))
                            if q % 2 == 0:
                                v.wait_ge(mf, free(i * 2 + q // 2))
                            nc.vector.reduce_sum(
                                m[:, q * QUAD:(q + 1) * QUAD, :],
                                pr[:, q % 2, :, :, :].rearrange("p t b o -> p t o b"), axis=AX).then_inc(red, 1)

                    scale(0, 0, 0)
                    scale(0, 1, 1)
                    with v.Fori(0, n_it - 1) as i:
                        turn(i, False)
                    turn(n_it - 1, True)

        def segment_loop(tag, width, rows, msg, acc):
            cs = ExitStack()
            with cs:
                g = sb(tag + "g", [P, RING, width], c=cs)
                ix = sb(tag + "ix", [P, RING], i32, c=cs)
                oh = sb(tag + "oh", [P, 2, HALF, P], c=cs)
                got = [sem(f"{tag}got{h}", cs) for h in range(2)]
                held = sem(tag + "held", cs)
                staged = sem(tag + "staged", cs)
                made = sem(tag + "made", cs)
                used = sem(tag + "used", cs)
                block = cs.enter_context(nc.Block())
                n_it = TS // RING
                per = 16 * HALF

                @block.scalar
                def _(act):
                    with act.Fori(0, n_it) as i:
                        for h in range(2):
                            act.wait_ge(used, free(i * 2 + h))
                            nc.scalar.copy(ix[:, h * HALF:h * HALF + HALF],
                                           rows[:, bass.ds(i * RING + h * HALF, HALF)]).then_inc(staged, 1)

                @block.gpsimd
                def _(pool):
                    with pool.Fori(0, n_it) as i:
                        for h in range(2):
                            pool.wait_ge(staged, i * 2 + h + 1)
                            hold(held, i * 2 + h)
                            for k in range(h * HALF, h * HALF + HALF):
                                nc.gpsimd.indirect_dma_start(
                                    out=g[:, k, :], out_offset=None, in_=msg,
                                    in_offset=bass.IndirectOffsetOnAxis(ap=ix[:, k:k + 1], axis=0),
                                    bounds_check=P * TC - 1, oob_is_err=False).then_inc(got[h], 16)

                @block.vector
                def _(v):
                    with v.Fori(0, n_it) as i:
                        for h in range(2):
                            v.wait_ge(used, free(i * 2 + h))
                            onehots(oh[:, h, :, :], h, i).then_inc(made, 1)

                @block.tensor
                def _(pe):
                    flat = acc[:, :, :].rearrange("p a b -> p (a b)")
                    regs = id_registers(pe, tag + "_seg")
                    pe.sem_inc(used, 2)
                    for s in range(acc.shape[1]):
                        nc.tensor.matmul(acc[:, s, :], zeros[:, 0:P], zeros[:, :], start=True, stop=True)
                    with pe.Fori(0, n_it) as i:
                        for h in range(2):
                            ids = load_ids(pe, regs, chunk_i, i * RING + h * HALF, NCH - 1)
                            pe.wait_ge(made, i * 2 + h + 1)
                            pe.wait_ge(got[h], (i + 1) * per)
                            for k in range(HALF):
                                last = nc.tensor.matmul(flat[:, bass.ds(ids[k] * width, width)], oh[:, h, k, :],
                                                        g[:, h * HALF + k, :], start=False, stop=True, skip_group_check=True)
                            last.then_inc(used, 1)

        def norm_steps(v, go, y, o, mean, sq, rootd, root_ready, n):
            bc = lambda a: a[:, :, None].to_broadcast([P, NCH, F])
            go(nc.vector.reduce_sum(mean[:, :], y, axis=AX))
            go(nc.vector.tensor_scalar(mean[:, :], mean[:, :], 1.0 / F, None, ALU.mult))
            go(nc.vector.tensor_tensor(o, y, bc(mean), ALU.subtract))
            go(nc.vector.tensor_tensor(sq[:, :, :], o, o, ALU.mult))
            go(nc.vector.reduce_sum(mean[:, :], sq[:, :, :], axis=AX))
            nc.vector.tensor_scalar(mean[:, :], mean[:, :], 1.0 / F, 1e-5, ALU.mult, ALU.add).then_inc(root_ready, 1)
            v.wait_ge(rootd, n)
            go(nc.vector.reciprocal(mean[:, :], mean[:, :]))
            go(nc.vector.tensor_tensor(o, o, bc(mean), ALU.mult))

        oht_v = oht_d.rearrange("p (t n) -> p t n", n=P)
        c3 = ExitStack()
        with c3:
            hat = sb("hat", [P, TS, 3, KS], c=c3)
            cs = ExitStack()
            with cs:
                pp4 = sb("pp4", [P, TS, 3], c=cs)
                ta = sb("ta", [P, TS, 3], c=cs)
                ld = sem("ldB", cs)
                block = cs.enter_context(nc.Block())

                @block.sync
                def _(sp):
                    sp.dma_start(rs[:, :, :].rearrange("p t w -> p (t w)"),
                                 rec_s.rearrange("(p t) w -> p (t w)", p=P)).then_inc(ld, 16)

                @block.vector
                def _(v):
                    go = line.on(v)
                    v.wait_ge(ld, 16)
                    p, t = pp4[:, :, :], ta[:, :, :]
                    hk = lambda k: hat[:, :, :, k]
                    go(nc.vector.tensor_scalar(p, rs[:, :, 2:5], float(KS - 1), None, ALU.mult))
                    go(nc.vector.tensor_scalar(t, p, -1.0, 1.0, ALU.mult, ALU.add))
                    go(nc.vector.tensor_scalar(hk(0), t, 0.0, None, ALU.max))
                    go(nc.vector.tensor_scalar(t, p, -1.0, 2.0, ALU.mult, ALU.add))
                    go(nc.vector.scalar_tensor_tensor(hk(1), t, 0.0, p, ALU.max, ALU.min))
                    go(nc.vector.tensor_scalar(t, p, -1.0, 3.0, ALU.mult, ALU.add))
                    go(nc.vector.scalar_tensor_tensor(t, p, 1.0, t, ALU.subtract, ALU.min))
                    go(nc.vector.tensor_scalar(hk(2), t, 0.0, None, ALU.max))
                    go(nc.vector.tensor_scalar(t, p, 2.0, 0.0, ALU.subtract, ALU.max))
                    go(nc.vector.tensor_scalar(hk(3), p, -1.0, 4.0, ALU.mult, ALU.add))
                    go(nc.vector.tensor_tensor(hk(3), hk(3), t, ALU.min))
                    go(nc.vector.tensor_scalar(hk(4), p, 3.0, 0.0, ALU.subtract, ALU.max))

            cp = ExitStack()
            with cp:
                acc = pb("acc1", [P, 7, 512], cp)
                cs = ExitStack()
                with cs:
                    ohf = sb("ohf", [P, 2, HALF, P], c=cs)
                    ohb = sb("ohb", [P, 2, HALF, P], bf16, c=cs)
                    b01 = sb("b01", [P, 2, HALF, KS * KS], c=cs)
                    bas = sb("bas", [P, 2, HALF, KK + 1], c=cs)
                    ot = sb("ot1", [P, 2, HALF, P], bf16, c=cs)
                    tp = pb("tp1", [P, HALF, P], cs, bf16)
                    made = sem("made", cs)
                    chv = sem("chv", cs)
                    used = sem("used", cs)
                    trd = sem("trd", cs)
                    tev = sem("tev", cs)
                    put = [sem(f"ot_put{h}", cs) for h in range(2)]
                    ini = sem("ini1", cs)

                    block = cs.enter_context(nc.Block())
                    n_it = TS // RING

                    @block.gpsimd
                    def _(pool):
                        by_cell.on_pool(pool, SORT_TURNS, EC // RING)

                    @block.sync
                    def _(sp):
                        by_cell.on_sync(sp, SORT_TURNS, EC // RING)

                    @block.vector
                    def _(v):
                        nc.vector.memset(bas[:, :, :, KK:KK + 1], 1.0).then_inc(ini, 1)
                        v.wait_ge(ini, 1)
                        with v.Fori(0, n_it) as i:
                            for h in range(2):
                                v.wait_ge(used, free(i * 2 + h))
                                at = bass.ds(i * RING + h * HALF, HALF)
                                lk = Chain(v, chv, i * 4 + h * 2)
                                lk(onehots(ohf[:, h, :, :], h, i))
                                nc.vector.tensor_copy(ohb[:, h, :, :], ohf[:, h, :, :])
                                lk(nc.vector.tensor_tensor(
                                    b01[:, h, :, :].rearrange("p t (a b) -> p t a b", a=KS),
                                    hat[:, at, 0, :, None].to_broadcast([P, HALF, KS, KS]),
                                    hat[:, at, 1, None, :].to_broadcast([P, HALF, KS, KS]), ALU.mult))
                                nc.vector.tensor_tensor(
                                    bas[:, h, :, 0:KK].rearrange("p t (a b) -> p t a b", b=KS),
                                    b01[:, h, :, :, None].to_broadcast([P, HALF, KS * KS, KS]),
                                    hat[:, at, 2, None, :].to_broadcast([P, HALF, KS * KS, KS]),
                                    ALU.mult).then_inc(made, 1)

                    @block.tensor
                    def _(pe):
                        flat = acc[:, :, :].rearrange("p a b -> p (a b)")
                        regs = id_registers(pe, "stn1")
                        pe.sem_inc(used, 2)
                        for s in range(7):
                            nc.tensor.matmul(acc[:, s, :], zeros[:, 0:P], zeros[:, :], start=True, stop=True)
                        with pe.Fori(0, n_it) as i:
                            for h in range(2):
                                ids = load_ids(pe, regs, chunk_i, i * RING + h * HALF, NCH - 1)
                                pe.wait_ge(made, i * 2 + h + 1)
                                pe.wait_ge(tev, i * 2 + (h + 1))
                                for k in range(HALF):
                                    last = nc.tensor.transpose(tp[:, k, :], ohb[:, h, k, :], identb[:, :])
                                last.then_inc(trd, 1)
                                for k in range(HALF):
                                    last = nc.tensor.matmul(flat[0:KK + 1, bass.ds(ids[k] * P, P)], bas[:, h, k, :],
                                                            ohf[:, h, k, :], start=False, stop=True, skip_group_check=True)
                                last.then_inc(used, 1)

                    @block.scalar
                    def _(act):
                        act.sem_inc(tev, 1)

                        act.sem_inc(put[0], 16)
                        act.sem_inc(put[1], 16)
                        with act.Fori(0, n_it) as i:
                            for h in range(2):
                                act.wait_ge(trd, i * 2 + h + 1)
                                act.wait_ge(put[h], (i + 1) * 16)
                                nc.scalar.copy(ot[:, h, :, :], tp[:, :, :]).then_inc(tev, 1)
                                act.wait_ge(tev, i * 2 + (h + 2))
                                act.dma_start(oht_v[:, bass.ds(i * RING + h * HALF, HALF), :], ot[:, h, :, :]).then_inc(put[h], 16)
                        for h in range(2):
                            act.wait_ge(put[h], (n_it + 1) * 16)

                s1acc = sb("s1acc", [KK + 1, NPAD], c=c3)
                cs = ExitStack()
                with cs:
                    cpd = sem("cpd", cs)
                    block = cs.enter_context(nc.Block())

                    @block.vector
                    def _(v):
                        nc.vector.tensor_copy(s1acc[:, :], acc[:, :, :].rearrange("p a b -> p (a b)")[0:KK + 1, 0:NPAD]).then_inc(cpd, 1)
                        v.wait_ge(cpd, 1)

            cs = ExitStack()
            with cs:
                w1x = sb("w1x", [KK + 1, H + 1], c=cs)
                bb1 = sb("bb1", [P, H], c=cs)
                h1 = sb("h1", [P, NCH, H + 1], c=cs)
                low = sb("low", [P, NCH, H], c=cs)
                hp = pb("hp", [P, 4, 512], cs)
                ld = sem("ldC", cs)
                wz = sem("wz", cs)
                h1p = sem("h1p", cs)
                er = sem("er", cs)
                ed = sem("ed", cs)
                st = sem("stC", cs)
                h1d = sem("h1d", cs)
                block = cs.enter_context(nc.Block())

                @block.sync
                def _(sp):
                    sp.wait_ge(wz, 1)
                    sp.dma_start(w1x[0:KK, 0:H], s1w.rearrange("k a h -> k (a h)")).then_inc(ld, 16)
                    sp.dma_start(w1x[KK:KK + 1, H:H + 1], ones[0:1, 0:1]).then_inc(ld, 16)
                    sp.dma_start(bb1[:, :], s1b.rearrange("(a n) -> a n", a=1).to_broadcast([P, H])).then_inc(ld, 16)
                    sp.wait_ge(h1d, 1)
                    sp.dma_start(h1_tab.rearrange("(c p) h -> p c h", p=P), h1[:, :, 0:H]).then_inc(st, 16)
                    sp.wait_ge(st, 16)

                @block.tensor
                def _(pe):
                    pe.wait_ge(ld, 48)
                    for c in range(NCH):
                        last = nc.tensor.matmul(hp[:, c // 7, (c % 7) * (H + 1):(c % 7 + 1) * (H + 1)],
                                                s1acc[:, c * P:(c + 1) * P], w1x[:, :], start=True, stop=True)
                    last.then_inc(h1p, 1)

                @block.scalar
                def _(act):
                    act.wait_ge(er, 1)
                    nc.scalar.activation(low[:, :, :], low[:, :, :], ACT.Exp).then_inc(ed, 1)

                @block.vector
                def _(v):
                    nc.vector.memset(w1x[:, :], 0.0).then_inc(wz, 1)
                    go = line.on(v)
                    v.wait_ge(h1p, 1)
                    v.wait_ge(ld, 48)
                    for b in range(4):
                        n = min(7, NCH - 7 * b)
                        go(nc.vector.tensor_copy(h1[:, 7 * b:7 * b + n, :].rearrange("p c h -> p (c h)"), hp[:, b, 0:n * (H + 1)]))
                    go(nc.vector.tensor_scalar(rdeg_s[:, :], h1[:, :, H], 1.0, None, ALU.max))
                    go(nc.vector.reciprocal(rdeg_s[:, :], rdeg_s[:, :]))
                    hh = h1[:, :, 0:H]
                    go(nc.vector.tensor_tensor(hh, hh, rdeg_s[:, :, None].to_broadcast([P, NCH, H]), ALU.mult))
                    go(nc.vector.tensor_tensor(hh, hh, bb1[:, None, :].to_broadcast([P, NCH, H]), ALU.add))
                    elu_steps(v, go, hh, low[:, :, :], er, ed, 1)
                    nc.vector.memset(low[0:1, 0, 0:1], 0.0).then_inc(h1d, 1)

        c0.close()
        c9 = ExitStack()
        with c9:
            koff = sb("koff", [P, TC], i32, c=c9)
            dst_i = sb("dst_i", [P, TS], i32, c=c9)
            posc_i = sb("posc_i", [P, TS], i32, c=c9)

            def first_kernel_steps(go, sh, lo):
                go(nc.vector.tensor_scalar(sh[:, :], cell_i[:, :], 4, None, ALU.arith_shift_right))
                go(nc.vector.tensor_copy(koff[:, :], sh[:, :]))
                go(nc.vector.tensor_scalar(koff[:, :], koff[:, :], float(KS), None, ALU.mult))
                go(nc.vector.tensor_scalar(sh[:, :], cell_i[:, :], 2, 3, ALU.arith_shift_right, ALU.bitwise_and))
                go(nc.vector.tensor_tensor(koff[:, :], koff[:, :], sh[:, :], ALU.add))
                go(nc.vector.tensor_scalar(koff[:, :], koff[:, :], float(KS), None, ALU.mult))
                go(nc.vector.tensor_scalar(lo[:, :], cell_i[:, :], 3, None, ALU.bitwise_and))
                go(nc.vector.tensor_tensor(koff[:, :], koff[:, :], lo[:, :], ALU.add))

            def corner_steps(go, fr, fg, w4, first, w2, other):
                go(nc.vector.tensor_copy(fg[:, :, :, 1], fr))
                go(nc.vector.tensor_scalar(fg[:, :, :, 0], fr, -1.0, 1.0, ALU.mult, ALU.add))
                go(nc.vector.tensor_tensor(w4[:, :, :].rearrange("p t (a b) -> p t a b", a=2),
                                           fg[:, :, first, :, None].to_broadcast([P, TC, 2, 2]),
                                           fg[:, :, first + 1, None, :].to_broadcast([P, TC, 2, 2]), ALU.mult))
                go(nc.vector.tensor_copy(w2[:, :, :], fg[:, :, other, :]))

            c5 = ExitStack()
            with c5:
                w2s = sb("w2s", [P, KK * H], c=c5)
                fg = sb("fg", [P, TC, 3, 2], c=c5)
                w01 = sb("w01", [P, TC, 4], c=c5)
                wz2 = sb("wz2", [P, TC, 2], c=c5)
                cdst = sb("cdst", [P, TC], i32, c=c5)
                cs = ExitStack()
                with cs:
                    rc = sb("rc", [P, TC, CW], c=cs)
                    sh = sb("shG", [P, TC], i32, c=cs)
                    lo = sb("loG", [P, TC], i32, c=cs)
                    ld = sem("ldG", cs)
                    block = cs.enter_context(nc.Block())

                    @block.sync
                    def _(sp):
                        sp.dma_start(rc[:, :, :].rearrange("p t w -> p (t w)"),
                                     rec_c.rearrange("(p t) w -> p (t w)", p=P)).then_inc(ld, 16)
                        sp.dma_start(w2s[0:H, :].rearrange("i (k o) -> i k o", o=H), s2w.rearrange("k i o -> i k o")).then_inc(ld, 16)
                        sp.dma_start(w2s[H:P, 0:(KK - 1) * H].rearrange("i (k o) -> i k o", o=H),
                                     s2w[1:KK, :, :].rearrange("k i o -> i k o")).then_inc(ld, 16)
                        sp.wait_ge(ld, 48)

                    @block.vector
                    def _(v):
                        go = line.on(v)
                        first_kernel_steps(go, sh, lo)
                        go(nc.vector.tensor_scalar(dst_i[:, :], rs[:, :, 1], 0.0, None, ALU.max))
                        go(nc.vector.tensor_copy(posc_i[:, :], rs[:, :, 5]))
                        v.wait_ge(ld, 48)
                        go(nc.vector.tensor_copy(cdst[:, :], rc[:, :, 0]))
                        corner_steps(go, rc[:, :, 1:4], fg, w01, 0, wz2, 2)

                cell_loop("c2", H, H, w2s, koff, wz2, w01, cdst, h1_tab, msg2)

            def node_copy(tag, acc, o, width):
                cs = ExitStack()
                with cs:
                    cpd = sem(tag + "cpd", cs)
                    block = cs.enter_context(nc.Block())

                    @block.vector
                    def _(v):
                        nc.vector.tensor_tensor(o[:, :, :], acc[:, :, :].rearrange("p a b -> p (a b)")[:, 0:NCH * width]
                                                .rearrange("p (c f) -> p c f", f=width),
                                                rdeg_s[:, :, None].to_broadcast([P, NCH, width]), ALU.mult).then_inc(cpd, 1)
                        v.wait_ge(cpd, 1)

            c6 = ExitStack()
            with c6:
                h2 = sb("h2", [P, NCH, H], c=c6)
                cp = ExitStack()
                with cp:
                    acc = pb("acc2", [P, 4, 512], cp)
                    segment_loop("m2", H, posc_i, msg2, acc)
                    node_copy("n2", acc, h2, H)
                cs = ExitStack()
                with cs:
                    low = sb("lowH", [P, NCH, H], c=cs)
                    h2T = sb("h2T", [H, NPAD], c=cs)
                    h3T = sb("h3T", [H, NPAD], c=cs)
                    lowT = sb("lowT", [H, NPAD], c=cs)
                    w3 = sb("w3", [H, H], c=cs)
                    w4 = sb("w4", [H, 3], c=cs)
                    bb = sb("bbH", [P, H], c=cs)
                    bc3 = sb("bc3", [H, 1], c=cs)
                    bb4 = sb("bb4", [P, 3], c=cs)
                    tn = sb("tn", [P, NCH, TW], c=cs)
                    trest = sb("trest", [P, NCH, 3], c=cs)
                    pT = pb("pT", [H, 7, 512], cs)
                    p4 = pb("p4", [P, 512], cs)
                    ld = sem("ldH", cs)
                    er = sem("erH", cs)
                    ed = sem("edH", cs)
                    h2d = sem("h2d", cs)
                    ptd = sem("ptd", cs)
                    ptc = sem("ptc", cs)
                    st = sem("stH", cs)
                    xd = sem("xdH", cs)
                    block = cs.enter_context(nc.Block())

                    @block.sync
                    def _(sp):
                        sp.dma_start(w3[:, :], s3w).then_inc(ld, 16)
                        sp.dma_start(w4[:, :], s4w).then_inc(ld, 16)
                        sp.dma_start(bb[:, :], s2b.rearrange("(a n) -> a n", a=1).to_broadcast([P, H])).then_inc(ld, 16)
                        sp.dma_start(bb4[:, :], s4b.rearrange("(a n) -> a n", a=1).to_broadcast([P, 3])).then_inc(ld, 16)
                        sp.dma_start(bc3[:, :], s3b.rearrange("(n a) -> n a", a=1)).then_inc(ld, 16)
                        sp.wait_ge(xd, 1)
                        sp.dma_start(t_tab.rearrange("(c p) w -> p c w", p=P), tn[:, :, :]).then_inc(st, 16)
                        sp.wait_ge(st, 16)

                    @block.scalar
                    def _(act):
                        act.wait_ge(er, 1)
                        nc.scalar.activation(low[:, :, :], low[:, :, :], ACT.Exp).then_inc(ed, 1)
                        act.wait_ge(er, 2)
                        nc.scalar.activation(lowT[:, :], lowT[:, :], ACT.Exp).then_inc(ed, 1)

                    @block.tensor
                    def _(pe):
                        pe.wait_ge(h2d, 1)
                        for c in range(NCH):
                            last = nc.tensor.transpose(pT[:, c // 4, (c % 4) * P:(c % 4 + 1) * P], h2[:, c, :], ident[:, :])
                        last.then_inc(ptd, 1)
                        pe.wait_ge(ptc, 1)
                        for s in range(7):
                            w = min(512, NPAD - s * 512)
                            last = nc.tensor.matmul(pT[:, s, 0:w], w3[:, :], h2T[:, s * 512:s * 512 + w], start=True, stop=True)
                        last.then_inc(ptd, 1)
                        pe.wait_ge(ptc, 2)
                        for c in range(NCH):
                            last = nc.tensor.matmul(p4[:, c * 3:c * 3 + 3], h3T[:, c * P:(c + 1) * P], w4[:, :], start=True, stop=True)
                        last.then_inc(ptd, 1)

                    @block.vector
                    def _(v):
                        go = line.on(v)
                        go(nc.vector.memset(tn[:, :, :], 0.0))
                        v.wait_ge(ld, 80)
                        go(nc.vector.tensor_tensor(h2[:, :, :], h2[:, :, :], bb[:, None, :].to_broadcast([P, NCH, H]), ALU.add))
                        elu_steps(v, go, h2[:, :, :], low[:, :, :], er, ed, 1)
                        nc.vector.memset(low[0:1, 0, 0:1], 0.0).then_inc(h2d, 1)
                        flat = pT[:, :, :].rearrange("p a b -> p (a b)")[:, 0:NPAD]
                        v.wait_ge(ptd, 1)
                        nc.vector.tensor_copy(h2T[:, :], flat).then_inc(ptc, 1)
                        v.wait_ge(ptd, 2)
                        go(nc.vector.tensor_scalar(h3T[:, :], flat, bc3[:, :], None, ALU.add))
                        elu_steps(v, go, h3T[:, :], lowT[:, :], er, ed, 2)
                        nc.vector.memset(lowT[0:1, 0:1], 0.0).then_inc(ptc, 1)
                        v.wait_ge(ptd, 3)
                        tt = tn[:, :, 0:3]
                        go(nc.vector.tensor_tensor(tt, p4[:, 0:3 * NCH].rearrange("p (c f) -> p c f", f=3),
                                                   bb4[:, None, :].to_broadcast([P, NCH, 3]), ALU.add))
                        split3(go, tt, [xt3[:, :, 3 * F + 3 * k:3 * F + 3 * k + 3] for k in range(3)], trest[:, :, :])
                        nc.vector.memset(trest[0:1, 0, 0:1], 0.0).then_inc(xd, 1)

            row_d = sb("row_d", [P, TS], i32, c=c9)
            c8 = ExitStack()
            with c8:
                tsrc = sb("tsrc", [P, TS, 9], c=c8)
                tdst = sb("tdst", [P, TS, TW], c=c8)
                recD = sb("recD", [P, TS, CW], c=c8)
                key_d = sb("key_d", [P, TS], c=c8)

                def sage_loop(tag, acc, dstc, sel, width, beside, first, end, tsrc):
                    cs = ExitStack()
                    with cs:
                        oh = sb(tag + "oh", [P, 2, HALF, P], bf16, c=cs)
                        d = sb(tag + "d", [P, RING // 2, DHALF], bf16, c=cs)
                        gs = sb(tag + "gs", [P, 4, QUAD, P], bf16, c=cs)
                        gp = pb(tag + "gp", [P, 512], cs)
                        ohl = [sem(f"{tag}ohl{h}", cs) for h in range(2)]
                        dm = sem(tag + "dm", cs)
                        du = sem(tag + "du", cs)
                        gd = sem(tag + "gd", cs)
                        ge = sem(tag + "ge", cs)
                        ini = sem(tag + "ini", cs)
                        block = cs.enter_context(nc.Block())
                        n_it = TS // RING
                        tab = xt3[:, :, :].rearrange("p c f -> p (c f)")

                        @block.sync
                        def _(sp):
                            beside.on_sync(sp, first, end)

                        @block.gpsimd
                        def _(pool):
                            beside.on_pool(pool, first, end)

                        @block.vector
                        def _(v):
                            nc.vector.memset(gs[:, :, :, 3 * F:P], 1.0).then_inc(ini, 1)
                            with v.Fori(0, n_it) as i:
                                for k in range(RING):
                                    v.wait_ge(du, i * RING + (k + 1))
                                    nc.vector.tensor_scalar(d[:, k % 8, :], iota16[:, :], dstc[:, bass.ds(i * RING + k, 1)],
                                                            None, ALU.is_equal).then_inc(dm, 1)

                        @block.scalar
                        def _(act):
                            def copy_rows(i, h, r, wait):
                                n = i * 4 + (2 * h + r)
                                act.wait_ge(gd, n + 1)
                                if wait:
                                    act.wait_ge(du, n * 4 - 4)
                                rows = gp[:, 0:QUAD * width].rearrange("p (a b) -> p a b", a=QUAD)
                                if width == XT:
                                    nc.scalar.copy(tsrc[:, bass.ds(n * QUAD, QUAD), :], rows[:, :, 3 * F:XT])
                                nc.scalar.copy(gs[:, 2 * h + r, :, 0:3 * F], rows[:, :, 0:3 * F]).then_inc(ge, 1)

                            def load(i, h):
                                act.dma_start(oh[:, h, :, :], oht_v[:, bass.ds(i * RING + h * HALF, HALF), :]).then_inc(ohl[h], 16)

                            for h in range(2):
                                load(0, h)
                            act.wait_ge(ini, 1)
                            act.sem_inc(ge, 1)
                            beside.first(act)
                            for r in range(2):
                                copy_rows(0, 0, r, False)
                            with act.Fori(0, n_it - 1) as i:
                                for h in range(2):
                                    load(i + 1, h)
                                    for r in range(2):
                                        copy_rows(i + h, 1 - h, r, True)
                                    beside.after(act, i, h, False)
                            for r in range(2):
                                copy_rows(n_it - 1, 1, r, True)
                            for h in range(2):
                                beside.after(act, n_it - 1, h, True)

                        @block.tensor
                        def _(pe):
                            regs = id_registers(pe, tag + "_g", 2 * HALF)
                            pe.sem_inc(du, 8)
                            flat = acc[:, :, :].rearrange("p a b -> p (a b)")
                            for s in range(7):
                                nc.tensor.matmul(acc[:, s, :], zeros[:, 0:P], zeros[:, :], start=True, stop=True)

                            def gather(i, h, r, ids):
                                if r == 0:
                                    pe.wait_ge(ohl[h], (i + 1) * 16)
                                pe.wait_ge(ge, i * 4 + (2 * h + r + 1))
                                for k in range(QUAD):
                                    last = nc.tensor.matmul(gp[:, k * width:(k + 1) * width], oh[:, h, r * QUAD + k, :],
                                                            tab[:, bass.ds(ids[r * QUAD + k] * XT, width)], start=True, stop=True)
                                last.then_inc(gd, 1)

                            def sums(i, h, r, halves):
                                q = 2 * h + r
                                pe.wait_ge(ge, i * 4 + (q + 2))
                                for k in range(QUAD):
                                    t = q * QUAD + k
                                    pe.wait_ge(dm, i * RING + (t + 1))
                                    for s in range(4):
                                        half = halves[r * QUAD + k]
                                        bank = half * 2048 + s * 512 if s < 3 else half * 1536 + 1536
                                        last = nc.tensor.matmul(flat[:, bass.ds(bank, DSEG)], gs[:, q, k, :],
                                                                d[:, t % 8, s * DSEG:(s + 1) * DSEG],
                                                                start=False, stop=True, skip_group_check=True)
                                    last.then_inc(du, 1)

                            def half_turn(i, h, last_half):
                                at = i * (2 * RING) + (h + 1) * RING
                                pe.load(regs, sel[0:1, bass.ds(at, RING)])
                                ids = [pe.snap(r, min_val=0, max_val=NCH - 1) for r in regs[0:HALF]]
                                halves = [pe.snap(r, min_val=0, max_val=1) for r in regs[HALF:RING]]
                                for r in range(2):
                                    if not last_half:
                                        gather(i + h, 1 - h, r, ids)
                                    sums(i, h, r, halves)

                            pe.load(regs, sel[0:1, 0:RING])
                            ids = [pe.snap(r, min_val=0, max_val=NCH - 1) for r in regs[0:HALF]]
                            for r in range(2):
                                gather(0, 0, r, ids)
                            with pe.Fori(0, n_it - 1) as i:
                                for h in range(2):
                                    half_turn(i, h, False)
                            for h in range(2):
                                half_turn(n_it - 1, h, h == 1)

                c4 = ExitStack()
                with c4:
                    dstc = sb("dstc", [P, TS], c=c4)
                    sel = sb("sel", [P, (TS // HALF + 1) * RING], i32, c=c4)
                    xn = sb("xn", [P, NCH, F], c=c4)
                    agg = sb("agg", [P, NPAD], c=c4)
                    q2 = sb("q2", [P, NCH, F], c=c4)
                    wa = sb("wa", [P, H], c=c4)
                    wd = sb("wd", [P, H], c=c4)
                    wr1 = sb("wr1", [F, H], c=c4)
                    w2 = sb("w2", [H, 2 * F], c=c4)
                    bc1 = sb("bc1", [H, 1], c=c4)
                    bb2 = sb("bb2", [P, F], c=c4)
                    fold = sb("fold", [P, F + 1], c=c4)
                    cs = ExitStack()
                    with cs:
                        rest = sb("rest", [P, NCH, F], c=cs)
                        ld = sem("ldD", cs)
                        ldx = sem("ldx", cs)
                        wz = sem("wzD", cs)
                        block = cs.enter_context(nc.Block())

                        @block.sync
                        def _(sp):
                            sp.wait_ge(wz, 2)
                            sp.dma_start(xn[:, 0:NCH - 1, :], x[0:(NCH - 1) * P, :].rearrange("(c p) f -> p c f", p=P)).then_inc(ldx, 16)
                            sp.dma_start(xn[0:NREM, NCH - 1, :], x[(NCH - 1) * P:N, :]).then_inc(ldx, 16)
                            for k in range(3):
                                sp.dma_start(wa[k * F:(k + 1) * F, :], w1l).then_inc(ld, 16)
                            sp.dma_start(wd[3 * F:3 * F + 1, :], ones[0:1, 0:H]).then_inc(ld, 16)
                            sp.dma_start(wr1[:, :], w1r).then_inc(ld, 16)
                            sp.dma_start(w2[:, 0:F], w2l).then_inc(ld, 16)
                            sp.dma_start(w2[:, F:2 * F], w2r).then_inc(ld, 16)
                            sp.dma_start(bc1[:, :], b1.rearrange("(n a) -> n a", a=1)).then_inc(ld, 16)
                            sp.dma_start(bb2[:, :], b2.rearrange("(a n) -> a n", a=1).to_broadcast([P, F])).then_inc(ld, 16)
                            for k in range(3):
                                sp.dma_start(fold[k * F:(k + 1) * F, 0:F], ident[0:F, 0:F]).then_inc(ld, 16)
                            sp.dma_start(fold[3 * F:3 * F + 1, F:F + 1], ones[0:1, 0:1]).then_inc(ld, 16)
                            sp.wait_ge(ld, 16 * 13)

                        @block.vector
                        def _(v):
                            nc.vector.memset(xn[:, :, :], 0.0).then_inc(wz, 1)
                            nc.vector.memset(wa[:, :], 0.0)
                            nc.vector.memset(fold[:, :], 0.0)
                            nc.vector.memset(wd[:, :], 0.0).then_inc(wz, 1)
                            go = line.on(v)
                            go(nc.vector.tensor_scalar(dstc[:, :], rs[:, :, 1], float(DHALF), float(-DHALF), ALU.is_ge, ALU.mult))
                            go(nc.vector.tensor_tensor(dstc[:, :], dstc[:, :], rs[:, :, 1], ALU.add))
                            selv = sel[:, :].rearrange("p (j k) -> p j k", k=RING)
                            go(nc.vector.memset(sel[:, :], 0))
                            go(nc.vector.tensor_copy(selv[:, 0:TS // HALF, 0:HALF], chunk_i[:, :].rearrange("p (j k) -> p j k", k=HALF)))
                            go(nc.vector.tensor_copy(selv[:, 1:, HALF:RING], half_i[:, :].rearrange("p (j k) -> p j k", k=HALF)))
                            v.wait_ge(ldx, 32)
                            split3(go, xn[:, :, :], [xt3[:, :, k * F:(k + 1) * F] for k in range(3)], rest[:, :, :])

                    def sage_sum(tag, width, beside, first, end, tsrc):
                        cp = ExitStack()
                        with cp:
                            acc = pb(tag + "acc", [P, 7, 512], cp)
                            sage_loop(tag, acc, dstc, sel, width, beside, first, end, tsrc)
                            cs = ExitStack()
                            with cs:
                                cpd = sem(tag + "cpd", cs)
                                block = cs.enter_context(nc.Block())

                                @block.vector
                                def _(v):
                                    nc.vector.memset(agg[:, N:NPAD], 0.0).then_inc(cpd, 1)
                                    v.wait_ge(cpd, 1)
                                    nc.vector.tensor_copy(agg[:, 0:6 * DSEG].rearrange("p (a b) -> p a b", a=6), acc[:, 0:6, 0:DSEG])
                                    nc.vector.tensor_copy(agg[:, 6 * DSEG:N], acc[:, 6, 0:N - 6 * DSEG]).then_inc(cpd, 1)
                                    v.wait_ge(cpd, 2)

                    cs = ExitStack()
                    with cs:
                        sage_sum("g1", XT, Gather("td", t_tab, NPAD, dst_i, tdst, cs), 0, TS // RING, tsrc)

                    cs = ExitStack()
                    with cs:
                        np_ = sb("np_", [P, TS, 3], c=cs)
                        fl = sb("fl3", [P, TS, 3], c=cs)
                        tt = sb("tt3", [P, TS, 3], c=cs)
                        block = cs.enter_context(nc.Block())

                        @block.vector
                        def _(v):
                            go = line.on(v)
                            p = np_[:, :, :]
                            go(nc.vector.reduce_sum(fl[:, :, :], tsrc[:, :, :].rearrange("p t (a d) -> p t d a", a=3), axis=AX))
                            go(nc.vector.tensor_tensor(p, rs[:, :, 2:5], tdst[:, :, 0:3], ALU.add))
                            go(nc.vector.tensor_tensor(p, p, fl[:, :, :], ALU.subtract))
                            go(nc.vector.tensor_scalar(p, p, 0.0, 1.0, ALU.max, ALU.min))
                            go(nc.vector.tensor_scalar(p, p, float(KS - 1), None, ALU.mult))
                            cell_steps(go, p, fl[:, :, :], tt[:, :, :], key_d[:, :])
                            go(nc.vector.tensor_copy(recD[:, :, 1:4], fl[:, :, :]))
                            go(nc.vector.tensor_copy(recD[:, :, 0], dst_i[:, :]))
                            go(nc.vector.tensor_scalar(tt[:, :, 0], rs[:, :, 0], 0.0, 1000.0, ALU.is_lt, ALU.mult))
                            go(nc.vector.tensor_tensor(key_d[:, :], key_d[:, :], tt[:, :, 0], ALU.add))

                    c2 = ExitStack()
                    with c2:
                        sort_block("sd", key_d[:, :], TS, CELLS, TC, row_d[:, :], cell_i, c2)

                    cn = ExitStack()
                    with cn:
                        by_new = Scatter("xd", recD, row_d, rec_d, P * TC, cn)
                        cs = ExitStack()
                        with cs:
                            xt = sb("xt", [F, NPAD], c=cs)
                            hT = sb("hT", [H, NPAD], c=cs)
                            rest = agg[:, 0:NCH * F].rearrange("p (c f) -> p c f", f=F)
                            pn = agg[:, NCH * F:2 * NCH * F].rearrange("p (c f) -> p c f", f=F)
                            pa = pb("pa", [H, 512], cs)
                            pd = pb("pd", [H, 512], cs)
                            pr_ = pb("prr", [H, 512], cs)
                            pq = pb("pq", [P, 4, 512], cs)
                            ld = sem("ldE", cs)
                            mm = sem("mmE", cs)
                            fr = sem("frE", cs)
                            rl = sem("rlE", cs)
                            pqd = sem("pqd", cs)
                            wz = sem("wzE", cs)
                            block = cs.enter_context(nc.Block())

                            @block.gpsimd
                            def _(pool):
                                by_new.on_pool(pool, 0, MID_TURNS)

                            @block.sync
                            def _(sp):
                                sp.wait_ge(wz, 1)
                                sp.dma_start(xt[:, 0:N], xT).then_inc(ld, 16)
                                by_new.on_sync(sp, 0, MID_TURNS)

                            @block.tensor
                            def _(pe):
                                pe.wait_ge(ld, 16)
                                for s in range(7):
                                    w = min(512, NPAD - s * 512)
                                    c = slice(s * 512, s * 512 + w)
                                    if s:
                                        pe.wait_ge(fr, s)
                                    nc.tensor.matmul(pa[:, 0:w], wa[:, :], agg[:, c], start=True, stop=True)
                                    nc.tensor.matmul(pd[:, 0:w], wd[:, :], agg[:, c], start=True, stop=True)
                                    nc.tensor.matmul(pr_[:, 0:w], wr1[:, :], xt[:, c], start=True, stop=True).then_inc(mm, 1)
                                pe.wait_ge(rl, 7)
                                for c in range(NCH):
                                    last = nc.tensor.matmul(pq[:, c // 8, (c % 8) * H:(c % 8 + 1) * H], hT[:, c * P:(c + 1) * P], w2[:, :],
                                                            start=True, stop=True)
                                last.then_inc(pqd, 1)

                            @block.scalar
                            def _(act):
                                for s in range(7):
                                    w = min(512, NPAD - s * 512)
                                    act.wait_ge(fr, s + 1)
                                    nc.scalar.activation(hT[:, s * 512:s * 512 + w], hT[:, s * 512:s * 512 + w], ACT.Relu, bias=bc1[:, :]).then_inc(rl, 1)

                            @block.vector
                            def _(v):
                                nc.vector.memset(xt[:, :], 0.0).then_inc(wz, 1)
                                go = line.on(v)
                                for s in range(7):
                                    w = min(512, NPAD - s * 512)
                                    v.wait_ge(mm, s + 1)
                                    a = hT[:, s * 512:s * 512 + w]
                                    go(nc.vector.tensor_scalar(a, pd[:, 0:w], 1.0, None, ALU.max))
                                    go(nc.vector.reciprocal(a, a))
                                    go(nc.vector.tensor_tensor(a, a, pa[:, 0:w], ALU.mult))
                                    nc.vector.tensor_tensor(a, a, pr_[:, 0:w], ALU.add).then_inc(fr, 1)
                                v.wait_ge(pqd, 1)
                                for b in range(4):
                                    n = min(8, NCH - 8 * b)
                                    view = pq[:, b, 0:n * H].rearrange("p (c f) -> p c f", f=H)
                                    go(nc.vector.tensor_copy(pn[:, 8 * b:8 * b + n, :], view[:, :, 0:F]))
                                    go(nc.vector.tensor_tensor(q2[:, 8 * b:8 * b + n, :], view[:, :, F:H],
                                                               bb2[:, None, :].to_broadcast([P, n, F]), ALU.add))
                                split3(go, pn[:, :, :], [xt3[:, :, k * F:(k + 1) * F] for k in range(3)], rest[:, :, :])

                        sage_sum("g2", 3 * F, by_new, MID_TURNS, TS // RING, None)

                    cs = ExitStack()
                    with cs:
                        pf = pb("pf", [P, 2, 512], cs)
                        y = sb("yE", [P, NCH, F], c=cs)
                        rd = sb("rdE", [P, NCH], c=cs)
                        mean = sb("meanE", [P, NCH], c=cs)
                        sq = sb("sqE", [P, NCH, F], c=cs)
                        fd = sem("fdF", cs)
                        rr = sem("rrF", cs)
                        rt = sem("rtF", cs)
                        xs = sem("x1_made", cs)
                        st = sem("x1_stored", cs)
                        block = cs.enter_context(nc.Block())
                        CB = 512 // (F + 1)

                        @block.tensor
                        def _(pe):
                            for c in range(NCH):
                                last = nc.tensor.matmul(pf[:, c // CB, (c % CB) * (F + 1):(c % CB + 1) * (F + 1)],
                                                        agg[:, c * P:(c + 1) * P], fold[:, :], start=True, stop=True)
                            last.then_inc(fd, 1)

                        @block.scalar
                        def _(act):
                            act.wait_ge(rr, 1)
                            nc.scalar.activation(mean[:, :], mean[:, :], ACT.Sqrt).then_inc(rt, 1)

                        @block.vector
                        def _(v):
                            go = line.on(v)
                            v.wait_ge(fd, 1)
                            for b in range(2):
                                n = min(CB, NCH - CB * b)
                                view = pf[:, b, 0:n * (F + 1)].rearrange("p (c f) -> p c f", f=F + 1)
                                s = slice(CB * b, CB * b + n)
                                go(nc.vector.tensor_scalar(rd[:, s], view[:, :, F], 1.0, None, ALU.max))
                                go(nc.vector.reciprocal(rd[:, s], rd[:, s]))
                                go(nc.vector.tensor_tensor(y[:, s, :], view[:, :, 0:F], rd[:, s, None].to_broadcast([P, n, F]), ALU.mult))
                            go(nc.vector.tensor_tensor(y[:, :, :], y[:, :, :], q2[:, :, :], ALU.add))
                            go(nc.vector.tensor_tensor(y[:, :, :], y[:, :, :], xn[:, :, :], ALU.add))
                            norm_steps(v, go, y[:, :, :], x1[:, :, :], mean, sq, rt, rr, 1)
                            nc.vector.memset(mean[0:1, 0:1], 0.0).then_inc(xs, 1)

                        @block.sync
                        def _(sp):
                            sp.wait_ge(xs, 1)
                            sp.dma_start(x1_tab.rearrange("(c p) f -> p c f", p=P), x1[:, :, :]).then_inc(st, 16)
                            sp.wait_ge(st, 16)

            c5 = ExitStack()
            with c5:
                cws = sb("cws", [P, KK * F], c=c5)
                fg = sb("fg3", [P, TC, 3, 2], c=c5)
                cdst = sb("cdst3", [P, TC], i32, c=c5)
                w12 = sb("w12", [P, TC, 4], c=c5)
                wx2 = sb("wx2", [P, TC, 2], c=c5)
                cs = ExitStack()
                with cs:
                    fr = sb("fr3", [P, TC, CW], c=cs)
                    sh = sb("shI", [P, TC], i32, c=cs)
                    lo = sb("loI", [P, TC], i32, c=cs)
                    ld = sem("ldI", cs)
                    block = cs.enter_context(nc.Block())

                    @block.sync
                    def _(sp):
                        sp.dma_start(fr[:, :, :].rearrange("p t w -> p (t w)"),
                                     rec_d.rearrange("(p t) w -> p (t w)", p=P)).then_inc(ld, 16)
                        for n, off in enumerate((0, 1, KS, KS + 1)):
                            sp.dma_start(cws[n * F:(n + 1) * F, 0:(KK - off) * F].rearrange("i (k o) -> i k o", o=F),
                                         cw[off:KK, :, :].rearrange("k i o -> i k o")).then_inc(ld, 16)
                        sp.wait_ge(ld, 80)

                    @block.vector
                    def _(v):
                        go = line.on(v)
                        first_kernel_steps(go, sh, lo)
                        go(nc.vector.tensor_scalar(row_d[:, :], row_d[:, :], float(P * TC - 1), None, ALU.min))
                        v.wait_ge(ld, 80)
                        go(nc.vector.tensor_copy(cdst[:, :], fr[:, :, 0]))
                        corner_steps(go, fr[:, :, 1:4], fg, w12, 1, wx2, 0)

                cell_loop("c3", F, F, cws, koff, w12, wx2, cdst, x1_tab, msg3)

            cs = ExitStack()
            with cs:
                y = sb("yJ", [P, NCH, F], c=cs)
                o = sb("oJ", [P, NCH, F], c=cs)
                cp = ExitStack()
                with cp:
                    acc = pb("acc3", [P, 2, 512], cp)
                    segment_loop("m3", F, row_d, msg3, acc)
                    node_copy("n3", acc, y, F)
                mean = sb("meanJ", [P, NCH], c=cs)
                sq = sb("sqJ", [P, NCH, F], c=cs)
                bb = sb("bbJ", [P, F], c=cs)
                ld = sem("ldJ", cs)
                rr = sem("rrJ", cs)
                rt = sem("rtJ", cs)
                od = sem("odJ", cs)
                st = sem("stJ", cs)
                block = cs.enter_context(nc.Block())

                @block.sync
                def _(sp):
                    sp.dma_start(bb[:, :], cb.rearrange("(a n) -> a n", a=1).to_broadcast([P, F])).then_inc(ld, 16)
                    sp.wait_ge(od, 1)
                    sp.dma_start(out[0:(NCH - 1) * P, :].rearrange("(c p) f -> p c f", p=P), o[:, 0:NCH - 1, :]).then_inc(st, 16)
                    sp.dma_start(out[(NCH - 1) * P:N, :], o[0:NREM, NCH - 1, :]).then_inc(st, 16)
                    sp.wait_ge(st, 32)

                @block.scalar
                def _(act):
                    act.wait_ge(rr, 1)
                    nc.scalar.activation(mean[:, :], mean[:, :], ACT.Sqrt).then_inc(rt, 1)

                @block.vector
                def _(v):
                    go = line.on(v)
                    v.wait_ge(ld, 16)
                    go(nc.vector.tensor_tensor(y[:, :, :], y[:, :, :], bb[:, None, :].to_broadcast([P, NCH, F]), ALU.add))
                    go(nc.vector.tensor_tensor(y[:, :, :], y[:, :, :], x1[:, :, :], ALU.add))
                    norm_steps(v, go, y[:, :, :], o[:, :, :], mean, sq, rt, rr, 1)
                    nc.vector.memset(mean[0:1, 0:1], 0.0).then_inc(od, 1)


def kernel(**inputs):
    import numpy as np
    import concourse.bacc as bacc
    from concourse.bass_utils import run_bass_kernel_spmd

    g = {k: np.asarray(v) for k, v in inputs.items()}
    lay = {
        "x": g["x"], "xT": g["x"].T, "src": g["src"], "dst": g["dst"], "ps": g["edge_attr_3"],
        "w1l": g["L0_gnn_W1_l"].T, "w1r": g["L0_gnn_W1_r"].T, "b1": g["L0_gnn_b1"],
        "w2l": g["L0_gnn_W2_l"].T, "w2r": g["L0_gnn_W2_r"].T, "b2": g["L0_gnn_b2"],
        "s1w": g["L1_gnn_stn1_w"], "s1b": g["L1_gnn_stn1_b"], "s2w": g["L1_gnn_stn2_w"], "s2b": g["L1_gnn_stn2_b"],
        "s3w": g["L1_gnn_stn3_w"], "s3b": g["L1_gnn_stn3_b"], "s4w": g["L1_gnn_stn4_w"], "s4b": g["L1_gnn_stn4_b"],
        "cw": g["L1_gnn_conv_w"], "cb": g["L1_gnn_conv_b"],
    }
    nc = bacc.Bacc("TRN2", target_bir_lowering=False, num_devices=1)
    arrays, args = {}, []
    for name, a in lay.items():
        a = np.ascontiguousarray(a)
        arrays["in_" + name] = a
        args.append(nc.dram_tensor("in_" + name, a.shape, mybir.dt.from_np(a.dtype), kind="ExternalInput").ap())
    args.append(nc.dram_tensor("out_0", (N, F), fp32, kind="ExternalOutput").ap())
    gnn_kernel(nc, *args)
    r = run_bass_kernel_spmd(nc, [arrays], core_ids=[0])
    return r.results[0]["out_0"]
```

```python
import concourse.bass as bass
from concourse import mybir
from contextlib import ExitStack

fp32 = mybir.dt.float32
bf16 = mybir.dt.bfloat16
fp16 = mybir.dt.float16
i32 = mybir.dt.int32
i16 = mybir.dt.int16
ALU = mybir.AluOpType
ACT = mybir.ActivationFunctionType
AX = mybir.AxisListType.X

P = 128
N = 3125
E = 53125
F = 32
H = 64
KS = 5
KK = KS ** 3
NCH = -(-N // P)
NPAD = NCH * P
NREM = N - (NCH - 1) * P
CELLS = (KS - 1) ** 3
HALF = 8
RING = 2 * HALF
EC = -(-(-(-E // P)) // RING) * RING
EFULL = E // EC
EREM = E - EFULL * EC
NBK = 2 * NCH
TS = -(-((E + NBK * (P - 1)) // P) // RING) * RING
TC = -(-((E + CELLS * (P - 1)) // P) // RING) * RING
FAR = P * 8192 + P - 1
DSEG = -(-N // 7)
DHALF = 4 * DSEG
RW = 6
CW = 4
TW = 4
XT = 3 * F + 9
assert EFULL == P - 1 and EREM > 0 and NPAD <= 7 * 512


QUAD = 4
LOOK = 8
SORT_TURNS = 8
HAT_TURNS = 1
LAST_TURNS = 2
MID_TURNS = 3
END_TURNS = 1


def free(step):
    return step + 1


def done(step):
    return step + 3


class Chain:

    def __init__(self, eng, sem, base=0):
        self.eng, self.sem, self.base, self.n = eng, sem, base, 0

    def on(self, eng):
        self.eng = eng
        return self

    def __call__(self, ins):
        self.n += 1
        ins.then_inc(self.sem, 1)
        self.eng.wait_ge(self.sem, self.base + self.n)


def gnn_kernel(nc, x, xT, src, dst, ps, w1l, w1r, b1, w2l, w2r, b2,
               s1w, s1b, s2w, s2b, s3w, s3b, s4w, s4b, cw, cb, out):
    ctx = ExitStack()

    def dram(name, shape, dt=fp32):
        return nc.dram_tensor(name, shape, dt, kind="Internal").ap()

    rec_s = dram("rec_s", (P * TS, RW))
    rec_c = dram("rec_c", (P * TC, CW))
    h1_tab = dram("h1_tab", (NPAD, H))
    msg2 = dram("msg2", (P * TC, H))
    oht_d = dram("oht_d", (P, TS * P), bf16)
    t_tab = dram("t_tab", (NPAD, TW))
    x1_tab = dram("x1_tab", (NPAD, F))
    rec_d = dram("rec_d", (P * TC, CW))
    msg3 = dram("msg3", (P * TC, F))

    def sb(name, shape, dt=fp32, c=ctx):
        return c.enter_context(nc.sbuf_tensor(name, shape, dt))

    def sem(name, c=ctx):
        return c.enter_context(nc.semaphore(name))

    def pb(name, shape, c, dt=fp32):
        return c.enter_context(nc.psum_tensor(name, shape, dt))

    with ctx:
        iota16 = sb("iota16", [P, DHALF], fp16)
        iota_f = sb("iota_f", [P, 512])
        line = Chain(None, sem("dve_line"))
        consts = sem("consts_made")
        ident = sb("ident", [P, P])
        identb = sb("identb", [P, P], bf16)
        tri = sb("tri", [P, P])
        ones = sb("ones", [P, P])
        zeros = sb("zeros", [P, 512])

        def hold(held):
            nc.gpsimd.sem_inc(held, 1)

        x1 = sb("x1", [P, NCH, F])
        rdeg_s = sb("rdeg_s", [P, NCH])
        xt3 = sb("xt3", [P, NCH, XT], bf16)
        rs = sb("rs", [P, TS, RW])
        chunk_i = sb("chunk_i", [P, TS], i32)
        half_i = sb("half_i", [P, TS], i32)
        cell_i = sb("cell_i", [P, TC], i32)

        def sort_block(tag, key, C, K, T, row, tile_i, c, beside=None, turns=0):
            KP = -(-K // LOOK) * LOOK
            cnt = sb(tag + "cnt", [P, KP], c=c)
            base = sb(tag + "base", [P, KP], c=c)
            tiles = sb(tag + "tiles", [P, KP], c=c)
            endt = sb(tag + "endt", [P, KP], c=c)
            ti = sb(tag + "ti", [P, KP], i32, c=c)
            ecol = sb(tag + "ecol", [P, 1], c=c)
            key16 = sb(tag + "key16", [P, C], fp16, c=c)
            masks = sb(tag + "masks", [P, KP, C], i16, c=c)
            mask = sb(tag + "mask", [P, LOOK, C], i16, c=c)
            run = sb(tag + "run", [P, LOOK, C], c=c)
            pos2 = sb(tag + "pos", [P, 2, C], c=c)
            pos = pos2[:, 0, :]
            rowlo = sb(tag + "rowlo", [P, C], i32, c=c)
            cmp = sb(tag + "cmp", [P, T], c=c)
            cs = ExitStack()
            with cs:
                pp = pb(tag + "pp", [P, 512], cs)
                pt = pb(tag + "pt", [P, 512], cs)
                v_cnt = sem(tag + "v_cnt", cs)
                pe_px = sem(tag + "pe_px", cs)
                v_cmp = sem(tag + "v_cmp", cs)
                pe_tb = sem(tag + "pe_tb", cs)
                masked = sem(tag + "masked", cs)
                ch2 = sem(tag + "ch2", cs)
                held = sem(tag + "held", cs)
                block = cs.enter_context(nc.Block())

                if beside:
                    @block.sync
                    def _(sp):
                        beside.on_sync(sp, 0, turns)

                    @block.gpsimd
                    def _(pool):
                        beside.on_pool(pool, 0, turns)

                @block.scalar
                def _(act):
                    act.wait_ge(v_cnt, KP)
                    with act.Fori(0, KP // LOOK) as b:
                        for k in range(LOOK):
                            act.wait_ge(ch2, b * (2 * LOOK) + (k + 1))
                            nc.scalar.copy(mask[:, k, :], masks[:, bass.ds(b * LOOK + k, 1), :].rearrange("p a c -> p (a c)")).then_inc(masked, 1)

                @block.tensor
                def _(pe):
                    pe.wait_ge(v_cnt, KP)
                    nc.tensor.matmul(pp[:, 0:KP], tri[:, :], cnt[:, :], start=True, stop=True).then_inc(pe_px, 1)
                    nc.tensor.matmul(pt[:, 0:KP], ones[:, :], cnt[:, :], start=True, stop=True).then_inc(pe_px, 1)
                    pe.wait_ge(v_cmp, 1)
                    nc.tensor.matmul(pp[:, 0:T], ones[0:KP, :], cmp[0:KP, :], start=True, stop=True).then_inc(pe_tb, 1)

                @block.vector
                def _(v):
                    go = line.on(v)
                    go(nc.vector.tensor_copy(key16[:, :], key))
                    with v.Fori(0, KP // LOOK) as b:
                        for k in range(LOOK):
                            b_k = bass.ds(b * LOOK + k, 1)
                            nc.vector.tensor_scalar(masks[:, b_k, :].rearrange("p a c -> p (a c)"), key16[:, :], iota_f[:, b_k], 0.0,
                                                    ALU.is_equal, ALU.add, accum_out=cnt[:, b_k]).then_inc(v_cnt, 1)
                    v.wait_ge(pe_px, 2)
                    go(nc.vector.tensor_scalar(ti[:, :], pt[:, 0:KP], float(P - 1), None, ALU.add))
                    go(nc.vector.tensor_scalar(ti[:, :], ti[:, :], 7, None, ALU.arith_shift_right))
                    go(nc.vector.tensor_copy(tiles[:, :], ti[:, :]))
                    go(nc.vector.tensor_tensor_scan(endt[:, :], tiles[:, :], zeros[:, 0:KP], 0.0, ALU.add, ALU.add))
                    go(nc.vector.tensor_tensor(tiles[:, :], endt[:, :], tiles[:, :], ALU.subtract))
                    go(nc.vector.tensor_scalar(tiles[:, :], tiles[:, :], float(P), -1.0, ALU.mult, ALU.add))
                    go(nc.vector.tensor_tensor(base[:, :], pp[:, 0:KP], tiles[:, :], ALU.add))
                    go(nc.vector.tensor_tensor(endt[:, :], endt[:, :], ident[:, 0:KP], ALU.mult))
                    go(nc.vector.reduce_sum(ecol[:, :], endt[:, :], axis=AX))
                    nc.vector.tensor_scalar(cmp[:, :], iota_f[:, 0:T], ecol[:, :], None, ALU.is_ge).then_inc(v_cmp, 1)
                    v.wait_ge(pe_tb, 1)
                    go(nc.vector.tensor_scalar(cmp[:, :], pp[:, 0:T], float(K - 1), None, ALU.min))
                    go(nc.vector.tensor_copy(tile_i[:, :], cmp[:, :]))
                    go(nc.vector.memset(pos2[:, :, :], float(FAR)))
                    v.sem_inc(ch2, LOOK)
                    with v.Fori(0, KP // LOOK) as b:
                        at = b * (2 * LOOK) + LOOK
                        for k in range(LOOK):
                            v.wait_ge(masked, b * LOOK + (k + 1))
                            nc.vector.tensor_tensor_scan(run[:, k, :], mask[:, k, :], zeros[:, 0:C],
                                                         base[:, bass.ds(b * LOOK + k, 1)], ALU.add, ALU.add).then_inc(ch2, 1)
                        for k in range(LOOK):
                            v.wait_ge(ch2, at + (LOOK + k - 1 if k >= 2 else k + 1))
                            v.sem_inc(held, 1)
                            nc.vector.copy_predicated(pos2[:, k % 2, :], mask[:, k, :], run[:, k, :]).then_inc(ch2, 1)
                    g3 = line.on(v)
                    v.wait_ge(ch2, 2 * KP + LOOK)
                    g3(nc.vector.tensor_tensor(pos, pos, pos2[:, 1, :], ALU.min))
                    g3(nc.vector.tensor_copy(row, pos))
                    g3(nc.vector.tensor_scalar(rowlo[:, :], row, P - 1, None, ALU.bitwise_and))
                    g3(nc.vector.tensor_scalar(row, row, 7, None, ALU.arith_shift_right))
                    g3(nc.vector.tensor_copy(pos, row))
                    g3(nc.vector.scalar_tensor_tensor(pos, rowlo[:, :], float(T), pos, ALU.mult, ALU.add))
                    g3(nc.vector.tensor_copy(row, pos))

        def cell_steps(go, p, flo, key):
            go(nc.vector.tensor_scalar(flo, p, 1.0, None, ALU.is_ge))
            go(nc.vector.scalar_tensor_tensor(flo, p, 2.0, flo, ALU.is_ge, ALU.add))
            go(nc.vector.scalar_tensor_tensor(flo, p, 3.0, flo, ALU.is_ge, ALU.add))
            go(nc.vector.tensor_scalar(key, flo[:, :, 0], 16.0, None, ALU.mult))
            go(nc.vector.scalar_tensor_tensor(key, flo[:, :, 1], 4.0, key, ALU.mult, ALU.add))
            go(nc.vector.tensor_tensor(key, key, flo[:, :, 2], ALU.add))
            go(nc.vector.tensor_tensor(flo, p, flo, ALU.subtract))

        class Scatter:

            def __init__(self, tag, a, r, table, rows, c):
                self.a, self.r, self.table, self.rows = a, r, table, rows
                self.d = sb(tag + "d", [P, RING, a.shape[2]], c=c)
                self.ix = sb(tag + "ix", [P, RING], i32, c=c)
                self.held = sem(tag + "held", c)
                self.staged = [sem(f"{tag}staged{h}", c) for h in range(2)]
                self.sent = [sem(f"{tag}sent{h}", c) for h in range(2)]

            def stage(self, sp, i, h):
                s = slice(h * HALF, h * HALF + HALF)
                sp.dma_start(self.d[:, s, :], self.a[:, bass.ds(i * RING + h * HALF, HALF), :]).then_inc(self.staged[h], 16)
                sp.dma_start(self.ix[:, s], self.r[:, bass.ds(i * RING + h * HALF, HALF)]).then_inc(self.staged[h], 16)

            def send(self, pool, i, h):
                pool.wait_ge(self.staged[h], (i + 1) * 32)
                hold(self.held)
                for k in range(h * HALF, h * HALF + HALF):
                    nc.gpsimd.indirect_dma_start(
                        out=self.table, out_offset=bass.IndirectOffsetOnAxis(ap=self.ix[:, k:k + 1], axis=0),
                        in_=self.d[:, k, :], in_offset=None, bounds_check=self.rows - 1,
                        oob_is_err=False).then_inc(self.sent[h], 16)

            def on_sync(self, sp, first, end):
                if first == 0:
                    for h in range(2):
                        self.stage(sp, 0, h)
                with sp.Fori(max(first, 1), end) as i:
                    for h in range(2):
                        sp.wait_ge(self.sent[h], i * (16 * HALF))
                        self.stage(sp, i, h)
                for h in range(2):
                    sp.wait_ge(self.sent[h], end * (16 * HALF))

            def on_pool(self, pool, first, end):
                with pool.Fori(first, end) as i:
                    for h in range(2):
                        self.send(pool, i, h)

            def first(self, act):
                pass

            def after(self, act, i, h, last_turn):
                pass

        class Gather:

            def __init__(self, tag, table, rows, r, o, c):
                self.table, self.rows, self.r, self.o = table, rows, r, o
                self.g = sb(tag + "g", [P, RING, o.shape[2]], c=c)
                self.ix = sb(tag + "ix", [P, RING], i32, c=c)
                self.staged = sem(tag + "staged", c)
                self.kept = sem(tag + "kept", c)
                self.held = sem(tag + "held", c)
                self.got = [sem(f"{tag}got{h}", c) for h in range(2)]

            def stage(self, act, i, h):
                nc.scalar.copy(self.ix[:, h * HALF:h * HALF + HALF],
                               self.r[:, bass.ds(i * RING + h * HALF, HALF)]).then_inc(self.staged, 1)

            def first(self, act):
                act.sem_inc(self.kept, 2)
                for h in range(2):
                    self.stage(act, 0, h)

            def keep(self, act, i, h):
                act.wait_ge(self.got[h], (i + 1) * (16 * HALF))
                nc.scalar.copy(self.o[:, bass.ds(i * RING + h * HALF, HALF), :],
                               self.g[:, h * HALF:h * HALF + HALF, :]).then_inc(self.kept, 1)

            def on_sync(self, sp, first, end):
                pass

            def on_pool(self, pool, first, end):
                with pool.Fori(first, end) as i:
                    for h in range(2):
                        self.send(pool, i, h)

            def after(self, act, i, h, last_turn):
                self.keep(act, i, h)
                if not last_turn:
                    self.stage(act, i + 1, h)

            def send(self, pool, i, h):
                pool.wait_ge(self.staged, i * 2 + h + 1)
                pool.wait_ge(self.kept, free(i * 2 + h))
                hold(self.held)
                for k in range(h * HALF, h * HALF + HALF):
                    nc.gpsimd.indirect_dma_start(
                        out=self.g[:, k, :], out_offset=None, in_=self.table,
                        in_offset=bass.IndirectOffsetOnAxis(ap=self.ix[:, k:k + 1], axis=0),
                        bounds_check=self.rows - 1, oob_is_err=False).then_inc(self.got[h], 16)

        def scatter_block(tag, a, r, table, rows, C):
            cs = ExitStack()
            with cs:
                sc = Scatter(tag, a, r, table, rows, cs)
                block = cs.enter_context(nc.Block())

                @block.sync
                def _(sp):
                    sc.on_sync(sp, 0, C // RING)

                @block.gpsimd
                def _(pool):
                    sc.on_pool(pool, 0, C // RING)

        c0 = ExitStack()
        recC = sb("recC", [P, EC, CW], c=c0)
        row_c = sb("row_c", [P, EC], i32, c=c0)
        by_cell = Scatter("xc", recC, row_c, rec_c, P * TC, c0)
        c1 = ExitStack()
        with c1:
            ei = sb("ei", [P, 2, EC], i32, c=c1)
            ri = sb("ri", [P, EC], i32, c=c1)
            recS = sb("recS", [P, EC, RW], c=c1)
            key_s = sb("key_s", [P, EC], c=c1)
            key_c = sb("key_c", [P, EC], c=c1)
            pos4 = sb("pos4", [P, EC, 3], c=c1)
            flo = sb("flo", [P, EC, 3], c=c1)
            tmp3 = sb("tmp3", [P, EC, 3], c=c1)
            row_s = sb("row_s", [P, EC], i32, c=c1)
            iota_i = sb("iota_i", [P, 512], i32, c=c1)
            pse = sb("pse", [P, EC, 3], c=c1)
            cs = ExitStack()
            with cs:
                fz = sb("fz", [P, TC * CW], c=cs)
                fillS = sb("fillS", [P, TS, RW], c=cs)
                ld = sem("ld", cs)
                fill = sem("fill", cs)
                pre = sem("pre", cs)
                block = cs.enter_context(nc.Block())

                @block.sync
                def _(sp):
                    sp.wait_ge(pre, 1)
                    for n, a in enumerate((src, dst)):
                        sp.dma_start(ei[0:EFULL, n, :], a[0:EFULL * EC].rearrange("(p c) -> p c", c=EC)).then_inc(ld, 16)
                        sp.dma_start(ei[EFULL:P, n, 0:EREM], a[EFULL * EC:E].rearrange("(p c) -> p c", p=1)).then_inc(ld, 16)
                    sp.dma_start(pse[0:EFULL, :, :], ps[0:EFULL * EC, :].rearrange("(p c) d -> p c d", c=EC)).then_inc(ld, 16)
                    sp.dma_start(pse[EFULL:P, 0:EREM, :], ps[EFULL * EC:E, :].rearrange("(p c) d -> p c d", p=1)).then_inc(ld, 16)
                    sp.wait_ge(ld, 96)
                    sp.dma_start(rec_s.rearrange("(p t) w -> p (t w)", p=P), fillS[:, :, :].rearrange("p t w -> p (t w)")).then_inc(fill, 16)
                    sp.dma_start(rec_c.rearrange("(p a) w -> p (a w)", p=P), fz[:, :]).then_inc(fill, 16)
                    sp.dma_start(rec_d.rearrange("(p a) w -> p (a w)", p=P), fz[:, :]).then_inc(fill, 16)
                    sp.wait_ge(fill, 48)

                @block.gpsimd
                def _(g):
                    g.iota(iota_i[:, :], pattern=[[1, 512]], base=0, channel_multiplier=0).then_inc(consts, 1)
                    g.iota(iota16[:, :], pattern=[[1, DHALF]], base=0, channel_multiplier=0,
                           allow_small_or_imprecise_dtypes=True).then_inc(consts, 1)
                    g.memset(ones[:, :], 1.0).then_inc(consts, 1)
                    g.memset(zeros[:, :], 0.0).then_inc(consts, 1)
                    g.wait_ge(consts, 4)
                    g.affine_select(out=ident[:, :], in_=ones[:, :], compare_op=ALU.is_equal, fill=0.0,
                                    base=0, pattern=[[-1, P]], channel_multiplier=1).then_inc(consts, 1)
                    g.affine_select(out=tri[:, :], in_=ones[:, :], compare_op=ALU.is_gt, fill=0.0,
                                    base=0, pattern=[[1, P]], channel_multiplier=-1).then_inc(consts, 1)

                @block.vector
                def _(v):
                    go = line.on(v)
                    go(nc.vector.memset(fz[:, :], 0.0))
                    go(nc.vector.memset(fillS[:, :, :], 0.0))
                    go(nc.vector.memset(fillS[:, :, 0:2], -1.0))
                    go(nc.vector.memset(ei[:, :, :], 127 * P))
                    nc.vector.memset(pse[:, :, :], 0.0).then_inc(pre, 1)
                    go(nc.vector.memset(recS[:, :, :], 0.0))
                    v.wait_ge(consts, 6)
                    go(nc.vector.tensor_copy(iota_f[:, :], iota_i[:, :]))
                    go(nc.vector.tensor_copy(identb[:, :], ident[:, :]))
                    v.wait_ge(ld, 96)
                    go(nc.vector.tensor_scalar(ri[:, :], ei[:, 0, :], 7, None, ALU.arith_shift_right))
                    go(nc.vector.tensor_copy(key_s[:, :], ri[:, :]))
                    go(nc.vector.tensor_scalar(tmp3[:, :, 1], ei[:, 1, :], float(DHALF), None, ALU.is_ge))
                    go(nc.vector.scalar_tensor_tensor(key_s[:, :], key_s[:, :], 2.0, tmp3[:, :, 1], ALU.mult, ALU.add))
                    go(nc.vector.tensor_scalar(ri[:, :], ei[:, 0, :], P - 1, None, ALU.bitwise_and))
                    go(nc.vector.tensor_copy(recS[:, :, 0], ri[:, :]))
                    go(nc.vector.tensor_copy(recS[:, :, 1], ei[:, 1, :]))
                    go(nc.vector.tensor_copy(recC[:, :, 0], ei[:, 1, :]))
                    go(nc.vector.tensor_copy(recS[:, :, 2:5], pse[:, :, :]))
                    go(nc.vector.tensor_scalar(pos4[:, :, :], pse[:, :, :], float(KS - 1), None, ALU.mult))
                    cell_steps(go, pos4[:, :, :], flo[:, :, :], key_c[:, :])
                    go(nc.vector.tensor_copy(recC[:, :, 1:4], flo[:, :, :]))
                    go(nc.vector.tensor_scalar(tmp3[:, :, 0], key_s[:, :], 100.0, 1000.0, ALU.is_ge, ALU.mult))
                    go(nc.vector.tensor_tensor(key_c[:, :], key_c[:, :], tmp3[:, :, 0], ALU.add))

            c2 = ExitStack()
            with c2:
                sort_block("sc", key_c[:, :], EC, CELLS, TC, row_c[:, :], cell_i, c2)
            c2 = ExitStack()
            with c2:
                sort_block("ss", key_s[:, :], EC, NBK, TS, row_s[:, :], chunk_i, c2, by_cell, SORT_TURNS)
            cs = ExitStack()
            with cs:
                block = cs.enter_context(nc.Block())

                @block.vector
                def _(v):
                    go = line.on(v)
                    go(nc.vector.tensor_copy(recS[:, :, 5], row_c[:, :]))
                    go(nc.vector.tensor_scalar(half_i[:, :], chunk_i[:, :], 1, None, ALU.bitwise_and))
                    go(nc.vector.tensor_scalar(chunk_i[:, :], chunk_i[:, :], 1, None, ALU.arith_shift_right))

            scatter_block("xs", recS, row_s, rec_s, P * TS, EC)

        def id_registers(pe, tag, n=HALF):
            return [pe.alloc_register(f"{tag}_tile{k}") for k in range(n)]

        def load_ids(pe, regs, table, at, most):
            pe.load(regs, table[0:1, bass.ds(at, len(regs))])
            return [pe.snap(r, min_val=0, max_val=most) for r in regs]

        def onehots(out_, h, i):
            return nc.vector.tensor_tensor(
                out_, iota_f[:, None, 0:P].to_broadcast([P, HALF, P]),
                rs[:, bass.ds(i * RING + h * HALF, HALF), 0:1].to_broadcast([P, HALF, P]), ALU.is_equal)


        def split3(go, a, parts, rest):
            go(nc.vector.tensor_copy(parts[0], a))
            go(nc.vector.tensor_tensor(rest, a, parts[0], ALU.subtract))
            go(nc.vector.tensor_copy(parts[1], rest))
            go(nc.vector.tensor_tensor(rest, rest, parts[1], ALU.subtract))
            go(nc.vector.tensor_copy(parts[2], rest))

        def elu_steps(v, go, h, low, exp_ready, exp_done, n):
            nc.vector.tensor_scalar(low, h, 0.0, None, ALU.min).then_inc(exp_ready, 1)
            go(nc.vector.tensor_scalar(h, h, 0.0, None, ALU.max))
            v.wait_ge(exp_done, n)
            go(nc.vector.scalar_tensor_tensor(h, low, 1.0, h, ALU.subtract, ALU.add))

        def cell_loop(tag, win, wout, w, koff, wa, wb, rows, table, msg, load, prepare):
            na = P // win
            nb = 8 // na
            steps = {2: [(KS * KS * wout, 2), (KS * wout, 2), (1, wout)], 4: [(KS * KS * wout, 2), (1, wout)]}[na]
            n_it = TC // RING
            per = 16 * HALF
            cs = ExitStack()
            with cs:
                u = sb(tag + "u", [P, RING, win], c=cs)
                ix = sb(tag + "ix", [P, RING], i32, c=cs)
                us = sb(tag + "us", [P, 2, QUAD, na, win], c=cs)
                ut = sb(tag + "ut", [P, 2, QUAD, P], c=cs)
                pr = sb(tag + "pr", [P, 2, QUAD, nb, wout], c=cs)
                m = sb(tag + "m", [P, RING, wout], c=cs)
                tp = pb(tag + "tp", [P, 2, QUAD, P], cs)
                z = pb(tag + "z", [P, 2, 1024], cs)
                got = [sem(f"{tag}got{h}", cs) for h in range(2)]
                put = [sem(f"{tag}put{h}", cs) for h in range(2)]
                held = sem(tag + "held", cs)
                staged = sem(tag + "staged", cs)
                uf = sem(tag + "uf", cs)
                sd = sem(tag + "sd", cs)
                trd = sem(tag + "trd", cs)
                tev = sem(tag + "tev", cs)
                zd = sem(tag + "zd", cs)
                zu = sem(tag + "zu", cs)
                red = sem(tag + "red", cs)
                mf = sem(tag + "mf", cs)
                indexed = sem(tag + "indexed", cs)
                ready = sem(tag + "ready", cs)
                block = cs.enter_context(nc.Block())
                msg_v = msg.rearrange("(p t) f -> p t f", p=P)
                cols = nb * wout

                def zq(b):
                    return z[:, b, 0:QUAD * cols]

                @block.scalar
                def _(act):
                    act.sem_inc(tev, 2)

                    def stage(i, h):
                        act.wait_ge(uf, free(i * 2 + h))
                        nc.scalar.copy(ix[:, h * HALF:h * HALF + HALF],
                                       rows[:, bass.ds(i * RING + h * HALF, HALF)]).then_inc(staged, 1)

                    def turn(i, last_turn):
                        for q in range(4):
                            act.wait_ge(trd, done(i * 4 + q))
                            act.wait_ge(zd, free(i * 4 + q))
                            nc.scalar.copy(ut[:, q % 2, :, :], tp[:, q % 2, :, :]).then_inc(tev, 1)
                            if q % 2 == 0 and not last_turn:
                                stage(i + 1, q // 2)

                    act.wait_ge(indexed, 1)
                    for h in range(2):
                        stage(0, h)
                    with act.Fori(0, n_it - 1) as i:
                        turn(i, False)
                    turn(n_it - 1, True)

                @block.gpsimd
                def _(pool):
                    with pool.Fori(0, n_it) as i:
                        for h in range(2):
                            pool.wait_ge(staged, i * 2 + h + 1)
                            hold(held)
                            for k in range(h * HALF, h * HALF + HALF):
                                nc.gpsimd.indirect_dma_start(
                                    out=u[:, k, :], out_offset=None, in_=table,
                                    in_offset=bass.IndirectOffsetOnAxis(ap=ix[:, k:k + 1], axis=0),
                                    bounds_check=NPAD - 1, oob_is_err=False).then_inc(got[h], 16)

                @block.sync
                def _(sp):
                    load(sp)
                    sp.sem_inc(mf, 2)
                    with sp.Fori(0, n_it) as i:
                        for h in range(2):
                            sp.wait_ge(red, done(i * 4 + 2 * h + 1))
                            sp.dma_start(msg_v[:, bass.ds(i * RING + h * HALF, HALF), :],
                                         m[:, h * HALF:h * HALF + HALF, :]).then_inc(put[h], 16)
                            sp.wait_ge(put[h], (i + 1) * 16)
                            sp.sem_inc(mf, 1)

                @block.tensor
                def _(pe):
                    regs = id_registers(pe, tag + "_z")
                    pe.sem_inc(trd, 2)
                    pe.sem_inc(zd, 2)

                    def transposes(n, b):
                        pe.wait_ge(sd, done(n))
                        pe.wait_ge(tev, free(n))
                        for k in range(QUAD):
                            last = nc.tensor.transpose(tp[:, b, k, :], us[:, b, k, :, :].rearrange("p a f -> p (a f)"), ident[:, :])
                        last.then_inc(trd, 1)

                    def turn(i, last_turn):
                        for q in range(4):
                            if not (last_turn and q == 3):
                                transposes(i * 4 + (q + 1), (q + 1) % 2)
                            if q % 2 == 0:
                                ids = load_ids(pe, regs, koff, i * RING + q * QUAD, 93)
                            pe.wait_ge(tev, done(i * 4 + q))
                            pe.wait_ge(zu, free(i * 4 + q))
                            for k in range(QUAD):
                                sub = w[:, bass.ds(ids[(q % 2) * QUAD + k] * wout, wout)]
                                ker = bass.AP(sub.tensor, sub.offset, [sub.ap[0]] + steps)
                                last = nc.tensor.matmul(zq(q % 2)[:, k * cols:(k + 1) * cols],
                                                        ut[:, q % 2, k, :], ker, start=True, stop=True)
                            last.then_inc(zd, 1)

                    pe.wait_ge(ready, 1)
                    transposes(0, 0)
                    with pe.Fori(0, n_it - 1) as i:
                        turn(i, False)
                    turn(n_it - 1, True)

                @block.vector
                def _(v):
                    v.sem_inc(uf, 2)
                    prepare(v, indexed, ready)
                    v.sem_inc(sd, 2)
                    v.sem_inc(zu, 2)
                    v.sem_inc(red, 2)

                    def scale(i, q, n):
                        if q % 2 == 0:
                            v.wait_ge(got[q // 2], (i + 1) * per)
                        v.wait_ge(trd, free(n))
                        nc.vector.tensor_tensor(
                            us[:, q % 2, :, :, :], u[:, q * QUAD:(q + 1) * QUAD, None, :].to_broadcast([P, QUAD, na, win]),
                            wa[:, bass.ds(i * RING + q * QUAD, QUAD), :, None].to_broadcast([P, QUAD, na, win]),
                            ALU.mult).then_inc(sd, 1)
                        if q % 2 == 1:
                            v.wait_ge(sd, done(n))
                            v.sem_inc(uf, 1)

                    def turn(i, last_turn):
                        for q in range(4):
                            n = i * 4 + q
                            if not (last_turn and q >= 2):
                                scale(i + (q + 2) // 4, (q + 2) % 4, n + 2)
                            v.wait_ge(zd, done(n))
                            v.wait_ge(red, free(n))
                            nc.vector.tensor_tensor(
                                pr[:, q % 2, :, :, :].rearrange("p t b o -> p (t b) o"),
                                zq(q % 2).rearrange("p (s o) -> p s o", o=wout),
                                wb[:, bass.ds(i * RING + q * QUAD, QUAD), :].rearrange("p t b -> p (t b)")
                                [:, :, None].to_broadcast([P, QUAD * nb, wout]),
                                ALU.mult).then_inc(zu, 1)
                            v.wait_ge(zu, done(n))
                            if q % 2 == 0:
                                v.wait_ge(mf, free(i * 2 + q // 2))
                            nc.vector.reduce_sum(
                                m[:, q * QUAD:(q + 1) * QUAD, :],
                                pr[:, q % 2, :, :, :].rearrange("p t b o -> p t o b"), axis=AX).then_inc(red, 1)

                    scale(0, 0, 0)
                    scale(0, 1, 1)
                    with v.Fori(0, n_it - 1) as i:
                        turn(i, False)
                    turn(n_it - 1, True)

        def segment_loop(tag, width, rows, msg, acc):
            cs = ExitStack()
            with cs:
                g = sb(tag + "g", [P, RING, width], c=cs)
                ix = sb(tag + "ix", [P, RING], i32, c=cs)
                oh = sb(tag + "oh", [P, 2, HALF, P], c=cs)
                got = [sem(f"{tag}got{h}", cs) for h in range(2)]
                held = sem(tag + "held", cs)
                staged = sem(tag + "staged", cs)
                made = sem(tag + "made", cs)
                used = sem(tag + "used", cs)
                block = cs.enter_context(nc.Block())
                n_it = TS // RING
                per = 16 * HALF

                @block.scalar
                def _(act):
                    with act.Fori(0, n_it) as i:
                        for h in range(2):
                            act.wait_ge(used, free(i * 2 + h))
                            nc.scalar.copy(ix[:, h * HALF:h * HALF + HALF],
                                           rows[:, bass.ds(i * RING + h * HALF, HALF)]).then_inc(staged, 1)

                @block.gpsimd
                def _(pool):
                    with pool.Fori(0, n_it) as i:
                        for h in range(2):
                            pool.wait_ge(staged, i * 2 + h + 1)
                            hold(held)
                            for k in range(h * HALF, h * HALF + HALF):
                                nc.gpsimd.indirect_dma_start(
                                    out=g[:, k, :], out_offset=None, in_=msg,
                                    in_offset=bass.IndirectOffsetOnAxis(ap=ix[:, k:k + 1], axis=0),
                                    bounds_check=P * TC - 1, oob_is_err=False).then_inc(got[h], 16)

                @block.vector
                def _(v):
                    with v.Fori(0, n_it) as i:
                        for h in range(2):
                            v.wait_ge(used, free(i * 2 + h))
                            onehots(oh[:, h, :, :], h, i).then_inc(made, 1)

                @block.tensor
                def _(pe):
                    flat = acc[:, :, :].rearrange("p a b -> p (a b)")
                    regs = id_registers(pe, tag + "_seg")
                    pe.sem_inc(used, 2)
                    for s in range(acc.shape[1]):
                        nc.tensor.matmul(acc[:, s, :], zeros[:, 0:P], zeros[:, :], start=True, stop=True)
                    with pe.Fori(0, n_it) as i:
                        for h in range(2):
                            ids = load_ids(pe, regs, chunk_i, i * RING + h * HALF, NCH - 1)
                            pe.wait_ge(made, i * 2 + h + 1)
                            pe.wait_ge(got[h], (i + 1) * per)
                            for k in range(HALF):
                                last = nc.tensor.matmul(flat[:, bass.ds(ids[k] * width, width)], oh[:, h, k, :],
                                                        g[:, h * HALF + k, :], start=False, stop=True, skip_group_check=True)
                            last.then_inc(used, 1)

        def norm_steps(v, go, y, o, mean, sq, rootd, root_ready, n):
            bc = lambda a: a[:, :, None].to_broadcast([P, NCH, F])
            go(nc.vector.reduce_sum(mean[:, :], y, axis=AX))
            go(nc.vector.tensor_scalar(mean[:, :], mean[:, :], 1.0 / F, None, ALU.mult))
            go(nc.vector.tensor_tensor(o, y, bc(mean), ALU.subtract))
            go(nc.vector.tensor_tensor(sq[:, :, :], o, o, ALU.mult))
            go(nc.vector.reduce_sum(mean[:, :], sq[:, :, :], axis=AX))
            nc.vector.tensor_scalar(mean[:, :], mean[:, :], 1.0 / F, 1e-5, ALU.mult, ALU.add).then_inc(root_ready, 1)
            v.wait_ge(rootd, n)
            go(nc.vector.reciprocal(mean[:, :], mean[:, :]))
            go(nc.vector.tensor_tensor(o, o, bc(mean), ALU.mult))

        oht_v = oht_d.rearrange("p (t n) -> p t n", n=P)
        c3 = ExitStack()
        with c3:
            hat = sb("hat", [P, TS, 3, KS], c=c3)
            cs = ExitStack()
            with cs:
                pp4 = sb("pp4", [P, TS, 3], c=cs)
                ta = sb("ta", [P, TS, 3], c=cs)
                ld = sem("ldB", cs)
                block = cs.enter_context(nc.Block())

                @block.sync
                def _(sp):
                    sp.dma_start(rs[:, :, :].rearrange("p t w -> p (t w)"),
                                 rec_s.rearrange("(p t) w -> p (t w)", p=P)).then_inc(ld, 16)
                    by_cell.on_sync(sp, SORT_TURNS, SORT_TURNS + HAT_TURNS)

                @block.gpsimd
                def _(pool):
                    by_cell.on_pool(pool, SORT_TURNS, SORT_TURNS + HAT_TURNS)

                @block.vector
                def _(v):
                    go = line.on(v)
                    v.wait_ge(ld, 16)
                    p, t = pp4[:, :, :], ta[:, :, :]
                    hk = lambda k: hat[:, :, :, k]
                    go(nc.vector.tensor_scalar(p, rs[:, :, 2:5], float(KS - 1), None, ALU.mult))
                    go(nc.vector.tensor_scalar(t, p, -1.0, 1.0, ALU.mult, ALU.add))
                    go(nc.vector.tensor_scalar(hk(0), t, 0.0, None, ALU.max))
                    go(nc.vector.tensor_scalar(t, p, -1.0, 2.0, ALU.mult, ALU.add))
                    go(nc.vector.scalar_tensor_tensor(hk(1), t, 0.0, p, ALU.max, ALU.min))
                    go(nc.vector.tensor_scalar(t, p, -1.0, 3.0, ALU.mult, ALU.add))
                    go(nc.vector.scalar_tensor_tensor(t, p, 1.0, t, ALU.subtract, ALU.min))
                    go(nc.vector.tensor_scalar(hk(2), t, 0.0, None, ALU.max))
                    go(nc.vector.tensor_scalar(t, p, 2.0, 0.0, ALU.subtract, ALU.max))
                    go(nc.vector.tensor_scalar(hk(3), p, -1.0, 4.0, ALU.mult, ALU.add))
                    go(nc.vector.tensor_tensor(hk(3), hk(3), t, ALU.min))
                    go(nc.vector.tensor_scalar(hk(4), p, 3.0, 0.0, ALU.subtract, ALU.max))

            cp = ExitStack()
            with cp:
                acc = pb("acc1", [P, 7, 512], cp)
                cs = ExitStack()
                with cs:
                    ohf = sb("ohf", [P, 2, HALF, P], c=cs)
                    ohb = sb("ohb", [P, 2, HALF, P], bf16, c=cs)
                    b01 = sb("b01", [P, 2, HALF, KS * KS], c=cs)
                    bas = sb("bas", [P, 2, HALF, KK + 1], c=cs)
                    ot = sb("ot1", [P, 2, HALF, P], bf16, c=cs)
                    tp = pb("tp1", [P, HALF, P], cs, bf16)
                    made = sem("made", cs)
                    chv = sem("chv", cs)
                    used = sem("used", cs)
                    trd = sem("trd", cs)
                    tev = sem("tev", cs)
                    put = [sem(f"ot_put{h}", cs) for h in range(2)]
                    ini = sem("ini1", cs)

                    block = cs.enter_context(nc.Block())
                    n_it = TS // RING

                    @block.gpsimd
                    def _(pool):
                        by_cell.on_pool(pool, SORT_TURNS + HAT_TURNS, EC // RING - LAST_TURNS)

                    @block.sync
                    def _(sp):
                        by_cell.on_sync(sp, SORT_TURNS + HAT_TURNS, EC // RING - LAST_TURNS)

                    @block.vector
                    def _(v):
                        nc.vector.memset(bas[:, :, :, KK:KK + 1], 1.0).then_inc(ini, 1)
                        v.wait_ge(ini, 1)
                        with v.Fori(0, n_it) as i:
                            for h in range(2):
                                v.wait_ge(used, free(i * 2 + h))
                                at = bass.ds(i * RING + h * HALF, HALF)
                                lk = Chain(v, chv, i * 4 + h * 2)
                                lk(onehots(ohf[:, h, :, :], h, i))
                                nc.vector.tensor_copy(ohb[:, h, :, :], ohf[:, h, :, :])
                                lk(nc.vector.tensor_tensor(
                                    b01[:, h, :, :].rearrange("p t (a b) -> p t a b", a=KS),
                                    hat[:, at, 0, :, None].to_broadcast([P, HALF, KS, KS]),
                                    hat[:, at, 1, None, :].to_broadcast([P, HALF, KS, KS]), ALU.mult))
                                nc.vector.tensor_tensor(
                                    bas[:, h, :, 0:KK].rearrange("p t (a b) -> p t a b", b=KS),
                                    b01[:, h, :, :, None].to_broadcast([P, HALF, KS * KS, KS]),
                                    hat[:, at, 2, None, :].to_broadcast([P, HALF, KS * KS, KS]),
                                    ALU.mult).then_inc(made, 1)

                    @block.tensor
                    def _(pe):
                        flat = acc[:, :, :].rearrange("p a b -> p (a b)")
                        regs = id_registers(pe, "stn1")
                        pe.sem_inc(used, 2)
                        for s in range(7):
                            nc.tensor.matmul(acc[:, s, :], zeros[:, 0:P], zeros[:, :], start=True, stop=True)
                        with pe.Fori(0, n_it) as i:
                            for h in range(2):
                                ids = load_ids(pe, regs, chunk_i, i * RING + h * HALF, NCH - 1)
                                pe.wait_ge(made, i * 2 + h + 1)
                                pe.wait_ge(tev, i * 2 + (h + 1))
                                for k in range(HALF):
                                    last = nc.tensor.transpose(tp[:, k, :], ohb[:, h, k, :], identb[:, :])
                                last.then_inc(trd, 1)
                                for k in range(HALF):
                                    last = nc.tensor.matmul(flat[0:KK + 1, bass.ds(ids[k] * P, P)], bas[:, h, k, :],
                                                            ohf[:, h, k, :], start=False, stop=True, skip_group_check=True)
                                last.then_inc(used, 1)

                    @block.scalar
                    def _(act):
                        act.sem_inc(tev, 1)

                        act.sem_inc(put[0], 16)
                        act.sem_inc(put[1], 16)
                        with act.Fori(0, n_it) as i:
                            for h in range(2):
                                act.wait_ge(trd, i * 2 + h + 1)
                                act.wait_ge(put[h], (i + 1) * 16)
                                nc.scalar.copy(ot[:, h, :, :], tp[:, :, :]).then_inc(tev, 1)
                                act.wait_ge(tev, i * 2 + (h + 2))
                                act.dma_start(oht_v[:, bass.ds(i * RING + h * HALF, HALF), :], ot[:, h, :, :]).then_inc(put[h], 16)
                        for h in range(2):
                            act.wait_ge(put[h], (n_it + 1) * 16)

                s1acc = sb("s1acc", [KK + 1, NPAD], c=c3)
                cs = ExitStack()
                with cs:
                    cpd = sem("cpd", cs)
                    block = cs.enter_context(nc.Block())

                    @block.vector
                    def _(v):
                        nc.vector.tensor_copy(s1acc[:, :], acc[:, :, :].rearrange("p a b -> p (a b)")[0:KK + 1, 0:NPAD]).then_inc(cpd, 1)
                        v.wait_ge(cpd, 1)

            cs = ExitStack()
            with cs:
                w1x = sb("w1x", [KK + 1, H + 1], c=cs)
                bb1 = sb("bb1", [P, H], c=cs)
                h1 = sb("h1", [P, NCH, H + 1], c=cs)
                low = sb("low", [P, NCH, H], c=cs)
                hp = pb("hp", [P, 4, 512], cs)
                ld = sem("ldC", cs)
                wz = sem("wz", cs)
                h1p = sem("h1p", cs)
                er = sem("er", cs)
                ed = sem("ed", cs)
                st = sem("stC", cs)
                h1d = sem("h1d", cs)
                block = cs.enter_context(nc.Block())

                @block.sync
                def _(sp):
                    sp.wait_ge(wz, 1)
                    sp.dma_start(w1x[0:KK, 0:H], s1w.rearrange("k a h -> k (a h)")).then_inc(ld, 16)
                    sp.dma_start(w1x[KK:KK + 1, H:H + 1], ones[0:1, 0:1]).then_inc(ld, 16)
                    sp.dma_start(bb1[:, :], s1b.rearrange("(a n) -> a n", a=1).to_broadcast([P, H])).then_inc(ld, 16)
                    by_cell.on_sync(sp, EC // RING - LAST_TURNS, EC // RING)

                @block.gpsimd
                def _(pool):
                    by_cell.on_pool(pool, EC // RING - LAST_TURNS, EC // RING)

                @block.tensor
                def _(pe):
                    pe.wait_ge(ld, 48)
                    for c in range(NCH):
                        last = nc.tensor.matmul(hp[:, c // 7, (c % 7) * (H + 1):(c % 7 + 1) * (H + 1)],
                                                s1acc[:, c * P:(c + 1) * P], w1x[:, :], start=True, stop=True)
                    last.then_inc(h1p, 1)

                @block.scalar
                def _(act):
                    act.wait_ge(er, 1)
                    nc.scalar.activation(low[:, :, :], low[:, :, :], ACT.Exp).then_inc(ed, 1)
                    act.wait_ge(h1d, 1)
                    act.dma_start(h1_tab.rearrange("(c p) h -> p c h", p=P), h1[:, :, 0:H]).then_inc(st, 16)
                    act.wait_ge(st, 16)

                @block.vector
                def _(v):
                    nc.vector.memset(w1x[:, :], 0.0).then_inc(wz, 1)
                    go = line.on(v)
                    v.wait_ge(h1p, 1)
                    v.wait_ge(ld, 48)
                    for b in range(4):
                        n = min(7, NCH - 7 * b)
                        go(nc.vector.tensor_copy(h1[:, 7 * b:7 * b + n, :].rearrange("p c h -> p (c h)"), hp[:, b, 0:n * (H + 1)]))
                    go(nc.vector.tensor_scalar(rdeg_s[:, :], h1[:, :, H], 1.0, None, ALU.max))
                    go(nc.vector.reciprocal(rdeg_s[:, :], rdeg_s[:, :]))
                    hh = h1[:, :, 0:H]
                    go(nc.vector.tensor_tensor(hh, hh, rdeg_s[:, :, None].to_broadcast([P, NCH, H]), ALU.mult))
                    go(nc.vector.tensor_tensor(hh, hh, bb1[:, None, :].to_broadcast([P, NCH, H]), ALU.add))
                    elu_steps(v, go, hh, low[:, :, :], er, ed, 1)
                    nc.vector.memset(low[0:1, 0, 0:1], 0.0).then_inc(h1d, 1)

        c0.close()
        c9 = ExitStack()
        with c9:
            koff = sb("koff", [P, TC], i32, c=c9)
            dst_i = sb("dst_i", [P, TS], i32, c=c9)
            posc_i = sb("posc_i", [P, TS], i32, c=c9)

            def first_kernel_steps(go, sh, lo):
                go(nc.vector.tensor_scalar(sh[:, :], cell_i[:, :], 4, None, ALU.arith_shift_right))
                go(nc.vector.tensor_copy(koff[:, :], sh[:, :]))
                go(nc.vector.tensor_scalar(koff[:, :], koff[:, :], float(KS), None, ALU.mult))
                go(nc.vector.tensor_scalar(sh[:, :], cell_i[:, :], 2, 3, ALU.arith_shift_right, ALU.bitwise_and))
                go(nc.vector.tensor_tensor(koff[:, :], koff[:, :], sh[:, :], ALU.add))
                go(nc.vector.tensor_scalar(koff[:, :], koff[:, :], float(KS), None, ALU.mult))
                go(nc.vector.tensor_scalar(lo[:, :], cell_i[:, :], 3, None, ALU.bitwise_and))
                go(nc.vector.tensor_tensor(koff[:, :], koff[:, :], lo[:, :], ALU.add))

            def corner_steps(go, fr, fg, w4, first, w2, other):
                go(nc.vector.tensor_copy(fg[:, :, :, 1], fr))
                go(nc.vector.tensor_scalar(fg[:, :, :, 0], fr, -1.0, 1.0, ALU.mult, ALU.add))
                go(nc.vector.tensor_tensor(w4[:, :, :].rearrange("p t (a b) -> p t a b", a=2),
                                           fg[:, :, first, :, None].to_broadcast([P, TC, 2, 2]),
                                           fg[:, :, first + 1, None, :].to_broadcast([P, TC, 2, 2]), ALU.mult))
                go(nc.vector.tensor_copy(w2[:, :, :], fg[:, :, other, :]))

            c5 = ExitStack()
            with c5:
                w2s = sb("w2s", [P, KK * H], c=c5)
                fg = sb("fg", [P, TC, 3, 2], c=c5)
                w01 = sb("w01", [P, TC, 4], c=c5)
                wz2 = sb("wz2", [P, TC, 2], c=c5)
                cdst = sb("cdst", [P, TC], i32, c=c5)
                rc = sb("rc", [P, TC, CW], c=c5)
                sh = sb("shG", [P, TC], i32, c=c5)
                lo = sb("loG", [P, TC], i32, c=c5)
                ldr = sem("ldr2", c5)
                ld = sem("ldG", c5)

                def load2(sp):
                    sp.dma_start(rc[:, :, :].rearrange("p t w -> p (t w)"),
                                 rec_c.rearrange("(p t) w -> p (t w)", p=P)).then_inc(ldr, 16)
                    sp.dma_start(w2s[0:H, :].rearrange("i (k o) -> i k o", o=H), s2w.rearrange("k i o -> i k o")).then_inc(ld, 16)
                    sp.dma_start(w2s[H:P, 0:(KK - 1) * H].rearrange("i (k o) -> i k o", o=H),
                                 s2w[1:KK, :, :].rearrange("k i o -> i k o")).then_inc(ld, 16)

                def prepare2(v, indexed, ready):
                    go = line.on(v)
                    v.wait_ge(ldr, 16)
                    nc.vector.tensor_copy(cdst[:, :], rc[:, :, 0]).then_inc(indexed, 1)
                    first_kernel_steps(go, sh, lo)
                    corner_steps(go, rc[:, :, 1:4], fg, w01, 0, wz2, 2)
                    go(nc.vector.tensor_scalar(dst_i[:, :], rs[:, :, 1], 0.0, None, ALU.max))
                    go(nc.vector.tensor_copy(posc_i[:, :], rs[:, :, 5]))
                    v.wait_ge(ld, 32)
                    nc.vector.memset(sh[:, :], 0).then_inc(ready, 1)

                cell_loop("c2", H, H, w2s, koff, wz2, w01, cdst, h1_tab, msg2, load2, prepare2)

            def node_copy(tag, acc, o, width):
                cs = ExitStack()
                with cs:
                    cpd = sem(tag + "cpd", cs)
                    block = cs.enter_context(nc.Block())

                    @block.vector
                    def _(v):
                        nc.vector.tensor_tensor(o[:, :, :], acc[:, :, :].rearrange("p a b -> p (a b)")[:, 0:NCH * width]
                                                .rearrange("p (c f) -> p c f", f=width),
                                                rdeg_s[:, :, None].to_broadcast([P, NCH, width]), ALU.mult).then_inc(cpd, 1)
                        v.wait_ge(cpd, 1)

            c6 = ExitStack()
            with c6:
                h2 = sb("h2", [P, NCH, H], c=c6)
                cp = ExitStack()
                with cp:
                    acc = pb("acc2", [P, 4, 512], cp)
                    segment_loop("m2", H, posc_i, msg2, acc)
                    node_copy("n2", acc, h2, H)
                cs = ExitStack()
                with cs:
                    low = sb("lowH", [P, NCH, H], c=cs)
                    h2T = sb("h2T", [H, NPAD], c=cs)
                    h3T = sb("h3T", [H, NPAD], c=cs)
                    lowT = sb("lowT", [H, NPAD], c=cs)
                    w3 = sb("w3", [H, H], c=cs)
                    w4 = sb("w4", [H, 3], c=cs)
                    bb = sb("bbH", [P, H], c=cs)
                    bc3 = sb("bc3", [H, 1], c=cs)
                    bb4 = sb("bb4", [P, 3], c=cs)
                    tn = sb("tn", [P, NCH, TW], c=cs)
                    trest = sb("trest", [P, NCH, 3], c=cs)
                    pT = pb("pT", [H, 7, 512], cs)
                    p4 = pb("p4", [P, 512], cs)
                    ld = sem("ldH", cs)
                    er = sem("erH", cs)
                    ed = sem("edH", cs)
                    h2d = sem("h2d", cs)
                    ptd = sem("ptd", cs)
                    ptc = sem("ptc", cs)
                    st = sem("stH", cs)
                    xd = sem("xdH", cs)
                    block = cs.enter_context(nc.Block())

                    @block.sync
                    def _(sp):
                        sp.dma_start(w3[:, :], s3w).then_inc(ld, 16)
                        sp.dma_start(w4[:, :], s4w).then_inc(ld, 16)
                        sp.dma_start(bb[:, :], s2b.rearrange("(a n) -> a n", a=1).to_broadcast([P, H])).then_inc(ld, 16)
                        sp.dma_start(bb4[:, :], s4b.rearrange("(a n) -> a n", a=1).to_broadcast([P, 3])).then_inc(ld, 16)
                        sp.dma_start(bc3[:, :], s3b.rearrange("(n a) -> n a", a=1)).then_inc(ld, 16)
                        sp.wait_ge(xd, 1)
                        sp.dma_start(t_tab.rearrange("(c p) w -> p c w", p=P), tn[:, :, :]).then_inc(st, 16)
                        sp.wait_ge(st, 16)

                    groups = [(0, 4), (4, 7)]

                    def nodes(g):
                        return slice(groups[g][0] * 512, min(groups[g][1] * 512, NPAD))

                    def chunks(g):
                        return slice(groups[g][0] * 4, min(groups[g][1] * 4, NCH))

                    @block.scalar
                    def _(act):
                        for g in range(2):
                            act.wait_ge(er, g + 1)
                            nc.scalar.activation(low[:, chunks(g), :], low[:, chunks(g), :], ACT.Exp).then_inc(ed, 1)
                        for g in range(2):
                            act.wait_ge(er, g + 3)
                            nc.scalar.activation(lowT[:, nodes(g)], lowT[:, nodes(g)], ACT.Exp).then_inc(ed, 1)

                    @block.tensor
                    def _(pe):
                        for g in range(2):
                            pe.wait_ge(h2d, g + 1)
                            for c in range(chunks(g).start, chunks(g).stop):
                                last = nc.tensor.transpose(pT[:, c // 4, (c % 4) * P:(c % 4 + 1) * P], h2[:, c, :], ident[:, :])
                            last.then_inc(ptd, 1)
                        for g in range(2):
                            pe.wait_ge(ptc, g + 1)
                            for s in range(*groups[g]):
                                w = min(512, NPAD - s * 512)
                                last = nc.tensor.matmul(pT[:, s, 0:w], w3[:, :], h2T[:, s * 512:s * 512 + w], start=True, stop=True)
                            last.then_inc(ptd, 1)
                        for g in range(2):
                            pe.wait_ge(ptc, g + 3)
                            for c in range(chunks(g).start, chunks(g).stop):
                                last = nc.tensor.matmul(p4[:, c * 3:c * 3 + 3], h3T[:, c * P:(c + 1) * P], w4[:, :], start=True, stop=True)
                            last.then_inc(ptd, 1)

                    @block.vector
                    def _(v):
                        go = line.on(v)
                        go(nc.vector.memset(tn[:, :, :], 0.0))
                        v.wait_ge(ld, 80)
                        flat = pT[:, :, :].rearrange("p a b -> p (a b)")
                        for g in range(2):
                            h, lo = h2[:, chunks(g), :], low[:, chunks(g), :]
                            go(nc.vector.tensor_tensor(h, h, bb[:, None, :].to_broadcast([P, h.shape[1], H]), ALU.add))
                            nc.vector.tensor_scalar(lo, h, 0.0, None, ALU.min).then_inc(er, 1)
                            go(nc.vector.tensor_scalar(h, h, 0.0, None, ALU.max))
                        for g in range(2):
                            h, lo = h2[:, chunks(g), :], low[:, chunks(g), :]
                            v.wait_ge(ed, g + 1)
                            nc.vector.scalar_tensor_tensor(h, lo, 1.0, h, ALU.subtract, ALU.add).then_inc(h2d, 1)
                        for g in range(2):
                            v.wait_ge(ptd, g + 1)
                            nc.vector.tensor_copy(h2T[:, nodes(g)], flat[:, nodes(g)]).then_inc(ptc, 1)
                        for g in range(2):
                            h, lo = h3T[:, nodes(g)], lowT[:, nodes(g)]
                            v.wait_ge(ptd, g + 3)
                            go(nc.vector.tensor_scalar(h, flat[:, nodes(g)], bc3[:, :], None, ALU.add))
                            nc.vector.tensor_scalar(lo, h, 0.0, None, ALU.min).then_inc(er, 1)
                            go(nc.vector.tensor_scalar(h, h, 0.0, None, ALU.max))
                        for g in range(2):
                            h, lo = h3T[:, nodes(g)], lowT[:, nodes(g)]
                            v.wait_ge(ed, g + 3)
                            nc.vector.scalar_tensor_tensor(h, lo, 1.0, h, ALU.subtract, ALU.add).then_inc(ptc, 1)
                        v.wait_ge(ptd, 6)
                        tt = tn[:, :, 0:3]
                        go(nc.vector.tensor_tensor(tt, p4[:, 0:3 * NCH].rearrange("p (c f) -> p c f", f=3),
                                                   bb4[:, None, :].to_broadcast([P, NCH, 3]), ALU.add))
                        split3(go, tt, [xt3[:, :, 3 * F + 3 * k:3 * F + 3 * k + 3] for k in range(3)], trest[:, :, :])
                        nc.vector.memset(trest[0:1, 0, 0:1], 0.0).then_inc(xd, 1)

            row_d = sb("row_d", [P, TS], i32, c=c9)
            c8 = ExitStack()
            with c8:
                tsrc = sb("tsrc", [P, TS, 9], c=c8)
                tdst = sb("tdst", [P, TS, TW], c=c8)
                recD = sb("recD", [P, TS, CW], c=c8)
                key_d = sb("key_d", [P, TS], c=c8)

                def sage_loop(tag, acc, dstc, sel, width, beside, first, end, tsrc):
                    cs = ExitStack()
                    with cs:
                        oh = sb(tag + "oh", [P, 2, HALF, P], bf16, c=cs)
                        d = sb(tag + "d", [P, RING // 2, DHALF], bf16, c=cs)
                        gs = sb(tag + "gs", [P, 4, QUAD, P], bf16, c=cs)
                        gp = pb(tag + "gp", [P, 512], cs)
                        ohl = [sem(f"{tag}ohl{h}", cs) for h in range(2)]
                        dm = sem(tag + "dm", cs)
                        du = sem(tag + "du", cs)
                        gd = sem(tag + "gd", cs)
                        ge = sem(tag + "ge", cs)
                        ini = sem(tag + "ini", cs)
                        block = cs.enter_context(nc.Block())
                        n_it = TS // RING
                        tab = xt3[:, :, :].rearrange("p c f -> p (c f)")

                        @block.sync
                        def _(sp):
                            beside.on_sync(sp, first, end)

                        @block.gpsimd
                        def _(pool):
                            beside.on_pool(pool, first, end)

                        @block.vector
                        def _(v):
                            nc.vector.memset(gs[:, :, :, 3 * F:P], 1.0).then_inc(ini, 1)
                            with v.Fori(0, n_it) as i:
                                for k in range(RING):
                                    v.wait_ge(du, i * RING + (k + 1))
                                    nc.vector.tensor_scalar(d[:, k % 8, :], iota16[:, :], dstc[:, bass.ds(i * RING + k, 1)],
                                                            None, ALU.is_equal).then_inc(dm, 1)

                        @block.scalar
                        def _(act):
                            def copy_rows(i, h, r, wait):
                                n = i * 4 + (2 * h + r)
                                act.wait_ge(gd, n + 1)
                                if wait:
                                    act.wait_ge(du, n * 4 - 4)
                                rows = gp[:, 0:QUAD * width].rearrange("p (a b) -> p a b", a=QUAD)
                                if width == XT:
                                    nc.scalar.copy(tsrc[:, bass.ds(n * QUAD, QUAD), :], rows[:, :, 3 * F:XT])
                                nc.scalar.copy(gs[:, 2 * h + r, :, 0:3 * F], rows[:, :, 0:3 * F]).then_inc(ge, 1)

                            def load(i, h):
                                act.dma_start(oh[:, h, :, :], oht_v[:, bass.ds(i * RING + h * HALF, HALF), :]).then_inc(ohl[h], 16)

                            for h in range(2):
                                load(0, h)
                            act.wait_ge(ini, 1)
                            act.sem_inc(ge, 1)
                            beside.first(act)
                            for r in range(2):
                                copy_rows(0, 0, r, False)
                            with act.Fori(0, n_it - 1) as i:
                                for h in range(2):
                                    load(i + 1, h)
                                    for r in range(2):
                                        copy_rows(i + h, 1 - h, r, True)
                                    beside.after(act, i, h, False)
                            for r in range(2):
                                copy_rows(n_it - 1, 1, r, True)
                            for h in range(2):
                                beside.after(act, n_it - 1, h, True)

                        @block.tensor
                        def _(pe):
                            regs = id_registers(pe, tag + "_g", 2 * HALF)
                            pe.sem_inc(du, 8)
                            flat = acc[:, :, :].rearrange("p a b -> p (a b)")
                            for s in range(7):
                                nc.tensor.matmul(acc[:, s, :], zeros[:, 0:P], zeros[:, :], start=True, stop=True)

                            def gather(i, h, r):
                                if r == 0:
                                    pe.wait_ge(ohl[h], (i + 1) * 16)
                                pe.wait_ge(ge, i * 4 + (2 * h + r + 1))
                                for k in range(QUAD):
                                    chunk = pe.snap(regs[r * QUAD + k], min_val=0, max_val=NCH - 1)
                                    last = nc.tensor.matmul(gp[:, k * width:(k + 1) * width], oh[:, h, r * QUAD + k, :],
                                                            tab[:, bass.ds(chunk * XT, width)], start=True, stop=True)
                                last.then_inc(gd, 1)

                            def sums(i, h, r):
                                q = 2 * h + r
                                pe.wait_ge(ge, i * 4 + (q + 2))
                                for k in range(QUAD):
                                    t = q * QUAD + k
                                    half = pe.snap(regs[HALF + r * QUAD + k], min_val=0, max_val=1)
                                    pe.wait_ge(dm, i * RING + (t + 1))
                                    for s in range(4):
                                        bank = half * 2048 + s * 512 if s < 3 else half * 1536 + 1536
                                        last = nc.tensor.matmul(flat[:, bass.ds(bank, DSEG)], gs[:, q, k, :],
                                                                d[:, t % 8, s * DSEG:(s + 1) * DSEG],
                                                                start=False, stop=True, skip_group_check=True)
                                    last.then_inc(du, 1)

                            def half_turn(i, h, last_half):
                                at = i * (2 * RING) + (h + 1) * RING
                                pe.load(regs, sel[0:1, bass.ds(at, RING)])
                                for r in range(2):
                                    if not last_half:
                                        gather(i + h, 1 - h, r)
                                    sums(i, h, r)

                            pe.load(regs, sel[0:1, 0:RING])
                            for r in range(2):
                                gather(0, 0, r)
                            with pe.Fori(0, n_it - 1) as i:
                                for h in range(2):
                                    half_turn(i, h, False)
                            for h in range(2):
                                half_turn(n_it - 1, h, h == 1)

                c4 = ExitStack()
                with c4:
                    dstc = sb("dstc", [P, TS], c=c4)
                    sel = sb("sel", [P, (TS // HALF + 1) * RING], i32, c=c4)
                    xn = sb("xn", [P, NCH, F], c=c4)
                    agg = sb("agg", [P, NPAD], c=c4)
                    q2 = sb("q2", [P, NCH, F], c=c4)
                    wa = sb("wa", [P, H], c=c4)
                    wd = sb("wd", [P, H], c=c4)
                    wr1 = sb("wr1", [F, H], c=c4)
                    w2 = sb("w2", [H, 2 * F], c=c4)
                    bc1 = sb("bc1", [H, 1], c=c4)
                    bb2 = sb("bb2", [P, F], c=c4)
                    fold = sb("fold", [P, F + 1], c=c4)
                    cs = ExitStack()
                    with cs:
                        rest = sb("rest", [P, NCH, F], c=cs)
                        ld = sem("ldD", cs)
                        ldx = sem("ldx", cs)
                        wz = sem("wzD", cs)
                        block = cs.enter_context(nc.Block())

                        @block.sync
                        def _(sp):
                            sp.wait_ge(wz, 2)
                            sp.dma_start(xn[:, 0:NCH - 1, :], x[0:(NCH - 1) * P, :].rearrange("(c p) f -> p c f", p=P)).then_inc(ldx, 16)
                            sp.dma_start(xn[0:NREM, NCH - 1, :], x[(NCH - 1) * P:N, :]).then_inc(ldx, 16)
                            for k in range(3):
                                sp.dma_start(wa[k * F:(k + 1) * F, :], w1l).then_inc(ld, 16)
                            sp.dma_start(wd[3 * F:3 * F + 1, :], ones[0:1, 0:H]).then_inc(ld, 16)
                            sp.dma_start(wr1[:, :], w1r).then_inc(ld, 16)
                            sp.dma_start(w2[:, 0:F], w2l).then_inc(ld, 16)
                            sp.dma_start(w2[:, F:2 * F], w2r).then_inc(ld, 16)
                            sp.dma_start(bc1[:, :], b1.rearrange("(n a) -> n a", a=1)).then_inc(ld, 16)
                            sp.dma_start(bb2[:, :], b2.rearrange("(a n) -> a n", a=1).to_broadcast([P, F])).then_inc(ld, 16)
                            for k in range(3):
                                sp.dma_start(fold[k * F:(k + 1) * F, 0:F], ident[0:F, 0:F]).then_inc(ld, 16)
                            sp.dma_start(fold[3 * F:3 * F + 1, F:F + 1], ones[0:1, 0:1]).then_inc(ld, 16)
                            sp.wait_ge(ld, 16 * 13)

                        @block.vector
                        def _(v):
                            nc.vector.memset(xn[:, :, :], 0.0).then_inc(wz, 1)
                            nc.vector.memset(wa[:, :], 0.0)
                            nc.vector.memset(fold[:, :], 0.0)
                            nc.vector.memset(wd[:, :], 0.0).then_inc(wz, 1)
                            go = line.on(v)
                            go(nc.vector.tensor_scalar(dstc[:, :], rs[:, :, 1], float(DHALF), float(-DHALF), ALU.is_ge, ALU.mult))
                            go(nc.vector.tensor_tensor(dstc[:, :], dstc[:, :], rs[:, :, 1], ALU.add))
                            selv = sel[:, :].rearrange("p (j k) -> p j k", k=RING)
                            go(nc.vector.memset(sel[:, :], 0))
                            go(nc.vector.tensor_copy(selv[:, 0:TS // HALF, 0:HALF], chunk_i[:, :].rearrange("p (j k) -> p j k", k=HALF)))
                            go(nc.vector.tensor_copy(selv[:, 1:, HALF:RING], half_i[:, :].rearrange("p (j k) -> p j k", k=HALF)))
                            v.wait_ge(ldx, 32)
                            split3(go, xn[:, :, :], [xt3[:, :, k * F:(k + 1) * F] for k in range(3)], rest[:, :, :])

                    def sage_sum(tag, width, beside, first, end, tsrc):
                        cp = ExitStack()
                        with cp:
                            acc = pb(tag + "acc", [P, 7, 512], cp)
                            sage_loop(tag, acc, dstc, sel, width, beside, first, end, tsrc)
                            cs = ExitStack()
                            with cs:
                                cpd = sem(tag + "cpd", cs)
                                block = cs.enter_context(nc.Block())

                                @block.vector
                                def _(v):
                                    nc.vector.memset(agg[:, N:NPAD], 0.0).then_inc(cpd, 1)
                                    v.wait_ge(cpd, 1)
                                    nc.vector.tensor_copy(agg[:, 0:6 * DSEG].rearrange("p (a b) -> p a b", a=6), acc[:, 0:6, 0:DSEG])
                                    nc.vector.tensor_copy(agg[:, 6 * DSEG:N], acc[:, 6, 0:N - 6 * DSEG]).then_inc(cpd, 1)
                                    v.wait_ge(cpd, 2)

                    cs = ExitStack()
                    with cs:
                        sage_sum("g1", XT, Gather("td", t_tab, NPAD, dst_i, tdst, cs), 0, TS // RING, tsrc)

                    cs = ExitStack()
                    with cs:
                        np_ = sb("np_", [P, TS, 3], c=cs)
                        fl = sb("fl3", [P, TS, 3], c=cs)
                        tt = sb("tt3", [P, TS, 3], c=cs)
                        block = cs.enter_context(nc.Block())

                        @block.vector
                        def _(v):
                            go = line.on(v)
                            p = np_[:, :, :]
                            go(nc.vector.reduce_sum(fl[:, :, :], tsrc[:, :, :].rearrange("p t (a d) -> p t d a", a=3), axis=AX))
                            go(nc.vector.tensor_tensor(p, rs[:, :, 2:5], tdst[:, :, 0:3], ALU.add))
                            go(nc.vector.tensor_tensor(p, p, fl[:, :, :], ALU.subtract))
                            go(nc.vector.tensor_scalar(p, p, 0.0, 1.0, ALU.max, ALU.min))
                            go(nc.vector.tensor_scalar(p, p, float(KS - 1), None, ALU.mult))
                            cell_steps(go, p, fl[:, :, :], key_d[:, :])
                            go(nc.vector.tensor_copy(recD[:, :, 1:4], fl[:, :, :]))
                            go(nc.vector.tensor_copy(recD[:, :, 0], dst_i[:, :]))
                            go(nc.vector.tensor_scalar(tt[:, :, 0], rs[:, :, 0], 0.0, 1000.0, ALU.is_lt, ALU.mult))
                            go(nc.vector.tensor_tensor(key_d[:, :], key_d[:, :], tt[:, :, 0], ALU.add))

                    c2 = ExitStack()
                    with c2:
                        sort_block("sd", key_d[:, :], TS, CELLS, TC, row_d[:, :], cell_i, c2)

                    cn = ExitStack()
                    with cn:
                        by_new = Scatter("xd", recD, row_d, rec_d, P * TC, cn)
                        cs = ExitStack()
                        with cs:
                            xt = sb("xt", [F, NPAD], c=cs)
                            hT = sb("hT", [H, NPAD], c=cs)
                            rest = agg[:, 0:NCH * F].rearrange("p (c f) -> p c f", f=F)
                            pn = agg[:, NCH * F:2 * NCH * F].rearrange("p (c f) -> p c f", f=F)
                            pm = pb("pm", [P, 8, 512], cs)
                            pq = pm[:, 0:4, :]
                            ld = sem("ldE", cs)
                            mm = sem("mmE", cs)
                            fr = sem("frE", cs)
                            rl = sem("rlE", cs)
                            pqd = sem("pqd", cs)
                            wz = sem("wzE", cs)

                            def products(s, w):
                                return [pm[0:H, 3 * (s % 2) + k, 0:w] for k in range(3)]

                            block = cs.enter_context(nc.Block())

                            @block.gpsimd
                            def _(pool):
                                by_new.on_pool(pool, 0, MID_TURNS)

                            @block.sync
                            def _(sp):
                                sp.wait_ge(wz, 1)
                                sp.dma_start(xt[:, 0:N], xT).then_inc(ld, 16)
                                by_new.on_sync(sp, 0, MID_TURNS)

                            @block.tensor
                            def _(pe):
                                pe.wait_ge(ld, 16)
                                for s in range(7):
                                    w = min(512, NPAD - s * 512)
                                    c = slice(s * 512, s * 512 + w)
                                    if s >= 2:
                                        pe.wait_ge(fr, s - 1)
                                    pa, pd, pr = products(s, w)
                                    nc.tensor.matmul(pa, wa[:, :], agg[:, c], start=True, stop=True)
                                    nc.tensor.matmul(pd, wd[:, :], agg[:, c], start=True, stop=True)
                                    nc.tensor.matmul(pr, wr1[:, :], xt[:, c], start=True, stop=True).then_inc(mm, 1)
                                pe.wait_ge(rl, 7)
                                for c in range(NCH):
                                    last = nc.tensor.matmul(pq[:, c // 8, (c % 8) * H:(c % 8 + 1) * H], hT[:, c * P:(c + 1) * P], w2[:, :],
                                                            start=True, stop=True)
                                last.then_inc(pqd, 1)

                            @block.scalar
                            def _(act):
                                for s in range(7):
                                    w = min(512, NPAD - s * 512)
                                    act.wait_ge(fr, s + 1)
                                    nc.scalar.activation(hT[:, s * 512:s * 512 + w], hT[:, s * 512:s * 512 + w], ACT.Relu, bias=bc1[:, :]).then_inc(rl, 1)

                            @block.vector
                            def _(v):
                                nc.vector.memset(xt[:, :], 0.0).then_inc(wz, 1)
                                go = line.on(v)
                                for s in range(7):
                                    w = min(512, NPAD - s * 512)
                                    v.wait_ge(mm, s + 1)
                                    a = hT[:, s * 512:s * 512 + w]
                                    pa, pd, pr = products(s, w)
                                    go(nc.vector.tensor_scalar(a, pd, 1.0, None, ALU.max))
                                    go(nc.vector.reciprocal(a, a))
                                    go(nc.vector.tensor_tensor(a, a, pa, ALU.mult))
                                    nc.vector.tensor_tensor(a, a, pr, ALU.add).then_inc(fr, 1)
                                v.wait_ge(pqd, 1)
                                for b in range(4):
                                    n = min(8, NCH - 8 * b)
                                    view = pq[:, b, 0:n * H].rearrange("p (c f) -> p c f", f=H)
                                    go(nc.vector.tensor_copy(pn[:, 8 * b:8 * b + n, :], view[:, :, 0:F]))
                                    go(nc.vector.tensor_tensor(q2[:, 8 * b:8 * b + n, :], view[:, :, F:H],
                                                               bb2[:, None, :].to_broadcast([P, n, F]), ALU.add))
                                split3(go, pn[:, :, :], [xt3[:, :, k * F:(k + 1) * F] for k in range(3)], rest[:, :, :])

                        sage_sum("g2", 3 * F, by_new, MID_TURNS, TS // RING - END_TURNS, None)

                        cs = ExitStack()
                        with cs:
                            pf = pb("pf", [P, 2, 512], cs)
                            y = sb("yE", [P, NCH, F], c=cs)
                            rd = sb("rdE", [P, NCH], c=cs)
                            mean = sb("meanE", [P, NCH], c=cs)
                            sq = sb("sqE", [P, NCH, F], c=cs)
                            fd = sem("fdF", cs)
                            rr = sem("rrF", cs)
                            rt = sem("rtF", cs)
                            xs = sem("x1_made", cs)
                            st = sem("x1_stored", cs)
                            block = cs.enter_context(nc.Block())
                            CB = 512 // (F + 1)

                            @block.tensor
                            def _(pe):
                                for c in range(NCH):
                                    last = nc.tensor.matmul(pf[:, c // CB, (c % CB) * (F + 1):(c % CB + 1) * (F + 1)],
                                                            agg[:, c * P:(c + 1) * P], fold[:, :], start=True, stop=True)
                                last.then_inc(fd, 1)

                            @block.scalar
                            def _(act):
                                act.wait_ge(rr, 1)
                                nc.scalar.activation(mean[:, :], mean[:, :], ACT.Sqrt).then_inc(rt, 1)
                                act.wait_ge(xs, 1)
                                act.dma_start(x1_tab.rearrange("(c p) f -> p c f", p=P), x1[:, :, :]).then_inc(st, 16)
                                act.wait_ge(st, 16)

                            @block.vector
                            def _(v):
                                go = line.on(v)
                                v.wait_ge(fd, 1)
                                for b in range(2):
                                    n = min(CB, NCH - CB * b)
                                    view = pf[:, b, 0:n * (F + 1)].rearrange("p (c f) -> p c f", f=F + 1)
                                    s = slice(CB * b, CB * b + n)
                                    go(nc.vector.tensor_scalar(rd[:, s], view[:, :, F], 1.0, None, ALU.max))
                                    go(nc.vector.reciprocal(rd[:, s], rd[:, s]))
                                    go(nc.vector.tensor_tensor(y[:, s, :], view[:, :, 0:F], rd[:, s, None].to_broadcast([P, n, F]), ALU.mult))
                                go(nc.vector.tensor_tensor(y[:, :, :], y[:, :, :], q2[:, :, :], ALU.add))
                                go(nc.vector.tensor_tensor(y[:, :, :], y[:, :, :], xn[:, :, :], ALU.add))
                                norm_steps(v, go, y[:, :, :], x1[:, :, :], mean, sq, rt, rr, 1)
                                nc.vector.memset(mean[0:1, 0:1], 0.0).then_inc(xs, 1)

                            @block.sync
                            def _(sp):
                                by_new.on_sync(sp, TS // RING - END_TURNS, TS // RING)

                            @block.gpsimd
                            def _(pool):
                                by_new.on_pool(pool, TS // RING - END_TURNS, TS // RING)

            c5 = ExitStack()
            with c5:
                cws = sb("cws", [P, KK * F], c=c5)
                fg = sb("fg3", [P, TC, 3, 2], c=c5)
                cdst = sb("cdst3", [P, TC], i32, c=c5)
                w12 = sb("w12", [P, TC, 4], c=c5)
                wx2 = sb("wx2", [P, TC, 2], c=c5)
                fr = sb("fr3", [P, TC, CW], c=c5)
                sh = sb("shI", [P, TC], i32, c=c5)
                lo = sb("loI", [P, TC], i32, c=c5)
                ldr = sem("ldr3", c5)
                ld = sem("ldI", c5)

                def load3(sp):
                    sp.dma_start(fr[:, :, :].rearrange("p t w -> p (t w)"),
                                 rec_d.rearrange("(p t) w -> p (t w)", p=P)).then_inc(ldr, 16)
                    for n, off in enumerate((0, 1, KS, KS + 1)):
                        sp.dma_start(cws[n * F:(n + 1) * F, 0:(KK - off) * F].rearrange("i (k o) -> i k o", o=F),
                                     cw[off:KK, :, :].rearrange("k i o -> i k o")).then_inc(ld, 16)

                def prepare3(v, indexed, ready):
                    go = line.on(v)
                    v.wait_ge(ldr, 16)
                    nc.vector.tensor_copy(cdst[:, :], fr[:, :, 0]).then_inc(indexed, 1)
                    first_kernel_steps(go, sh, lo)
                    corner_steps(go, fr[:, :, 1:4], fg, w12, 1, wx2, 0)
                    go(nc.vector.tensor_scalar(row_d[:, :], row_d[:, :], float(P * TC - 1), None, ALU.min))
                    v.wait_ge(ld, 64)
                    nc.vector.memset(sh[:, :], 0).then_inc(ready, 1)

                cell_loop("c3", F, F, cws, koff, w12, wx2, cdst, x1_tab, msg3, load3, prepare3)

            cs = ExitStack()
            with cs:
                y = sb("yJ", [P, NCH, F], c=cs)
                o = sb("oJ", [P, NCH, F], c=cs)
                cp = ExitStack()
                with cp:
                    acc = pb("acc3", [P, 2, 512], cp)
                    segment_loop("m3", F, row_d, msg3, acc)
                    node_copy("n3", acc, y, F)
                mean = sb("meanJ", [P, NCH], c=cs)
                sq = sb("sqJ", [P, NCH, F], c=cs)
                bb = sb("bbJ", [P, F], c=cs)
                ld = sem("ldJ", cs)
                rr = sem("rrJ", cs)
                rt = sem("rtJ", cs)
                od = sem("odJ", cs)
                st = sem("stJ", cs)
                block = cs.enter_context(nc.Block())

                @block.sync
                def _(sp):
                    sp.dma_start(bb[:, :], cb.rearrange("(a n) -> a n", a=1).to_broadcast([P, F])).then_inc(ld, 16)
                    sp.wait_ge(od, 1)
                    sp.dma_start(out[0:(NCH - 1) * P, :].rearrange("(c p) f -> p c f", p=P), o[:, 0:NCH - 1, :]).then_inc(st, 16)
                    sp.dma_start(out[(NCH - 1) * P:N, :], o[0:NREM, NCH - 1, :]).then_inc(st, 16)
                    sp.wait_ge(st, 32)

                @block.scalar
                def _(act):
                    act.wait_ge(rr, 1)
                    nc.scalar.activation(mean[:, :], mean[:, :], ACT.Sqrt).then_inc(rt, 1)

                @block.vector
                def _(v):
                    go = line.on(v)
                    v.wait_ge(ld, 16)
                    go(nc.vector.tensor_tensor(y[:, :, :], y[:, :, :], bb[:, None, :].to_broadcast([P, NCH, F]), ALU.add))
                    go(nc.vector.tensor_tensor(y[:, :, :], y[:, :, :], x1[:, :, :], ALU.add))
                    norm_steps(v, go, y[:, :, :], o[:, :, :], mean, sq, rt, rr, 1)
                    nc.vector.memset(mean[0:1, 0:1], 0.0).then_inc(od, 1)


def kernel(**inputs):
    import numpy as np
    import concourse.bacc as bacc
    from concourse.bass_utils import run_bass_kernel_spmd

    g = {k: np.asarray(v) for k, v in inputs.items()}
    lay = {
        "x": g["x"], "xT": g["x"].T, "src": g["src"], "dst": g["dst"], "ps": g["edge_attr_3"],
        "w1l": g["L0_gnn_W1_l"].T, "w1r": g["L0_gnn_W1_r"].T, "b1": g["L0_gnn_b1"],
        "w2l": g["L0_gnn_W2_l"].T, "w2r": g["L0_gnn_W2_r"].T, "b2": g["L0_gnn_b2"],
        "s1w": g["L1_gnn_stn1_w"], "s1b": g["L1_gnn_stn1_b"], "s2w": g["L1_gnn_stn2_w"], "s2b": g["L1_gnn_stn2_b"],
        "s3w": g["L1_gnn_stn3_w"], "s3b": g["L1_gnn_stn3_b"], "s4w": g["L1_gnn_stn4_w"], "s4b": g["L1_gnn_stn4_b"],
        "cw": g["L1_gnn_conv_w"], "cb": g["L1_gnn_conv_b"],
    }
    nc = bacc.Bacc("TRN2", target_bir_lowering=False, num_devices=1)
    arrays, args = {}, []
    for name, a in lay.items():
        a = np.ascontiguousarray(a)
        arrays["in_" + name] = a
        args.append(nc.dram_tensor("in_" + name, a.shape, mybir.dt.from_np(a.dtype), kind="ExternalInput").ap())
    args.append(nc.dram_tensor("out_0", (N, F), fp32, kind="ExternalOutput").ap())
    gnn_kernel(nc, *args)
    r = run_bass_kernel_spmd(nc, [arrays], core_ids=[0])
    return r.results[0]["out_0"]
```
